# Optimizing a Trainium2 kernel written in Bass

```python
import numpy as np
import jax
import jax.numpy as jnp

def _softmax(x, axis=-1):
    return jax.nn.softmax(x, axis=axis)

def _gelu(x):
    return jax.nn.gelu(x, approximate=True)

def _silu(x):
    return jax.nn.silu(x)

def _sigmoid(x):
    return jax.nn.sigmoid(x)

def _layernorm(x, axis=-1, eps=1e-05):
    m = jnp.mean(x, axis=axis, keepdims=True)
    v = jnp.var(x, axis=axis, keepdims=True)
    return (x - m) / jnp.sqrt(v + eps)

def _scatter_add(tgt, idx, src, axis=0):
    return tgt.at[idx].add(src)

def _segment_sum(src, seg, n):
    return jax.ops.segment_sum(src, seg, n)
kernel_name = 'mk_gnn_resnorm_d4_gnn_r8_7186e8'

def setup_inputs(seed: int=0):
    np.random.seed(seed)
    _w = jnp.asarray

    def _rec_inputs():
        import jax
        import jax.numpy as jnp
        _gk = jax.random.key(seed)
        x = -0.000202 + 1 * jax.random.normal(jax.random.fold_in(_gk, 1), (12500, 64), jnp.float32)
        src = jax.random.randint(jax.random.fold_in(_gk, 2), (200000,), 0, 12500, jnp.int32)
        dst = jnp.minimum((12500 * jax.random.uniform(jax.random.fold_in(_gk, 3), (200000,)) ** 2.0).astype(jnp.int32), 99999)
        _o = jnp.argsort(dst, stable=True)
        src = src[_o]
        dst = dst[_o]
        edge_type_16 = jax.random.randint(jax.random.fold_in(_gk, 13), (200000,), 0, 16, jnp.int32)
        return (x, src, dst, edge_type_16)
    x, src, dst, edge_type_16 = _rec_inputs()

    def _L0_gnn_setup():
        import jax, jax.numpy as jnp
        import numpy as np
        N_NODES = 12500
        N_EDGES = 156250
        D_IN = 64
        D_OUT = 64
        K = 3
        LAMBDA_MAX = 2.0
        key = jax.random.key(seed)
        k1, k2, k3, k4 = jax.random.split(key, 4)
        feat = jax.random.normal(k1, (N_NODES, D_IN), dtype=jnp.float32)
        src = jax.random.randint(k2, (N_EDGES,), 0, N_NODES, dtype=jnp.int32)
        dst = jax.random.randint(k3, (N_EDGES,), 0, N_NODES, dtype=jnp.int32)
        W = jax.random.normal(k4, (K * D_IN, D_OUT), dtype=jnp.float32) * (1.0 / np.sqrt(K * D_IN))
        b = jnp.zeros((D_OUT,), dtype=jnp.float32)
        return {'feat': feat, 'src': src, 'dst': dst, 'W': W, 'b': b}
    _L0_gnn_all = _L0_gnn_setup()
    _L0_gnn_in = {k: v for k, v in _L0_gnn_all.items() if k in ('W', 'b')}
    del _L0_gnn_all

    def _L1_gnn_setup():
        import jax, jax.numpy as jnp
        import numpy as np
        N = 12500
        E = 200000
        D = 64
        H = 5
        NEG_SLOPE = 0.2
        key = jax.random.key(seed)
        k1, k2, k3, k4, k5, k6 = jax.random.split(key, 6)
        features = jax.random.normal(k1, (N, D), dtype=jnp.float32)
        edge_index = jax.random.randint(k2, (2, E), 0, N, dtype=jnp.int64)
        W = jax.random.normal(k3, (D, H * D), dtype=jnp.float32) * (1.0 / np.sqrt(D))
        att_src = jax.random.normal(k4, (H, D), dtype=jnp.float32) * 0.1
        att_dst = jax.random.normal(k5, (H, D), dtype=jnp.float32) * 0.1
        bias = jnp.zeros((D,), dtype=jnp.float32)
        return {'features': features, 'edge_index': edge_index, 'W': W, 'att_src': att_src, 'att_dst': att_dst, 'bias': bias}
    _L1_gnn_all = _L1_gnn_setup()
    _L1_gnn_in = {k: v for k, v in _L1_gnn_all.items() if k in ('W', 'att_src', 'att_dst', 'bias')}
    del _L1_gnn_all

    def _L2_gnn_setup():
        import jax, jax.numpy as jnp
        import numpy as np
        N_NODES = 12500
        N_EDGES = 150000
        HID = 64
        N_LAYERS = 3
        GAMMA = -0.45
        ZETA = 1.05
        key = jax.random.key(seed)
        ks = jax.random.split(key, 8)
        s = 0.05
        return {'features': jax.random.normal(ks[0], (N_NODES, HID), jnp.float32), 'nb_W': jax.random.normal(ks[1], (N_LAYERS, HID, HID), jnp.float32) * s, 'nb_b': jnp.zeros((N_LAYERS, HID), jnp.float32), 'self_W': jax.random.normal(ks[2], (N_LAYERS, HID, HID), jnp.float32) * s, 'self_b': jnp.zeros((N_LAYERS, HID), jnp.float32), 'att1_W': jax.random.normal(ks[3], (N_LAYERS, 2 * HID, HID), jnp.float32) * s, 'att1_b': jnp.zeros((N_LAYERS, HID), jnp.float32), 'att2_W': jax.random.normal(ks[4], (N_LAYERS, HID, 1), jnp.float32) * s, 'att2_b': jnp.zeros((N_LAYERS, 1), jnp.float32), 'row': jax.random.randint(ks[5], (N_EDGES,), 0, N_NODES, jnp.int32), 'col': jax.random.randint(ks[6], (N_EDGES,), 0, N_NODES, jnp.int32)}
    _L2_gnn_all = _L2_gnn_setup()
    _L2_gnn_in = {k: v for k, v in _L2_gnn_all.items() if k in ('nb_W', 'nb_b', 'self_W', 'self_b', 'att1_W', 'att1_b', 'att2_W', 'att2_b')}
    del _L2_gnn_all

    def _L3_gnn_setup():
        import jax, jax.numpy as jnp
        import numpy as np
        N_NODES = 12500
        N_EDGES = 125000
        IN_FEAT = 64
        OUT_FEAT = 64
        NUM_RELS = 16
        key = jax.random.key(seed)
        ks = jax.random.split(key, 7)
        xavier = np.sqrt(2.0) * np.sqrt(6.0 / (IN_FEAT + OUT_FEAT))
        feat = jax.random.normal(ks[0], (N_NODES, IN_FEAT), dtype=jnp.float32)
        weight = jax.random.uniform(ks[1], (NUM_RELS, IN_FEAT, OUT_FEAT), dtype=jnp.float32, minval=-xavier, maxval=xavier)
        h_bias = jnp.zeros((OUT_FEAT,), dtype=jnp.float32)
        loop_weight = jax.random.uniform(ks[2], (IN_FEAT, OUT_FEAT), dtype=jnp.float32, minval=-xavier, maxval=xavier)
        src = jax.random.randint(ks[3], (N_EDGES,), 0, N_NODES, dtype=jnp.int32)
        dst = jax.random.randint(ks[4], (N_EDGES,), 0, N_NODES, dtype=jnp.int32)
        etype = jax.random.randint(ks[5], (N_EDGES,), 0, NUM_RELS, dtype=jnp.int32)
        return {'feat': feat, 'weight': weight, 'h_bias': h_bias, 'loop_weight': loop_weight, 'src': src, 'dst': dst, 'etype': etype}
    _L3_gnn_all = _L3_gnn_setup()
    _L3_gnn_in = {k: v for k, v in _L3_gnn_all.items() if k in ('weight', 'h_bias', 'loop_weight')}
    del _L3_gnn_all
    return {'x': x, 'src': src, 'dst': dst, 'edge_type_16': edge_type_16, 'L0_gnn_W': _L0_gnn_in['W'], 'L0_gnn_b': _L0_gnn_in['b'], 'L1_gnn_W': _L1_gnn_in['W'], 'L1_gnn_att_src': _L1_gnn_in['att_src'], 'L1_gnn_att_dst': _L1_gnn_in['att_dst'], 'L1_gnn_bias': _L1_gnn_in['bias'], 'L2_gnn_nb_W': _L2_gnn_in['nb_W'], 'L2_gnn_nb_b': _L2_gnn_in['nb_b'], 'L2_gnn_self_W': _L2_gnn_in['self_W'], 'L2_gnn_self_b': _L2_gnn_in['self_b'], 'L2_gnn_att1_W': _L2_gnn_in['att1_W'], 'L2_gnn_att1_b': _L2_gnn_in['att1_b'], 'L2_gnn_att2_W': _L2_gnn_in['att2_W'], 'L2_gnn_att2_b': _L2_gnn_in['att2_b'], 'L3_gnn_weight': _L3_gnn_in['weight'], 'L3_gnn_h_bias': _L3_gnn_in['h_bias'], 'L3_gnn_loop_weight': _L3_gnn_in['loop_weight']}

def reference(x, src, dst, edge_type_16, L0_gnn_W, L0_gnn_b, L1_gnn_W, L1_gnn_att_src, L1_gnn_att_dst, L1_gnn_bias, L2_gnn_nb_W, L2_gnn_nb_b, L2_gnn_self_W, L2_gnn_self_b, L2_gnn_att1_W, L2_gnn_att1_b, L2_gnn_att2_W, L2_gnn_att2_b, L3_gnn_weight, L3_gnn_h_bias, L3_gnn_loop_weight):
    import jax
    import jax.numpy as jnp

    def _L0_gnn_ref(feat, src, dst, W, b):
        import jax, jax.numpy as jnp
        import numpy as np
        N_NODES = 12500
        N_EDGES = 156250
        D_IN = 64
        D_OUT = 64
        K = 3
        LAMBDA_MAX = 2.0
        n = feat.shape[0]
        deg = jax.ops.segment_sum(jnp.ones_like(dst, dtype=feat.dtype), dst, num_segments=n)
        d_sqrt = jnp.power(jnp.clip(deg, 1.0, None), -0.5)[:, None]

        def unn_laplacian(x):
            msg = (x * d_sqrt)[src]
            agg = jax.ops.segment_sum(msg, dst, num_segments=n)
            return agg * d_sqrt
        re_norm = 2.0 / LAMBDA_MAX
        X0 = feat
        Xs = [X0]
        if K > 1:
            X1 = -re_norm * unn_laplacian(X0) + X0 * (re_norm - 1.0)
            Xs.append(X1)
            for _ in range(2, K):
                Xi = -2.0 * re_norm * unn_laplacian(X1) + X1 * (2.0 * (re_norm - 1.0)) - X0
                Xs.append(Xi)
                X0, X1 = (X1, Xi)
        Xt = jnp.concatenate(Xs, axis=1)
        return jax.nn.relu(Xt @ W + b)

    def _L1_gnn_ref(features, edge_index, W, att_src, att_dst, bias):
        import jax, jax.numpy as jnp
        import numpy as np
        N = 12500
        E = 200000
        D = 64
        H = 5
        NEG_SLOPE = 0.2
        n = features.shape[0]
        x = (features @ W).reshape(n, H, D)
        a_src = jnp.einsum('nhd,hd->nh', x, att_src)
        a_dst = jnp.einsum('nhd,hd->nh', x, att_dst)
        loops = jnp.arange(n, dtype=edge_index.dtype)
        src = jnp.concatenate([edge_index[0], loops])
        dst = jnp.concatenate([edge_index[1], loops])
        e = jax.nn.leaky_relu(a_src[src] + a_dst[dst], negative_slope=NEG_SLOPE)
        emax = jax.ops.segment_max(e, dst, num_segments=n)
        e = jnp.exp(e - emax[dst])
        esum = jax.ops.segment_sum(e, dst, num_segments=n)
        alpha = e / (esum[dst] + 1e-16)
        msg = x[src] * alpha[:, :, None]
        out = jax.ops.segment_sum(msg, dst, num_segments=n)
        out = out.mean(axis=1) + bias
        return features + out

    def _L2_gnn_ref(features, nb_W, nb_b, self_W, self_b, att1_W, att1_b, att2_W, att2_b, row, col):
        import jax, jax.numpy as jnp
        import numpy as np
        N_NODES = 12500
        N_EDGES = 150000
        HID = 64
        N_LAYERS = 3
        GAMMA = -0.45
        ZETA = 1.05
        n = features.shape[0]
        x = features
        out = features
        for l in range(N_LAYERS):
            f1 = jax.nn.relu(x[row] @ nb_W[l] + nb_b[l])
            f2 = jax.nn.relu(x[col] @ self_W[l] + self_b[l])
            h = jax.nn.relu(jnp.concatenate([f1, f2], axis=1) @ att1_W[l] + att1_b[l])
            log_alpha = (h @ att2_W[l] + att2_b[l])[:, 0]
            mask = jnp.clip(jax.nn.sigmoid(log_alpha) * (ZETA - GAMMA) + GAMMA, 0.0, 1.0)
            rowsum = jax.ops.segment_sum(mask, row, num_segments=n) + 1e-06
            d_inv_sqrt = jnp.clip(rowsum ** (-0.5), 0.0, 10.0)
            vals = mask * d_inv_sqrt[row] * d_inv_sqrt[col]
            x = jax.ops.segment_sum(vals[:, None] * x[col], row, num_segments=n)
            out = out + x
        return out

    def _L3_gnn_ref(feat, weight, h_bias, loop_weight, src, dst, etype):
        import jax, jax.numpy as jnp
        import numpy as np
        N_NODES = 12500
        N_EDGES = 125000
        IN_FEAT = 64
        OUT_FEAT = 64
        NUM_RELS = 16
        xproj = jnp.einsum('ni,rio->rno', feat, weight)
        m = xproj[etype, src]
        agg = jax.ops.segment_sum(m, dst, num_segments=feat.shape[0])
        return agg + h_bias + feat @ loop_weight
    edge_index = jnp.stack([src, dst])
    x = _layernorm(x + _L0_gnn_ref(x, src, dst, L0_gnn_W, L0_gnn_b), axis=-1)
    x = _layernorm(x + _L1_gnn_ref(x, edge_index, L1_gnn_W, L1_gnn_att_src, L1_gnn_att_dst, L1_gnn_bias), axis=-1)
    x = _layernorm(x + _L2_gnn_ref(x, L2_gnn_nb_W, L2_gnn_nb_b, L2_gnn_self_W, L2_gnn_self_b, L2_gnn_att1_W, L2_gnn_att1_b, L2_gnn_att2_W, L2_gnn_att2_b, src, dst), axis=-1)
    x = _layernorm(x + _L3_gnn_ref(x, L3_gnn_weight, L3_gnn_h_bias, L3_gnn_loop_weight, src, dst, edge_type_16), axis=-1)
    return x

_drawn_inputs = setup_inputs


def setup_inputs(seed=0):
    import zlib

    import numpy as np

    out = dict(_drawn_inputs(seed))
    spreads = {'L0_gnn_b': (0.0, 0.1),
     'L1_gnn_bias': (0.0, 0.1),
     'L2_gnn_nb_b': (0.0, 0.8),
     'L2_gnn_self_b': (0.0, 0.8),
     'L2_gnn_att1_b': (0.0, 0.8),
     'L2_gnn_att2_b': (0.0, 0.8),
     'L3_gnn_h_bias': (0.0, 0.437)}
    factors = {'L1_gnn_att_dst': 4.548,
     'L2_gnn_nb_W': 8.0,
     'L2_gnn_self_W': 6.371,
     'L2_gnn_att1_W': 7.295,
     'L2_gnn_att2_W': 7.377}
    for name, (base, spread) in spreads.items():
        noise = np.random.default_rng([zlib.crc32(name.encode()), seed]).standard_normal(out[name].shape)
        drawn = base * np.exp(spread * noise) if base else spread * noise
        out[name] = jnp.asarray(drawn.astype(out[name].dtype))
    for name, factor in factors.items():
        out[name] = (out[name] * factor).astype(out[name].dtype)
    return out
```

```python
from contextlib import ExitStack

import numpy as np

import concourse.bass as bass
from concourse import mybir
from concourse.alu_op_type import AluOpType as ALU

ACT = mybir.ActivationFunctionType
F32 = mybir.dt.float32
BF16 = mybir.dt.bfloat16
I32 = mybir.dt.int32
AX_X = mybir.AxisListType.X

P = 128
N_NODES, N_EDGES, D = 12500, 200000, 64
HEADS, N_LAYERS, N_RELS = 5, 3, 16
NC = -(-N_NODES // P)
NP = NC * P
K = 28
EC = -(-N_EDGES // (P * 2 * K)) * 2 * K
EP = EC * P
EIT = EC // (2 * K)
NK = 7
NIT = NC // (2 * NK)
PAD_NODE = NP - 1
NO_EDGE_ROW = EP
BIG = 1.0e30
HW_ = D + 2
ROW1 = HEADS * HW_
TAB1 = 72
GAMMA, ZETA = -0.45, 1.05
LOGB = 7


class Signal:

    def __init__(self, ctx, nc, name, dma):
        self.sem = ctx.enter_context(nc.semaphore(name))
        self.dma = dma
        self.total = 0
        self.pending = 0

    def at(self, n):
        return n + self.total

    def counted(self, n):
        self.pending += n


class Steps:

    def __init__(self, eng, signal, i=None, per=0):
        self.eng, self.counter, self.i, self.per, self.k = eng, signal, i, per, 0
        self.base = signal.total + signal.pending

    def mark(self, ins):
        self.k += 1
        ins.then_inc(self.counter.sem, 1)

    def wait(self):
        if self.i is None:
            self.eng.wait_ge(self.counter.sem, self.base + self.k)
        else:
            self.eng.wait_ge(self.counter.sem, self.i * self.per + (self.base + self.k))

    def then(self, ins):
        self.mark(ins)
        self.wait()

    def close(self, iterations=1):
        assert self.i is None or self.per == self.k, (self.per, self.k)
        self.counter.counted(iterations * self.k)


class Core:

    def __init__(self, nc, ctx, prefix="", turns=4):
        self.nc, self.ctx = nc, ctx
        self.phase = 0
        self.all_signals = []

        def signal(name, dma=False):
            self.all_signals.append(Signal(ctx, nc, prefix + name, dma))
            return self.all_signals[-1]

        self.moved = signal("moved", True)
        self.gathered_by_turn = [[signal(f"gathered{n}_{s}", True) for s in range(2)] for n in range(turns)]
        self.gathered = self.gathered_by_turn[0]
        self.stored = [signal(f"stored{s}", True) for s in range(2)]
        self.loaded = [signal(f"loaded{s}", True) for s in range(2)]
        self.staged = [signal(f"staged{s}") for s in range(2)]
        self.computed = [signal(f"computed{s}") for s in range(2)]
        self.taken = [signal(f"taken{s}") for s in range(2)]
        self.dve_step = signal("dve_step")
        self.act_step = signal("act_step")
        self.pool_step = signal("pool_step")
        self.sp_turn = signal("sp_turn")
        self.pool_turn = signal("pool_turn")
        self.pe_turn = signal("pe_turn")
        self.dve_gave = signal("dve_gave")
        self.act_gave = signal("act_gave")
        self.pe_gave = signal("pe_gave")
        self.act_gave2 = signal("act_gave2")
        self.pe_gave2 = signal("pe_gave2")
        self.dve_gave2 = signal("dve_gave2")
        self.loaded_by_dve = signal("loaded_by_dve")

    def signals(self):
        return self.all_signals

    def end_phase(self):
        self.phase += 1
        for s in self.signals():
            s.total += s.pending
            s.pending = 0
        if len(self.gathered_by_turn) > 1 and self.gathered[0].total + 16 * (K * EIT + 1) > 65535:
            self.gathered = self.gathered_by_turn[self.gathered_by_turn.index(self.gathered) + 1]

    def place(self, name, ctx):
        return f"{name}_{self.phase}" if ctx else name

    def sb(self, name, shape, dt=F32, ctx=None):
        return (ctx or self.ctx).enter_context(self.nc.sbuf_tensor(self.place(name, ctx), shape, dt))

    def ps(self, name, shape, dt=F32, ctx=None):
        return (ctx or self.ctx).enter_context(self.nc.psum_tensor(self.place(name, ctx), shape, dt))

    def dram(self, name, shape, dt=F32):
        return self.nc.dram_tensor(name, shape, dt, kind="Internal").ap()


def spread(ap, shape):
    return ap.to_broadcast(list(shape))


def at_rows(ap):
    return bass.IndirectOffsetOnAxis(ap=ap, axis=0)



def start(c, g, a):
    nc = c.nc
    c.x = c.sb("x_now", [P, NC, D])
    c.ident = c.sb("ident", [P, P])
    c.iota_f = c.sb("iota_f", [P, P])
    c.iota_row = c.sb("iota_row", [P, P], BF16)
    c.before = c.sb("before", [P, P], BF16)
    c.ones = c.sb("ones", [P, P], BF16)
    c.node_of = c.sb("node_of", [P, NK, P])
    c.w0a = c.sb("w0a", [P, D])
    c.w0b = c.sb("w0b", [D, D])
    c.bias0 = c.sb("bias0", [P, D])
    c.w1h = [c.sb(f"w1h{i}", [min(P, HEADS * D - P * i), D]) for i in range(3)]
    c.wa = c.sb("wa", [D, 2 * HEADS])
    c.bias1 = c.sb("bias1", [P, D])
    c.wf = [c.sb(f"wf{l}", [D, P]) for l in range(N_LAYERS)]
    c.bf = [c.sb(f"bf{l}", [P, 1]) for l in range(N_LAYERS)]
    c.wuv = [c.sb(f"wuv{l}", [P, P]) for l in range(N_LAYERS)]
    c.buv = [c.sb(f"buv{l}", [P, D]) for l in range(N_LAYERS)]
    c.w2 = [c.sb(f"w2{l}", [P, D]) for l in range(N_LAYERS)]
    c.b2 = [c.sb(f"b2{l}", [P, 1]) for l in range(N_LAYERS)]
    c.w3loop = c.sb("w3loop", [D, D])
    c.bias3 = c.sb("bias3", [P, D])
    c.eps = c.sb("eps", [P, 1])

    full = N_NODES // NC
    rest = N_NODES - full * NC
    with ExitStack() as ctx:
        w1 = c.sb("w1", [D, HEADS * D], ctx=ctx)
        att = c.sb("att", [D, 2, HEADS * D], ctx=ctx)
        seed = c.sb("seed", [P, 2 * len(c.gathered_by_turn + g.gathered_by_turn)], ctx=ctx)

        def row(v):
            return spread(v.rearrange("(a n) -> a n", a=1), [P, v.shape[0]])

        loads = [
            (c.x[0:96, :, :], a["x"][0:96 * NC, :].rearrange("(p c) f -> p c f", c=NC)),
            (c.x[96:full, :, :], a["x"][96 * NC:full * NC, :].rearrange("(p c) f -> p c f", c=NC)),
            (c.x[full:full + 1, 0:rest, :], a["x"][full * NC:N_NODES, :].rearrange("(p c) f -> p c f", p=1)),
            (c.w0a[:], a["L0_gnn_W"][0:P, :]),
            (c.w0b[:], a["L0_gnn_W"][P:3 * D, :]),
            (c.bias0[:], row(a["L0_gnn_b"])),
            (w1[:], a["L1_gnn_W"]),
            (c.bias1[:], row(a["L1_gnn_bias"])),
            (c.w3loop[:], a["L3_gnn_loop_weight"]),
            (c.bias3[:], row(a["L3_gnn_h_bias"])),
        ]
        for h in range(HEADS):
            loads.append((c.w1h[h // 2][D * (h % 2):D * (h % 2) + D, :], a["L1_gnn_W"][:, h * D:(h + 1) * D]))
        for k, name in enumerate(("L1_gnn_att_src", "L1_gnn_att_dst")):
            flat = a[name].rearrange("(a h) d -> a (h d)", a=1)
            loads.append((att[:, k, :], spread(flat, [D, HEADS * D])))
        for l in range(N_LAYERS):
            loads += [
                (c.wf[l][:, 0:D], a["L2_gnn_nb_W"][l]),
                (c.wf[l][:, D:P], a["L2_gnn_self_W"][l]),
                (c.bf[l][0:D, :], a["L2_gnn_nb_b"][l].rearrange("(n a) -> n a", a=1)),
                (c.bf[l][D:P, :], a["L2_gnn_self_b"][l].rearrange("(n a) -> n a", a=1)),
                (c.wuv[l][0:D, 0:D], a["L2_gnn_att1_W"][l, 0:D, :]),
                (c.wuv[l][D:P, D:P], a["L2_gnn_att1_W"][l, D:P, :]),
                (c.buv[l][:], row(a["L2_gnn_att1_b"][l])),
                (c.w2[l][:], row(a["L2_gnn_att2_W"][l].rearrange("n a -> (n a)"))),
                (c.b2[l][:], row(a["L2_gnn_att2_b"][l])),
            ]
        by_pool = [s for pair in c.gathered_by_turn + g.gathered_by_turn for s in pair]
        signals = c.signals() + g.signals()
        by_sp = [s for s in signals if s.dma and s not in by_pool]

        with nc.Block() as block:
            @block.gpsimd
            def _(pool):
                st = Steps(pool, c.pool_step)
                st.mark(nc.gpsimd.memset(c.ident[:], 0.0))
                st.mark(nc.gpsimd.memset(c.before[:], 0.0))
                st.mark(nc.gpsimd.iota(c.iota_f[:], [[1, P]], base=0, channel_multiplier=0,
                                       allow_small_or_imprecise_dtypes=True))
                st.mark(nc.gpsimd.iota(c.node_of[:], [[1, NK], [NC, P]], base=0, channel_multiplier=0,
                                       allow_small_or_imprecise_dtypes=True))
                st.wait()
                st.mark(nc.gpsimd.affine_select(out=c.ident[:], in_=c.ident[:], compare_op=ALU.not_equal, fill=1.0,
                                                base=0, pattern=[[-1, P]], channel_multiplier=1))
                st.mark(nc.gpsimd.affine_select(out=c.before[:], in_=c.before[:], compare_op=ALU.is_ge, fill=1.0,
                                                base=0, pattern=[[-1, P]], channel_multiplier=1))
                st.wait()
                st.close()
                for k, s in enumerate(by_pool):
                    pool.dma_start(seed[:, k:k + 1], spread(a["x"][0:1, 0:1], [P, 1])).then_inc(s.sem, 16)
                    s.counted(16)
                    pool.wait_ge(s.sem, 16)

            @block.vector
            def _(dve):
                st = Steps(dve, c.dve_step)
                st.mark(nc.vector.memset(c.x[:], 0.0))
                for l in range(N_LAYERS):
                    st.mark(nc.vector.memset(c.wuv[l][:], 0.0))
                st.mark(nc.vector.memset(c.ones[:], 1.0))
                st.mark(nc.vector.memset(c.eps[:], 1e-5))
                for s in signals:
                    if not s.dma and s not in (c.dve_step, c.pool_step):
                        dve.sem_inc(s.sem, 1)
                        s.counted(1)
                dve.wait_ge(c.pool_step.sem, 4)
                st.mark(nc.vector.tensor_copy(c.iota_row[:], c.iota_f[:]))
                for k, s in enumerate(by_sp):
                    dve.wait_ge(s.sem, 16 * len(loads[k::len(by_sp)]))
                st.then(nc.vector.tensor_tensor(att[:], att[:], spread(w1[:][:, None, :], [D, 2, HEADS * D]), ALU.mult))
                st.then(nc.vector.tensor_reduce(c.wa[:], att[:].rearrange("p a (h d) -> p (a h) d", h=HEADS),
                                                AX_X, ALU.add))
                st.close()

            @block.sync
            def _(sp):
                sp.wait_ge(c.dve_step.sem, 1 + N_LAYERS)
                for k, (dst, src) in enumerate(loads):
                    s = by_sp[k % len(by_sp)]
                    sp.dma_start(dst, src).then_inc(s.sem, 16)
                    s.counted(16)
        c.end_phase()
        g.end_phase()



class Order:

    def __init__(self, c, name, fields):
        self.name, self.fields = name, fields
        self.list = c.dram(f"{name}_list", [EP + 2, fields], I32)
        self.spare = c.dram(f"{name}_spare", [EP + 2, fields], I32)
        self.rows_d = c.dram(f"{name}_rows", [3, NP])
        self.keep = c.sb(f"{name}_keep", [P, EC])
        self.spill = c.sb(f"{name}_spill", [P, 1])
        self.spill_at = c.sb(f"{name}_spill_at", [P, 2 * NIT])
        self.first_key = c.sb(f"{name}_first_key", [P, 1], I32)
        self.last_row = c.sb(f"{name}_last_row", [P, NC], I32)
        self.first_row = c.sb(f"{name}_first_row", [P, NC], I32)
        self.degree = c.sb(f"{name}_degree", [P, NC])


def records(edge_list):
    return edge_list[1:EP + 1, :].rearrange("(p j) r -> p j r", j=EC)


def write_list(c, order, columns):
    nc = c.nc
    full = N_EDGES // EC
    rest = N_EDGES - full * EC
    cuts = [0, 112, full - 1, full]
    with ExitStack() as ctx:
        cols = c.sb("list_cols", [P, len(columns), EC], I32, ctx)
        recs = c.sb("list_recs", [P, EC, order.fields], I32, ctx)
        ends = c.sb("list_ends", [2, order.fields], I32, ctx)
        with nc.Block() as block:
            @block.vector
            def _(dve):
                st = Steps(dve, c.dve_step)
                for f in range(len(columns)):
                    st.mark(nc.vector.memset(cols[:, f, :], 0 if f else PAD_NODE))
                st.mark(nc.vector.memset(ends[:], -1))
                dve.wait_ge(c.moved.sem, c.moved.at(16 * 4 * len(columns)))
                for f in range(len(columns)):
                    st.mark(nc.vector.tensor_copy(recs[:, :, f], cols[:, f, :]))
                st.close()

            @block.sync
            def _(sp):
                sp.wait_ge(c.dve_step.sem, c.dve_step.at(len(columns) + 1))
                for f, e in enumerate(columns):
                    for lo, hi in zip(cuts, cuts[1:]):
                        sp.dma_start(cols[lo:hi, f, :],
                                     e[lo * EC:hi * EC].rearrange("(p j) -> p j", j=EC)).then_inc(c.moved.sem, 16)
                    sp.dma_start(cols[full:full + 1, f, 0:rest],
                                 e[full * EC:N_EDGES].rearrange("(p j) -> p j", p=1)).then_inc(c.moved.sem, 16)
                sp.wait_ge(c.dve_step.sem, c.dve_step.at(2 * len(columns) + 1))
                sp.dma_start(records(order.list), recs[:]).then_inc(c.moved.sem, 16)
                for edge_list in (order.list, order.spare):
                    sp.dma_start(edge_list[0:1, :], ends[0:1, :]).then_inc(c.moved.sem, 16)
                    sp.dma_start(edge_list[EP + 1:EP + 2, :], ends[1:2, :]).then_inc(c.moved.sem, 16)
                c.moved.counted(16 * (4 * len(columns) + 5))
                sp.wait_ge(c.moved.sem, c.moved.at(16 * (4 * len(columns) + 5)))
        c.end_phase()


def split_bytes(nc, st, parts, whole_i, tmp_i, n):
    for k in range(n):
        st.then(nc.vector.tensor_scalar(tmp_i, whole_i, 0xFF << (8 * k), None, ALU.bitwise_and))
        st.then(nc.vector.tensor_copy(parts[k], tmp_i))


def find_disorder(c, order, flag):
    nc = c.nc
    with ExitStack() as ctx:
        recs = c.sb("recs", [P, EC, order.fields], I32, ctx)
        next_key = c.sb("next_key", [P, 1], I32, ctx)
        falls = c.sb("falls", [P, EC], ctx=ctx)
        any_fall = c.sb("any_fall", [P, 1], ctx=ctx)
        any_bf = c.sb("any_bf", [P, 1], BF16, ctx)
        where = c.ps("where", [P, 1], ctx=ctx)
        with nc.Block() as block:
            @block.sync
            def _(sp):
                sp.dma_start(recs[:], records(order.list)).then_inc(c.moved.sem, 16)
                beyond = order.list[2:EP + 2, :].rearrange("(p j) r -> p j r", j=EC)
                sp.dma_start(next_key[:], beyond[:, EC - 1, 0:1], allow_slow_non_contiguous=True).then_inc(c.moved.sem, 16)
                c.moved.counted(32)

            @block.vector
            def _(dve):
                st = Steps(dve, c.dve_step)
                st.then(nc.vector.memset(falls[:], 0.0))
                dve.wait_ge(c.moved.sem, c.moved.at(32))
                st.mark(nc.vector.tensor_tensor(falls[:, 0:EC - 1], recs[:, 0:EC - 1, 0], recs[:, 1:EC, 0], ALU.is_gt))
                st.then(nc.vector.tensor_tensor(falls[0:P - 1, EC - 1:EC], recs[0:P - 1, EC - 1, 0:1],
                                                next_key[0:P - 1, :], ALU.is_gt))
                st.then(nc.vector.tensor_reduce(any_fall[:], falls[:], AX_X, ALU.max))
                st.then(nc.vector.tensor_copy(any_bf[:], any_fall[:]))
                dve.sem_inc(c.dve_gave.sem, 1)
                dve.wait_ge(c.pe_gave.sem, c.pe_gave.at(1))
                st.mark(nc.vector.tensor_scalar(flag[:], where[:], 1.0, None, ALU.min))
                st.close()

            @block.tensor
            def _(pe):
                pe.wait_ge(c.dve_gave.sem, c.dve_gave.at(1))
                nc.tensor.matmul(where[:], c.ones[:], any_bf[:], start=True, stop=True).then_inc(c.pe_gave.sem, 1)
        c.dve_gave.counted(1)
        c.pe_gave.counted(1)
        c.end_phase()


def radix_sort(c, order, g, flag=None):
    nc = c.nc
    R = order.fields
    passes = [(order.list, order.spare, 0), (order.spare, order.list, LOGB)]
    with ExitStack() as ctx:
        recs = c.sb("recs", [P, EC, R], I32, ctx)
        digit_i = c.sb("digit_i", [P, EC], I32, ctx)
        digit = c.sb("digit", [P, EC], ctx=ctx)
        match = c.sb("match", [P, EC], BF16, ctx)
        count = c.sb("count", [P, P], ctx=ctx)
        count_i = c.sb("count_i", [P, P], I32, ctx)
        part_i = c.sb("part_i", [P, P], I32, ctx)
        part = [c.sb(f"part{k}", [P, P], BF16, ctx) for k in range(2)]
        total = c.sb("total", [P, P], ctx=ctx)
        upto = c.sb("upto", [P, P], ctx=ctx)
        unit = c.sb("unit", [P, P], ctx=ctx)
        next_row = [c.sb(f"next_row{k}", [P, P], ctx=ctx) for k in range(2)]
        hot = [c.sb(f"hot{k}", [P, P], BF16, ctx) for k in range(2)]
        spent = c.sb("spent", [P, P], ctx=ctx)
        rank = [c.sb(f"rank{s}", [P, K], ctx=ctx) for s in range(2)]
        rank_i = [c.sb(f"rank_i{s}", [P, K], I32, ctx) for s in range(2)]
        digit_s = [c.sb(f"digit_s{s}", [P, K], ctx=ctx) for s in range(2)]
        send = [c.sb(f"send{s}", [P, K, R], I32, ctx) for s in range(2)]
        earlier = c.ps("earlier", [P, P], ctx=ctx)
        totals = c.ps("totals", [P, P], ctx=ctx)

        def if_wanted(eng, program):
            if flag is None:
                program()
            else:
                wanted = eng.value_load(flag[0:1, 0:1], min_val=0, max_val=1)
                with eng.If(wanted > 0):
                    program()

        def load(sp):
            for n, (source, _, _) in enumerate(passes):
                if n:
                    for s in range(2):
                        sp.wait_ge(g.gathered[s].sem, g.gathered[s].at(16 * K * EIT))
                sp.dma_start(recs[:], records(source)).then_inc(g.moved.sem, 16)

        def rank_edges(dve):
            for n, (_, _, shift) in enumerate(passes):
                st = Steps(dve, g.dve_step)
                dve.wait_ge(g.moved.sem, g.moved.at(16 * n + 16))
                st.then(nc.vector.tensor_scalar(digit_i[:], recs[:, :, 0], shift, P - 1,
                                                ALU.arith_shift_right, ALU.bitwise_and))
                st.mark(nc.vector.memset(unit[:], 1.0))
                st.then(nc.vector.tensor_copy(digit[:], digit_i[:]))
                dve.sem_inc(g.dve_gave.sem, 1)
                st.close()
                with dve.Fori(0, P) as d:
                    st = Steps(dve, g.dve_step, d, 1)
                    st.then(nc.vector.tensor_scalar(match[:], digit[:], c.iota_f[:, bass.ds(d, 1)], 0.0, ALU.is_equal,
                                                    ALU.add, accum_out=count[:, bass.ds(d, 1)]))
                st.close(P)
                st = Steps(dve, g.dve_step)
                st.then(nc.vector.tensor_copy(count_i[:], count[:]))
                split_bytes(nc, st, [t[:] for t in part], count_i[:], part_i[:], 2)
                dve.sem_inc(g.dve_gave.sem, 1)
                dve.wait_ge(g.pe_gave.sem, g.pe_gave.at(2 * n + 2))
                st.then(nc.vector.tensor_copy(total[:], totals[:]))
                st.then(nc.vector.tensor_tensor_scan(upto[:], unit[:], total[:], 1.0, ALU.mult, ALU.add))
                st.then(nc.vector.tensor_tensor(upto[:], upto[:], total[:], ALU.subtract))
                st.then(nc.vector.tensor_tensor(next_row[0][:], earlier[:], upto[:], ALU.add))
                st.close()
                with dve.Fori(0, EIT) as i:
                    st = Steps(dve, g.dve_step, i, 2 * (3 * K + 1))
                    for s in range(2):
                        dve.wait_ge(g.staged[s].sem, g.staged[s].at(2 * i + (2 * EIT * n + 2)))
                        for k in range(K):
                            st.mark(nc.vector.tensor_scalar(hot[k % 2][:], c.iota_row[:], digit_s[s][:, k:k + 1], None,
                                                            ALU.is_equal))
                            st.wait()
                            st.mark(nc.vector.tensor_tensor_reduce(spent[:], hot[k % 2][:], next_row[k % 2][:], 1.0, 0.0,
                                                                   ALU.mult, ALU.add, rank[s][:, k:k + 1]))
                            st.mark(nc.vector.tensor_tensor(next_row[1 - k % 2][:], next_row[k % 2][:], hot[k % 2][:],
                                                            ALU.add))
                        st.wait()
                        dve.wait_ge(g.gathered[s].sem, g.gathered[s].at(16 * K * i + 16 * K * EIT * n))
                        st.then(nc.vector.tensor_copy(rank_i[s][:], rank[s][:]))
                        dve.sem_inc(g.computed[s].sem, 1)
                st.close(EIT)

        def count_before(pe):
            for n in range(2):
                pe.wait_ge(g.dve_gave.sem, g.dve_gave.at(2 * n + 2))
                for k in range(2):
                    last = nc.tensor.matmul(earlier[:], c.before[:], part[k][:], start=k == 0, stop=k == 1)
                last.then_inc(g.pe_gave.sem, 1)
                for k in range(2):
                    last = nc.tensor.matmul(totals[:], c.ones[:], part[k][:], start=k == 0, stop=k == 1)
                last.then_inc(g.pe_gave.sem, 1)

        def stage(act):
            for n in range(2):
                act.wait_ge(g.dve_gave.sem, g.dve_gave.at(2 * n + 1))
                with act.Fori(0, EIT) as i:
                    for s in range(2):
                        here = bass.ds(2 * K * i + s * K, K)
                        act.wait_ge(g.computed[s].sem, g.computed[s].at(i + EIT * n))
                        act.wait_ge(g.gathered[s].sem, g.gathered[s].at(16 * K * i + 16 * K * EIT * n))
                        nc.scalar.activation(digit_s[s][:], digit[:, here], ACT.Copy).then_inc(g.staged[s].sem, 1)
                        nc.scalar.activation(send[s][:], recs[:, here, :], ACT.Copy).then_inc(g.staged[s].sem, 1)

        def send_records(pool):
            for n, (_, target, _) in enumerate(passes):
                with pool.Fori(0, EIT) as i:
                    for s in range(2):
                        pool.wait_ge(g.staged[s].sem, g.staged[s].at(2 * i + (2 * EIT * n + 2)))
                        pool.wait_ge(g.computed[s].sem, g.computed[s].at(i + (EIT * n + 1)))
                        pool.sem_inc(g.pool_turn.sem, 1)
                        for k in range(K):
                            pool.indirect_dma_start(out=target, out_offset=at_rows(rank_i[s][:, k:k + 1]),
                                                    in_=send[s][:, k, :], in_offset=None).then_inc(g.gathered[s].sem, 16)
            for s in range(2):
                pool.wait_ge(g.gathered[s].sem, g.gathered[s].at(2 * 16 * K * EIT))

        with nc.Block() as block:
            @block.sync
            def _(sp):
                if_wanted(sp, lambda: load(sp))

            @block.vector
            def _(dve):
                if_wanted(dve, lambda: rank_edges(dve))

            @block.tensor
            def _(pe):
                if_wanted(pe, lambda: count_before(pe))

            @block.scalar
            def _(act):
                if_wanted(act, lambda: stage(act))

            @block.gpsimd
            def _(pool):
                if_wanted(pool, lambda: send_records(pool))
        g.moved.counted(32)
        g.dve_gave.counted(4)
        g.pe_gave.counted(4)
        for s in range(2):
            g.gathered[s].counted(2 * 16 * K * EIT)
            g.computed[s].counted(2 * EIT)
            g.staged[s].counted(4 * EIT)
        g.end_phase()
        if g is not c:
            c.end_phase()


def read_order(c, order, neighbours):
    nc = c.nc
    R = order.fields
    with ExitStack() as ctx:
        recs = c.sb("recs", [P, EC, R], I32, ctx)
        next_key = c.sb("next_key", [P, 1], I32, ctx)
        same = c.sb("same", [P, 1], ctx=ctx)
        digit_i = c.sb("digit_i", [P, 2, EC], I32, ctx)
        digit = c.sb("digit", [P, 2, EC], ctx=ctx)
        hot = [c.sb(f"hot{s}", [P, 2, K, P], BF16, ctx) for s in range(2)]
        nothing = c.sb("nothing", [P, P], BF16, ctx)
        unit = c.sb("unit", [P, P], ctx=ctx)
        cnt = c.sb("cnt", [P, P], ctx=ctx)
        upto = c.sb("upto", [P, P], ctx=ctx)
        tot_i = c.sb("tot_i", [P, 1], I32, ctx)
        byte_i = c.sb("byte_i", [P, 1], I32, ctx)
        byte = [c.sb(f"byte{k}", [P, 1], BF16, ctx) for k in range(3)]
        first = c.sb("first", [P, P], ctx=ctx)
        has = c.sb("has", [P, P], ctx=ctx)
        spare_row = c.sb("spare_row", [P, P], ctx=ctx)
        found = c.sb("found", [P, 3, P], ctx=ctx)
        back = c.sb("back", [P, 3, NC], ctx=ctx)
        counts = c.ps("counts", [P, P], ctx=ctx)
        before = c.ps("rows_before", [P, 1], ctx=ctx)
        hi_rows = NP // P

        with nc.Block() as block:
            @block.gpsimd
            def _(pool):
                st = Steps(pool, c.pool_step)
                st.mark(nc.gpsimd.iota(spare_row[:], [[1, P]], base=EP + 1, channel_multiplier=P,
                                       allow_small_or_imprecise_dtypes=True))
                st.close()

            @block.sync
            def _(sp):
                sp.dma_start(recs[:], records(order.list)).then_inc(c.moved.sem, 16)
                beyond = order.list[2:EP + 2, :].rearrange("(p j) r -> p j r", j=EC)
                sp.dma_start(next_key[:], beyond[:, EC - 1, 0:1], allow_slow_non_contiguous=True).then_inc(c.moved.sem, 16)
                sp.wait_ge(c.dve_gave.sem, c.dve_gave.at(2))
                for f in range(3):
                    sp.dma_start(order.rows_d[f].rearrange("(p n) -> p n", n=P), found[0:hi_rows, f, :]).then_inc(c.moved.sem, 16)
                sp.wait_ge(c.moved.sem, c.moved.at(16 * 5))
                for f in range(3):
                    sp.dma_start(back[:, f, :], order.rows_d[f].rearrange("(p n) -> p n", n=NC)).then_inc(c.moved.sem, 16)
                c.moved.counted(16 * 8)

            @block.vector
            def _(dve):
                st = Steps(dve, c.dve_step)
                st.mark(nc.vector.memset(order.keep[:, 0:1], 0.0))
                st.mark(nc.vector.memset(nothing[:], 0.0))
                st.mark(nc.vector.memset(unit[:], 1.0))
                dve.wait_ge(c.moved.sem, c.moved.at(32))
                st.mark(nc.vector.tensor_tensor(order.keep[:, 1:EC], recs[:, 1:EC, 0], recs[:, 0:EC - 1, 0], ALU.is_equal))
                st.mark(nc.vector.tensor_copy(order.first_key[:], recs[:, 0, 0:1]))
                st.then(nc.vector.tensor_tensor(same[:], recs[:, EC - 1, 0:1], next_key[:], ALU.is_equal))
                st.then(nc.vector.tensor_scalar(order.spill[:], recs[:, EC - 1, 0:1], 1.0, None, ALU.add))
                st.then(nc.vector.tensor_tensor(order.spill[:], order.spill[:], same[:], ALU.mult))
                st.then(nc.vector.tensor_scalar(order.spill[:], order.spill[:], -1.0, None, ALU.add))
                for t in range(2 * NIT):
                    st.mark(nc.vector.tensor_scalar(order.spill_at[:, t:t + 1], order.spill[:], float(-NK * t), None, ALU.add))
                neighbours(nc, st, recs)
                st.mark(nc.vector.tensor_scalar(digit_i[:, 0, :], recs[:, :, 0], LOGB, None, ALU.arith_shift_right))
                st.then(nc.vector.tensor_scalar(digit_i[:, 1, :], recs[:, :, 0], P - 1, None, ALU.bitwise_and))
                st.then(nc.vector.tensor_copy(digit[:], digit_i[:]))
                dve.sem_inc(c.dve_gave.sem, 1)
                st.close()
                with dve.Fori(0, EIT) as i:
                    for s in range(2):
                        here = bass.ds(2 * K * i + s * K, K)
                        dve.wait_ge(c.taken[s].sem, c.taken[s].at(i))
                        for g in range(2):
                            nc.vector.tensor_tensor(
                                hot[s][:, g, :, :], spread(digit[:, g, here][:, :, None], [P, K, P]),
                                spread(c.iota_f[:][:, None, :], [P, K, P]), ALU.is_equal).then_inc(c.computed[s].sem, 1)
                for s in range(2):
                    c.computed[s].counted(2 * EIT)
                st = Steps(dve, c.dve_step)
                dve.wait_ge(c.pe_gave.sem, c.pe_gave.at(1))
                st.then(nc.vector.tensor_copy(cnt[:], counts[:]))
                st.then(nc.vector.tensor_tensor_scan(upto[:], unit[:], cnt[:], 0.0, ALU.mult, ALU.add))
                st.then(nc.vector.tensor_copy(tot_i[:], upto[:, P - 1:P]))
                split_bytes(nc, st, [b[:] for b in byte], tot_i[:], byte_i[:], 3)
                dve.sem_inc(c.dve_gave2.sem, 1)
                c.dve_gave2.counted(1)
                st.then(nc.vector.tensor_tensor(first[:], upto[:], cnt[:], ALU.subtract))
                dve.wait_ge(c.pe_gave.sem, c.pe_gave.at(2))
                st.then(nc.vector.tensor_copy(same[:], before[:]))
                st.then(nc.vector.tensor_scalar(first[:], first[:], same[:], None, ALU.add))
                st.mark(nc.vector.tensor_scalar(has[:], cnt[:], 1.0, None, ALU.min))
                st.then(nc.vector.tensor_tensor(found[:, 0, :], first[:], cnt[:], ALU.add))
                st.then(nc.vector.tensor_scalar(found[:, 0, :], found[:, 0, :], -1.0 - NO_EDGE_ROW, None, ALU.add))
                st.then(nc.vector.tensor_tensor(found[:, 0, :], found[:, 0, :], has[:], ALU.mult))
                st.then(nc.vector.tensor_scalar(found[:, 0, :], found[:, 0, :], float(NO_EDGE_ROW), None, ALU.add))
                dve.wait_ge(c.pool_step.sem, c.pool_step.at(1))
                st.then(nc.vector.tensor_tensor(found[:, 1, :], first[:], spare_row[:], ALU.subtract))
                st.then(nc.vector.tensor_tensor(found[:, 1, :], found[:, 1, :], has[:], ALU.mult))
                st.then(nc.vector.tensor_tensor(found[:, 1, :], found[:, 1, :], spare_row[:], ALU.add))
                st.then(nc.vector.tensor_copy(found[:, 2, :], cnt[:]))
                dve.sem_inc(c.dve_gave.sem, 1)
                c.dve_gave.counted(2)
                dve.wait_ge(c.moved.sem, c.moved.at(16 * 8))
                st.mark(nc.vector.tensor_copy(order.last_row[:], back[:, 0, :]))
                st.mark(nc.vector.tensor_copy(order.first_row[:], back[:, 1, :]))
                st.mark(nc.vector.tensor_copy(order.degree[:], back[:, 2, :]))
                st.close()

            @block.tensor
            def _(pe):
                pe.wait_ge(c.dve_step.sem, c.dve_step.at(2))
                nc.tensor.matmul(counts[:], nothing[:], nothing[:], start=True, stop=False, skip_group_check=True)
                with pe.Fori(0, EIT) as i:
                    for s in range(2):
                        pe.wait_ge(c.computed[s].sem, c.computed[s].at(2 * i + 2))
                        pe.sem_inc(c.pe_turn.sem, 1)
                        for k in range(K):
                            last = nc.tensor.matmul(counts[:], hot[s][:, 0, k, :], hot[s][:, 1, k, :],
                                                    start=False, stop=False, skip_group_check=True)
                        last.then_inc(c.taken[s].sem, 1)
                for s in range(2):
                    c.taken[s].counted(EIT)
                nc.tensor.matmul(counts[:], nothing[:], nothing[:], start=False, stop=True,
                                 skip_group_check=True).then_inc(c.pe_gave.sem, 1)
                pe.wait_ge(c.dve_gave2.sem, c.dve_gave2.at(1))
                for k in range(3):
                    last = nc.tensor.matmul(before[:], c.before[:], byte[k][:], start=k == 0, stop=k == 2)
                last.then_inc(c.pe_gave.sem, 1)
                c.pe_gave.counted(2)
        c.end_phase()



def edge_sum(c, order, neighbour, table, scanned, carry, weight=None):
    nc = c.nc
    with ExitStack() as ctx:
        rows = [c.sb(f"rows{s}", [P, K, D], ctx=ctx) for s in range(2)]
        index = [c.sb(f"index{s}", [P, K], I32, ctx) for s in range(2)]
        keep = [c.sb(f"keep{s}", [P, K], ctx=ctx) for s in range(2)]
        weigh = [c.sb(f"weigh{s}", [P, K], ctx=ctx) for s in range(2)]
        n_staged = 2 if weight is None else 3
        with nc.Block() as block:
            @block.scalar
            def _(act):
                with act.Fori(0, EIT) as i:
                    for s in range(2):
                        here = bass.ds(2 * K * i + s * K, K)
                        act.wait_ge(c.gathered[s].sem, c.gathered[s].at(16 * K * i))
                        act.wait_ge(c.computed[s].sem, c.computed[s].at(i))
                        nc.scalar.activation(index[s][:], neighbour[:, here], ACT.Copy).then_inc(c.staged[s].sem, 1)
                        nc.scalar.activation(keep[s][:], order.keep[:, here], ACT.Copy).then_inc(c.staged[s].sem, 1)
                        if weight is not None:
                            nc.scalar.activation(weigh[s][:], weight[:, here], ACT.Copy).then_inc(c.staged[s].sem, 1)

            @block.gpsimd
            def _(pool):
                with pool.Fori(0, EIT) as i:
                    for s in range(2):
                        pool.wait_ge(c.staged[s].sem, c.staged[s].at(n_staged * i + 1))
                        pool.wait_ge(c.stored[s].sem, c.stored[s].at(16 * i))
                        pool.wait_ge(c.computed[s].sem, c.computed[s].at(i))
                        pool.sem_inc(c.pool_turn.sem, 1)
                        for k in range(K):
                            pool.indirect_dma_start(out=rows[s][:, k, :], out_offset=None, in_=table,
                                                    in_offset=at_rows(index[s][:, k:k + 1])).then_inc(c.gathered[s].sem, 16)

            per = 2 * (D + 1 + (weight is not None))

            @block.vector
            def _(dve):
                st = Steps(dve, c.dve_step)
                st.then(nc.vector.memset(carry[:], 0.0))
                st.close()
                with dve.Fori(0, EIT) as i:
                    st = Steps(dve, c.dve_step, i, per)
                    for s in range(2):
                        dve.wait_ge(c.gathered[s].sem, c.gathered[s].at(16 * K * i + 16 * K))
                        dve.wait_ge(c.staged[s].sem, c.staged[s].at(n_staged * i + n_staged))
                        if weight is not None:
                            st.mark(nc.vector.tensor_tensor(rows[s][:], rows[s][:],
                                                            spread(weigh[s][:][:, :, None], [P, K, D]), ALU.mult))
                        st.wait()
                        for f in range(D):
                            st.mark(nc.vector.tensor_tensor_scan(rows[s][:, :, f], keep[s][:], rows[s][:, :, f],
                                                                 carry[:, f:f + 1], ALU.mult, ALU.add))
                        st.wait()
                        st.then(nc.vector.tensor_copy(carry[:], rows[s][:, K - 1, :]))
                        dve.sem_inc(c.computed[s].sem, 1)
                st.close(EIT)

            @block.sync
            def _(sp):
                out = scanned[0:EP, :].rearrange("(p j) f -> p j f", j=EC)
                with sp.Fori(0, EIT) as i:
                    for s in range(2):
                        sp.wait_ge(c.dve_step.sem, c.dve_step.at(1 + i * per + (s + 1) * per // 2 - 1))
                        sp.sem_inc(c.sp_turn.sem, 1)
                        sp.dma_start(out[:, bass.ds(2 * K * i + s * K, K), :], rows[s][:]).then_inc(c.stored[s].sem, 16)
                for s in range(2):
                    c.stored[s].counted(16 * EIT)
                    sp.wait_ge(c.stored[s].sem, c.stored[s].at(16 * EIT))
        for s in range(2):
            c.gathered[s].counted(16 * K * EIT)
            c.computed[s].counted(EIT)
            c.staged[s].counted(n_staged * EIT)
        c.end_phase()


def node_sums(c, order, scanned, carry, out):
    nc = c.nc
    W = out.shape[2]
    with ExitStack() as ctx:
        rows = [c.sb(f"rows{s}", [P, NK, W], ctx=ctx) for s in range(2)]
        index = [c.sb(f"index{s}", [P, NK], I32, ctx) for s in range(2)]
        spills = [c.sb(f"spills{s}", [P, NK, P], ctx=ctx) for s in range(2)]
        extra = [c.ps(f"extra{s}", [P, NK, W], ctx=ctx) for s in range(2)]
        with nc.Block() as block:
            @block.scalar
            def _(act):
                with act.Fori(0, NIT) as i:
                    for s in range(2):
                        act.wait_ge(c.gathered[s].sem, c.gathered[s].at(16 * NK * i))
                        nc.scalar.activation(index[s][:], order.last_row[:, bass.ds(2 * NK * i + s * NK, NK)],
                                             ACT.Copy).then_inc(c.staged[s].sem, 1)

            @block.gpsimd
            def _(pool):
                with pool.Fori(0, NIT) as i:
                    for s in range(2):
                        pool.wait_ge(c.staged[s].sem, c.staged[s].at(i + 1))
                        pool.wait_ge(c.computed[s].sem, c.computed[s].at(i))
                        pool.sem_inc(c.pool_turn.sem, 1)
                        for k in range(NK):
                            pool.indirect_dma_start(out=rows[s][:, k, :], out_offset=None, in_=scanned,
                                                    in_offset=at_rows(index[s][:, k:k + 1])).then_inc(c.gathered[s].sem, 16)

            @block.vector
            def _(dve):
                with dve.Fori(0, NIT) as i:
                    for s in range(2):
                        dve.wait_ge(c.pe_gave.sem, c.pe_gave.at(2 * i + s - 1))
                        nc.vector.tensor_scalar(spills[s][:], c.node_of[:], order.spill_at[:, bass.ds(2 * i + s, 1)], None,
                                                ALU.is_equal).then_inc(c.dve_gave.sem, 1)
                        dve.wait_ge(c.gathered[s].sem, c.gathered[s].at(16 * NK * i + 16 * NK))
                        dve.wait_ge(c.pe_gave.sem, c.pe_gave.at(2 * i + s + 1))
                        nc.vector.tensor_tensor(out[:, bass.ds(2 * NK * i + s * NK, NK), :], rows[s][:], extra[s][:],
                                                ALU.add).then_inc(c.computed[s].sem, 1)

            @block.tensor
            def _(pe):
                with pe.Fori(0, NIT) as i:
                    for s in range(2):
                        pe.wait_ge(c.dve_gave.sem, c.dve_gave.at(2 * i + s + 1))
                        pe.wait_ge(c.computed[s].sem, c.computed[s].at(i))
                        pe.sem_inc(c.pe_turn.sem, 1)
                        for k in range(NK):
                            last = nc.tensor.matmul(extra[s][:, k, :], spills[s][:, k, :], carry[:], start=True, stop=True)
                        last.then_inc(c.pe_gave.sem, 1)
        for s in range(2):
            c.gathered[s].counted(16 * NK * NIT)
            c.staged[s].counted(NIT)
            c.computed[s].counted(NIT)
        c.pe_gave.counted(2 * NIT)
        c.dve_gave.counted(2 * NIT)
        c.end_phase()


def node_scatter(c, order, values, first, filled):
    nc = c.nc
    W = values.shape[2]
    with ExitStack() as ctx:
        rows = [c.sb(f"rows{s}", [P, NK, W], ctx=ctx) for s in range(2)]
        index = [c.sb(f"index{s}", [P, NK], I32, ctx) for s in range(2)]
        begin = c.sb("begin", [P, W], ctx=ctx)
        with nc.Block() as block:
            @block.scalar
            def _(act):
                with act.Fori(0, NIT) as i:
                    for s in range(2):
                        here = bass.ds(2 * NK * i + s * NK, NK)
                        act.wait_ge(c.gathered[s].sem, c.gathered[s].at(16 * NK * i))
                        nc.scalar.activation(index[s][:], order.first_row[:, here], ACT.Copy).then_inc(c.staged[s].sem, 1)
                        nc.scalar.activation(rows[s][:], values[:, here, :], ACT.Copy).then_inc(c.staged[s].sem, 1)

            @block.gpsimd
            def _(pool):
                with pool.Fori(0, NIT) as i:
                    for s in range(2):
                        pool.wait_ge(c.staged[s].sem, c.staged[s].at(2 * i + 2))
                        pool.sem_inc(c.pool_turn.sem, 1)
                        for k in range(NK):
                            pool.indirect_dma_start(out=filled, out_offset=at_rows(index[s][:, k:k + 1]),
                                                    in_=rows[s][:, k, :], in_offset=None).then_inc(c.gathered[s].sem, 16)
                for s in range(2):
                    pool.wait_ge(c.gathered[s].sem, c.gathered[s].at(16 * NK * NIT))
                pool.indirect_dma_start(out=begin[:], out_offset=None, in_=first,
                                        in_offset=at_rows(order.first_key[:])).then_inc(c.gathered[0].sem, 16)

            @block.sync
            def _(sp):
                sp.wait_ge(c.gathered[1].sem, c.gathered[1].at(16 * NK * NIT))
                sp.wait_ge(c.gathered[0].sem, c.gathered[0].at(16 * NK * NIT + 16))
                sp.dma_start(filled[0:EP, :].rearrange("(p j) f -> p j f", j=EC)[:, 0, :], begin[:]).then_inc(c.moved.sem, 16)
                sp.wait_ge(c.moved.sem, c.moved.at(16))
        c.gathered[0].counted(16 * NK * NIT + 16)
        c.gathered[1].counted(16 * NK * NIT)
        for s in range(2):
            c.staged[s].counted(2 * NIT)
        c.moved.counted(16)
        c.end_phase()



def project(c, sources, weights, finish, finish_steps):
    nc = c.nc
    width = sum(x.shape[2] for x in sources)
    n = weights[0].shape[1]
    cuts = [(lo, min(lo + P, width)) for lo in range(0, width, P)]
    J, S = len(cuts), len(sources)
    with ExitStack() as ctx:
        side = c.sb("side", [P, NK, width], ctx=ctx)
        turned = [c.sb(f"turned{j}", [hi - lo, NK, P], ctx=ctx) for j, (lo, hi) in enumerate(cuts)]
        turn = c.ps("turn", [P, NK + 1, P], ctx=ctx)
        product = c.ps("product", [P, NK, n], ctx=ctx)
        with nc.Block() as block:
            @block.scalar
            def _(act):
                with act.Fori(0, 2 * NIT) as i:
                    here = bass.ds(NK * i, NK)
                    act.wait_ge(c.pe_gave.sem, c.pe_gave.at(J * i))
                    at = 0
                    for x in sources:
                        nc.scalar.activation(side[:, :, at:at + x.shape[2]], x[:, here, :], ACT.Copy)\
                            .then_inc(c.act_gave.sem, 1)
                        at += x.shape[2]
                    act.wait_ge(c.pe_gave2.sem, c.pe_gave2.at(i))
                    for j, (lo, hi) in enumerate(cuts):
                        act.wait_ge(c.pe_gave.sem, c.pe_gave.at(J * i + j + 1))
                        nc.scalar.activation(turned[j][:], turn[0:hi - lo, 0:NK, :], ACT.Copy)\
                            .then_inc(c.act_gave2.sem, 1)

            @block.tensor
            def _(pe):
                with pe.Fori(0, 2 * NIT) as i:
                    pe.wait_ge(c.act_gave.sem, c.act_gave.at(S * i + S))
                    pe.sem_inc(c.pe_turn.sem, 1)
                    for j, (lo, hi) in enumerate(cuts):
                        pe.wait_ge(c.act_gave2.sem, c.act_gave2.at(J * i + j))
                        pe.sem_inc(c.pe_turn.sem, 1)
                        for k in range(NK):
                            last = nc.tensor.transpose(turn[0:hi - lo, k, :], side[:, k, lo:hi], c.ident[:])
                        last.then_inc(c.pe_gave.sem, 1)
                    pe.wait_ge(c.act_gave2.sem, c.act_gave2.at(J * i + J))
                    pe.wait_ge(c.dve_gave.sem, c.dve_gave.at(i))
                    pe.sem_inc(c.pe_turn.sem, 1)
                    for k in range(NK):
                        for j in range(J):
                            last = nc.tensor.matmul(product[:, k, :], turned[j][:, k, :], weights[j],
                                                    start=j == 0, stop=j == J - 1)
                    last.then_inc(c.pe_gave2.sem, 1)

            @block.vector
            def _(dve):
                with dve.Fori(0, 2 * NIT) as i:
                    st = Steps(dve, c.dve_step, i, finish_steps)
                    dve.wait_ge(c.pe_gave2.sem, c.pe_gave2.at(i + 1))
                    finish(nc, st, bass.ds(NK * i, NK), product)
                    st.wait()
                    dve.sem_inc(c.dve_gave.sem, 1)
                st.close(2 * NIT)
        T = 2 * NIT
        c.act_gave.counted(S * T)
        c.act_gave2.counted(J * T)
        c.pe_gave.counted(J * T)
        c.pe_gave2.counted(T)
        c.dve_gave.counted(T)
        c.end_phase()


def vector_phase(c, work, stores=()):
    nc = c.nc
    roots = []
    with nc.Block() as block:
        @block.vector
        def _(dve):
            st = Steps(dve, c.dve_step)

            def by_act(func, out, in_, bias=0.0, scale=1.0):
                st.wait()
                roots.append((func, out, in_, bias, scale, st.base + st.k))
                dve.wait_ge(c.act_step.sem, c.act_step.at(len(roots)))

            work(nc, st, by_act)
            st.close()

        @block.scalar
        def _(act):
            for func, out, in_, bias, scale, when in roots:
                act.wait_ge(c.dve_step.sem, when)
                nc.scalar.activation(out, in_, func, bias=bias, scale=scale).then_inc(c.act_step.sem, 1)
            c.act_step.counted(len(roots))

        @block.sync
        def _(sp):
            sp.wait_ge(c.dve_step.sem, c.dve_step.at(c.dve_step.pending))
            for dst, src in stores:
                sp.dma_start(dst, src).then_inc(c.moved.sem, 16)
            c.moved.counted(16 * len(stores))
            sp.wait_ge(c.moved.sem, c.moved.at(16 * len(stores)))
    c.end_phase()


def node_rows(table):
    return table[0:NP, :].rearrange("(p c) f -> p c f", c=NC)


def whole(ap):
    return ap[:].rearrange("p c f -> p (c f)")


def layer_norm(c, nc, st, by_act, x, tmp, small):
    st.then(nc.vector.tensor_reduce(small[:], x[:], AX_X, ALU.add))
    st.then(nc.vector.tensor_scalar(small[:], small[:], 1.0 / D, None, ALU.mult))
    st.then(nc.vector.tensor_tensor(x[:], x[:], spread(small[:][:, :, None], [P, NC, D]), ALU.subtract))
    st.then(nc.vector.tensor_tensor(whole(tmp), whole(x), whole(x), ALU.mult))
    st.then(nc.vector.tensor_reduce(small[:], tmp[:], AX_X, ALU.add))
    by_act(ACT.Sqrt, small[:], small[:], c.eps[:], 1.0 / D)
    st.then(nc.vector.reciprocal(small[:], small[:]))
    st.then(nc.vector.tensor_tensor(x[:], x[:], spread(small[:][:, :, None], [P, NC, D]), ALU.mult))



def chebyshev_layer(c, order):
    with ExitStack() as ctx:
        norm = c.sb("norm", [P, NC], ctx=ctx)
        agg = c.sb("agg", [P, NC, D], ctx=ctx)
        x1 = c.sb("x1", [P, NC, D], ctx=ctx)
        by_norm = [P, NC, D]

        def first_table(nc, st, by_act):
            st.then(nc.vector.tensor_scalar(norm[:], order.degree[:], 1.0, None, ALU.max))
            by_act(ACT.Sqrt, norm[:], norm[:])
            st.then(nc.vector.reciprocal(norm[:], norm[:]))
            st.then(nc.vector.tensor_tensor(agg[:], c.x[:], spread(norm[:][:, :, None], by_norm), ALU.mult))

        vector_phase(c, first_table, [(node_rows(c.table), agg[:])])
        edge_sum(c, order, c.from_src, c.table, c.scanned, c.carry)
        node_sums(c, order, c.scanned, c.carry, agg)

        def second_table(nc, st, by_act):
            st.then(nc.vector.tensor_tensor(agg[:], agg[:], spread(norm[:][:, :, None], by_norm), ALU.mult))
            st.then(nc.vector.tensor_scalar(whole(x1), whole(agg), -1.0, None, ALU.mult))
            st.then(nc.vector.tensor_tensor(agg[:], x1[:], spread(norm[:][:, :, None], by_norm), ALU.mult))

        vector_phase(c, second_table, [(node_rows(c.table), agg[:])])
        edge_sum(c, order, c.from_src, c.table, c.scanned, c.carry)
        node_sums(c, order, c.scanned, c.carry, agg)

        def third(nc, st, by_act):
            st.then(nc.vector.tensor_tensor(agg[:], agg[:], spread(norm[:][:, :, None], by_norm), ALU.mult))
            st.then(nc.vector.scalar_tensor_tensor(out=whole(agg), in0=whole(agg), scalar=-2.0, in1=whole(c.x),
                                                   op0=ALU.mult, op1=ALU.subtract))

        vector_phase(c, third)

        def finish(nc, st, here, product):
            st.then(nc.vector.tensor_tensor(agg[:, here, :], product[:], spread(c.bias0[:][:, None, :], [P, NK, D]), ALU.add))
            st.mark(nc.vector.scalar_tensor_tensor(out=c.x[:, here, :], in0=agg[:, here, :], scalar=0.0,
                                                   in1=c.x[:, here, :], op0=ALU.max, op1=ALU.add))

        project(c, [c.x, x1, agg], [c.w0a[:], c.w0b[:]], finish, 2)
        vector_phase(c, lambda nc, st, by_act: layer_norm(c, nc, st, by_act, c.x, x1, norm))



def head_scores(c, scores):
    def finish(nc, st, here, product):
        st.mark(nc.vector.tensor_copy(scores[:, here, :], product[:]))

    project(c, [c.x], [c.wa[:]], finish, 1)


def attention_tables(c, scores, rows, a_dst):
    def work(nc, st, by_act):
        st.mark(nc.vector.memset(rows[:, :, D:TAB1], 1.0))
        st.mark(nc.vector.tensor_copy(a_dst[:], scores[:, :, HEADS:2 * HEADS]))
        st.then(nc.vector.tensor_copy(rows[:, :, 0:D], c.x[:]))
        st.then(nc.vector.tensor_copy(rows[:, :, D + 1:D + 1 + HEADS], scores[:, :, 0:HEADS]))

    vector_phase(c, work, [(node_rows(c.table1), rows[:]), (node_rows(c.a_dst_d), a_dst[:])])


def attention_edges(c, order, carry):
    nc = c.nc
    small = [P, K, HEADS]
    with ExitStack() as ctx:
        rows = [c.sb(f"rows{s}", [P, K, TAB1], ctx=ctx) for s in range(2)]
        index = [c.sb(f"index{s}", [P, K], I32, ctx) for s in range(2)]
        keep = [c.sb(f"keep{s}", [P, K], ctx=ctx) for s in range(2)]
        target = [c.sb(f"target{s}", small, ctx=ctx) for s in range(2)]
        sums = [c.sb(f"sums{s}", [P, K, HEADS, HW_], ctx=ctx) for s in range(2)]
        target_carry = c.sb("target_carry", [P, HEADS], ctx=ctx)
        reset = c.sb("reset", [P, K], ctx=ctx)
        raw = c.sb("raw", small, ctx=ctx)
        score = c.sb("score", small, ctx=ctx)
        top = c.sb("top", [P, K + 1, HEADS], ctx=ctx)
        gap = c.sb("gap", small, ctx=ctx)
        fall = c.sb("fall", small, ctx=ctx)
        power = c.sb("power", small, ctx=ctx)
        flat_carry = carry[:].rearrange("p h f -> p (h f)")
        PER_SLOT = HEADS + 1 + 1 + 1 + 1 + HEADS + 1 + 1 + 1 + 1 + HEADS * (D + 1) + 1 + 1 + 1

        with nc.Block() as block:
            @block.scalar
            def _(act):
                with act.Fori(0, EIT) as i:
                    for s in range(2):
                        here = bass.ds(2 * K * i + s * K, K)
                        act.wait_ge(c.gathered[s].sem, c.gathered[s].at(16 * K * i))
                        act.wait_ge(c.computed[s].sem, c.computed[s].at(i))
                        nc.scalar.activation(index[s][:], c.from_src[:, here], ACT.Copy).then_inc(c.staged[s].sem, 1)
                        nc.scalar.activation(keep[s][:], order.keep[:, here], ACT.Copy).then_inc(c.staged[s].sem, 1)
                    for s in range(2):
                        act.wait_ge(c.dve_gave.sem, c.dve_gave.at(2 * (2 * i + s) + 1))
                        nc.scalar.activation(fall[:], gap[:], ACT.Exp).then_inc(c.act_gave.sem, 1)
                        act.wait_ge(c.dve_gave.sem, c.dve_gave.at(2 * (2 * i + s) + 2))
                        nc.scalar.activation(power[:], score[:], ACT.Exp).then_inc(c.act_gave.sem, 1)

            @block.gpsimd
            def _(pool):
                with pool.Fori(0, EIT) as i:
                    for s in range(2):
                        pool.wait_ge(c.staged[s].sem, c.staged[s].at(2 * i + 1))
                        pool.wait_ge(c.computed[s].sem, c.computed[s].at(i))
                        pool.sem_inc(c.pool_turn.sem, 1)
                        for k in range(K):
                            pool.indirect_dma_start(out=rows[s][:, k, :], out_offset=None, in_=c.table1,
                                                    in_offset=at_rows(index[s][:, k:k + 1])).then_inc(c.gathered[s].sem, 16)

            @block.sync
            def _(sp):
                fill = c.fill1[0:EP, :].rearrange("(p j) f -> p j f", j=EC)
                out = c.scanned1[0:EP, :].rearrange("(p j) f -> p j f", j=EC)
                with sp.Fori(0, EIT) as i:
                    for s in range(2):
                        sp.wait_ge(c.computed[s].sem, c.computed[s].at(i))
                        sp.sem_inc(c.sp_turn.sem, 1)
                        sp.dma_start(target[s][:], fill[:, bass.ds(2 * K * i + s * K, K), :]).then_inc(c.loaded[s].sem, 16)
                    for s in range(2):
                        sp.wait_ge(c.computed[s].sem, c.computed[s].at(i + 1))
                        sp.sem_inc(c.sp_turn.sem, 1)
                        sp.dma_start(out[:, bass.ds(2 * K * i + s * K, K), :],
                                     sums[s][:].rearrange("p k h f -> p k (h f)")).then_inc(c.stored[s].sem, 16)
                for s in range(2):
                    c.stored[s].counted(16 * EIT)
                    c.loaded[s].counted(16 * EIT)
                    sp.wait_ge(c.stored[s].sem, c.stored[s].at(16 * EIT))

            @block.vector
            def _(dve):
                st = Steps(dve, c.dve_step)
                st.mark(nc.vector.memset(carry[:], 0.0))
                st.mark(nc.vector.memset(target_carry[:], 0.0))
                st.then(nc.vector.memset(top[:, K, :], -BIG))
                st.then(nc.vector.tensor_copy(top[:, 0, :], top[:, K, :]))
                st.close()
                with dve.Fori(0, EIT) as i:
                    st = Steps(dve, c.dve_step, i, 2 * PER_SLOT)
                    for s in range(2):
                        each = [P, K, HEADS]
                        dve.wait_ge(c.loaded[s].sem, c.loaded[s].at(16 * i + 16))
                        dve.wait_ge(c.staged[s].sem, c.staged[s].at(2 * i + 2))
                        st.wait()
                        for h in range(HEADS):
                            st.mark(nc.vector.tensor_tensor_scan(target[s][:, :, h], keep[s][:], target[s][:, :, h],
                                                                 target_carry[:, h:h + 1], ALU.mult, ALU.add))
                        st.then(nc.vector.tensor_scalar(reset[:], keep[s][:], -1.0, BIG, ALU.add, ALU.mult))
                        dve.wait_ge(c.gathered[s].sem, c.gathered[s].at(16 * K * i + 16 * K))
                        st.then(nc.vector.tensor_tensor(raw[:], rows[s][:, :, D + 1:D + 1 + HEADS], target[s][:], ALU.add))
                        st.then(nc.vector.scalar_tensor_tensor(out=score[:], in0=raw[:], scalar=0.2, in1=raw[:],
                                                               op0=ALU.mult, op1=ALU.max))
                        st.mark(nc.vector.tensor_copy(target_carry[:], target[s][:, K - 1, :]))
                        for h in range(HEADS):
                            st.mark(nc.vector.tensor_tensor_scan(top[:, 1:K + 1, h], reset[:], score[:, :, h],
                                                                 top[:, 0, h:h + 1], ALU.add, ALU.max))
                        st.wait()
                        st.then(nc.vector.tensor_tensor(gap[:], top[:, 0:K, :], top[:, 1:K + 1, :], ALU.subtract))
                        st.then(nc.vector.tensor_tensor(gap[:], gap[:], spread(reset[:][:, :, None], each), ALU.add))
                        dve.sem_inc(c.dve_gave.sem, 1)
                        st.then(nc.vector.tensor_tensor(score[:], score[:], top[:, 1:K + 1, :], ALU.subtract))
                        dve.sem_inc(c.dve_gave.sem, 1)
                        dve.wait_ge(c.stored[s].sem, c.stored[s].at(16 * i))
                        dve.wait_ge(c.act_gave.sem, c.act_gave.at(2 * (2 * i + s) + 2))
                        st.then(nc.vector.tensor_tensor(sums[s][:, :, :, 0:D + 1],
                                                        spread(rows[s][:, :, None, 0:D + 1], [P, K, HEADS, D + 1]),
                                                        spread(power[:][:, :, :, None], [P, K, HEADS, D + 1]), ALU.mult))
                        for h in range(HEADS):
                            for f in range(D + 1):
                                st.mark(nc.vector.tensor_tensor_scan(sums[s][:, :, h, f], fall[:, :, h], sums[s][:, :, h, f],
                                                                     carry[:, h, f:f + 1], ALU.mult, ALU.add))
                        st.mark(nc.vector.tensor_copy(sums[s][:, :, :, D + 1], top[:, 1:K + 1, :]))
                        st.wait()
                        st.mark(nc.vector.tensor_copy(carry[:], sums[s][:, K - 1, :, :]))
                        st.then(nc.vector.tensor_copy(top[:, 0, :], top[:, K, :]))
                        dve.sem_inc(c.computed[s].sem, 1)
                st.close(EIT)
        for s in range(2):
            c.gathered[s].counted(16 * K * EIT)
            c.computed[s].counted(EIT)
            c.staged[s].counted(2 * EIT)
        c.dve_gave.counted(4 * EIT)
        c.act_gave.counted(4 * EIT)
        c.end_phase()


def merge_carries(c, order, carry, merged):
    nc = c.nc
    with ExitStack() as ctx:
        tops = c.sb("tops", [P, P, HEADS], ctx=ctx)
        nodes = c.sb("nodes", [P, P], ctx=ctx)
        follow = c.sb("follow", [P, 1], ctx=ctx)
        last = c.sb("last", [P, 1], ctx=ctx)
        apart = c.sb("apart", [P, P], ctx=ctx)
        seen = c.sb("seen", [P, HEADS, P], ctx=ctx)
        top = c.sb("top", [P, HEADS], ctx=ctx)
        own = c.sb("own", [P, HEADS], ctx=ctx)
        scale = c.sb("scale", [P, HEADS], ctx=ctx)
        end = c.sb("end", [P, 1], ctx=ctx)
        wide = [P, HEADS, D + 1]
        with nc.Block() as block:
            @block.sync
            def _(sp):
                sp.wait_ge(c.dve_gave.sem, c.dve_gave.at(1))
                sp.dma_start(c.tops_d, own[:]).then_inc(c.moved.sem, 16)
                sp.dma_start(c.nodes_d[0:P, :], order.spill[:]).then_inc(c.moved.sem, 16)
                sp.dma_start(c.nodes_d[P:P + 1, :], end[0:1, :]).then_inc(c.moved.sem, 16)
                sp.wait_ge(c.moved.sem, c.moved.at(48))
                sp.dma_start(tops[:].rearrange("p q h -> p (q h)"),
                             spread(c.tops_d.rearrange("(a q) h -> a (q h)", a=1), [P, P * HEADS])).then_inc(c.moved.sem, 16)
                sp.dma_start(nodes[:], spread(c.nodes_d[0:P, :].rearrange("q a -> a q"), [P, P]),
                             allow_slow_non_contiguous=True).then_inc(c.moved.sem, 16)
                sp.dma_start(follow[:], c.nodes_d[1:P + 1, :]).then_inc(c.moved.sem, 16)
                c.moved.counted(96)

            @block.vector
            def _(dve):
                st = Steps(dve, c.dve_step)
                st.mark(nc.vector.memset(end[:], -2.0))
                st.then(nc.vector.tensor_copy(own[:], carry[:, :, D + 1]))
                dve.sem_inc(c.dve_gave.sem, 1)
                dve.wait_ge(c.moved.sem, c.moved.at(96))
                st.then(nc.vector.tensor_scalar(apart[:], nodes[:], order.spill[:], None, ALU.is_equal))
                st.then(nc.vector.tensor_scalar(apart[:], apart[:], -1.0, BIG, ALU.add, ALU.mult))
                st.then(nc.vector.tensor_tensor(seen[:], tops[:].rearrange("p q h -> p h q"),
                                                spread(apart[:][:, None, :], [P, HEADS, P]), ALU.add))
                st.then(nc.vector.tensor_reduce(top[:], seen[:], AX_X, ALU.max))
                st.then(nc.vector.tensor_tensor(scale[:], own[:], top[:], ALU.subtract))
                dve.sem_inc(c.dve_gave.sem, 1)
                st.then(nc.vector.tensor_tensor(last[:], follow[:], order.spill[:], ALU.is_equal))
                st.then(nc.vector.tensor_scalar(last[:], last[:], -1.0, 1.0, ALU.mult, ALU.add))
                st.mark(nc.vector.tensor_copy(merged[:, ROW1:ROW1 + 1], last[:]))
                grid = merged[:, 0:ROW1].rearrange("p (h f) -> p h f", h=HEADS)
                st.mark(nc.vector.tensor_scalar(grid[:, :, D + 1], top[:], last[:], None, ALU.mult))
                dve.wait_ge(c.act_gave.sem, c.act_gave.at(1))
                st.mark(nc.vector.tensor_tensor(grid[:, :, 0:D + 1], carry[:, :, 0:D + 1],
                                                spread(scale[:][:, :, None], wide), ALU.mult))
                st.close()

            @block.scalar
            def _(act):
                act.wait_ge(c.dve_gave.sem, c.dve_gave.at(2))
                nc.scalar.activation(scale[:], scale[:], ACT.Exp).then_inc(c.act_gave.sem, 1)
        c.dve_gave.counted(2)
        c.act_gave.counted(1)
        c.end_phase()


def attention_nodes(c, order, scores, merged, out):
    nc = c.nc
    cuts = [(lo, min(lo + P, HEADS * D)) for lo in range(0, HEADS * D, P)]
    J = len(cuts)
    with ExitStack() as ctx:
        rows = [c.sb(f"rows{s}", [P, NK, ROW1], ctx=ctx) for s in range(2)]
        index = [c.sb(f"index{s}", [P, NK], I32, ctx) for s in range(2)]
        spills = c.sb("spills", [P, NK, P], ctx=ctx)
        extra = c.sb("extra", [P, NK, ROW1 + 1], ctx=ctx)
        own = c.sb("own", [P, NC, HEADS], ctx=ctx)
        top = c.sb("top", [P, NK, HEADS], ctx=ctx)
        tops3 = c.sb("tops3", [P, 3, NK, HEADS], ctx=ctx)
        scale = c.sb("scale", [P, 3, NK, HEADS], ctx=ctx)
        mean = c.sb("mean", [P, NK, HEADS, D + 1], ctx=ctx)
        part = c.sb("part", [P, NK, HEADS, D + 1], ctx=ctx)
        weight = c.sb("weight", [P, NK, HEADS], ctx=ctx)
        normed = c.sb("normed", [P, NK, HEADS * D], ctx=ctx)
        turned = [c.sb(f"turned{j}", [hi - lo, NK, P], ctx=ctx) for j, (lo, hi) in enumerate(cuts)]
        spilled = [c.ps(f"spilled{k}", [P, 512], ctx=ctx) for k in range(2)]
        turn = c.ps("turn", [P, NK + 1, P], ctx=ctx)
        product = c.ps("product", [P, NK, D], ctx=ctx)
        T = 2 * NIT
        PER_SLOT = 20

        with nc.Block() as block:
            @block.gpsimd
            def _(pool):
                with pool.Fori(0, NIT) as i:
                    for s in range(2):
                        pool.wait_ge(c.staged[s].sem, c.staged[s].at(i + 1))
                        pool.wait_ge(c.computed[s].sem, c.computed[s].at(i))
                        pool.sem_inc(c.pool_turn.sem, 1)
                        for k in range(NK):
                            pool.indirect_dma_start(out=rows[s][:, k, :], out_offset=None, in_=c.scanned1,
                                                    in_offset=at_rows(index[s][:, k:k + 1])).then_inc(c.gathered[s].sem, 16)

            @block.tensor
            def _(pe):
                with pe.Fori(0, T) as i:
                    pe.wait_ge(c.dve_gave.sem, c.dve_gave.at(i + 1))
                    pe.sem_inc(c.pe_turn.sem, 1)
                    for k in range(NK):
                        pe.wait_ge(c.act_gave.sem, c.act_gave.at(NK * i + k - 1))
                        pe.sem_inc(c.pe_turn.sem, 1)
                        nc.tensor.matmul(spilled[k % 2][:, 0:ROW1 + 1], spills[:, k, :], merged[:],
                                         start=True, stop=True).then_inc(c.pe_gave.sem, 1)
                    pe.wait_ge(c.dve_gave2.sem, c.dve_gave2.at(i + 1))
                    pe.sem_inc(c.pe_turn.sem, 1)
                    for j, (lo, hi) in enumerate(cuts):
                        pe.wait_ge(c.act_gave2.sem, c.act_gave2.at(J * i + j))
                        pe.sem_inc(c.pe_turn.sem, 1)
                        for k in range(NK):
                            last = nc.tensor.transpose(turn[0:hi - lo, k, :], normed[:, k, lo:hi], c.ident[:])
                        last.then_inc(c.pe_gave2.sem, 1)
                    pe.wait_ge(c.act_gave2.sem, c.act_gave2.at(J * i + J))
                    pe.wait_ge(c.taken[0].sem, c.taken[0].at(i))
                    pe.sem_inc(c.pe_turn.sem, 1)
                    for k in range(NK):
                        for j in range(J):
                            last = nc.tensor.matmul(product[:, k, :], turned[j][:, k, :], c.w1h[j][:],
                                                    start=j == 0, stop=j == J - 1)
                    last.then_inc(c.taken[1].sem, 1)

            @block.scalar
            def _(act):
                with act.Fori(0, NIT) as i2:
                    for s in range(2):
                        act.wait_ge(c.gathered[s].sem, c.gathered[s].at(16 * NK * i2))
                        nc.scalar.activation(index[s][:], order.last_row[:, bass.ds(2 * NK * i2 + s * NK, NK)],
                                             ACT.Copy).then_inc(c.staged[s].sem, 1)
                    for s in range(2):
                        i = 2 * i2 + s
                        act.wait_ge(c.dve_gave2.sem, c.dve_gave2.at(i))
                        for k in range(NK):
                            act.wait_ge(c.pe_gave.sem, c.pe_gave.at(NK * i + k + 1))
                            nc.scalar.activation(extra[:, k, :], spilled[k % 2][:, 0:ROW1 + 1], ACT.Copy)\
                                .then_inc(c.act_gave.sem, 1)
                        act.wait_ge(c.loaded_by_dve.sem, c.loaded_by_dve.at(i + 1))
                        nc.scalar.activation(scale[:], tops3[:], ACT.Exp).then_inc(c.act_step.sem, 1)
                        act.wait_ge(c.taken[1].sem, c.taken[1].at(i))
                        for j, (lo, hi) in enumerate(cuts):
                            act.wait_ge(c.pe_gave2.sem, c.pe_gave2.at(J * i + j + 1))
                            nc.scalar.activation(turned[j][:], turn[0:hi - lo, 0:NK, :], ACT.Copy)\
                                .then_inc(c.act_gave2.sem, 1)

            @block.vector
            def _(dve):
                st = Steps(dve, c.dve_step)
                st.then(nc.vector.tensor_tensor(own[:], scores[:, :, 0:HEADS], scores[:, :, HEADS:2 * HEADS], ALU.add))
                st.then(nc.vector.scalar_tensor_tensor(out=own[:], in0=own[:], scalar=0.2, in1=own[:],
                                                       op0=ALU.mult, op1=ALU.max))
                st.close()
                wide = [P, NK, HEADS, D + 1]
                with dve.Fori(0, NIT) as i2:
                    st = Steps(dve, c.dve_step, i2, 2 * PER_SLOT)
                    for s in range(2):
                        i = 2 * i2 + s
                        here = bass.ds(NK * i, NK)
                        got = rows[s][:].rearrange("p k (h f) -> p k h f", h=HEADS)
                        more = extra[:, :, 0:ROW1].rearrange("p k (h f) -> p k h f", h=HEADS)
                        dve.wait_ge(c.pe_gave.sem, c.pe_gave.at(NK * i))
                        st.then(nc.vector.tensor_scalar(spills[:], c.node_of[:], order.spill_at[:, bass.ds(i, 1)], None,
                                                        ALU.is_equal))
                        dve.sem_inc(c.dve_gave.sem, 1)
                        dve.wait_ge(c.act_gave.sem, c.act_gave.at(NK * i + NK))
                        dve.wait_ge(c.gathered[s].sem, c.gathered[s].at(16 * NK * i2 + 16 * NK))
                        st.then(nc.vector.tensor_scalar(weight[:], spread(extra[:, :, ROW1:ROW1 + 1], [P, NK, HEADS]),
                                                        -1.0, BIG, ALU.add, ALU.mult))
                        st.then(nc.vector.tensor_tensor(tops3[:, 1, :, :], more[:, :, :, D + 1], weight[:], ALU.add))
                        st.mark(nc.vector.tensor_copy(tops3[:, 0, :, :], got[:, :, :, D + 1]))
                        st.then(nc.vector.tensor_copy(tops3[:, 2, :, :], own[:, here, :]))
                        st.then(nc.vector.tensor_tensor(top[:], tops3[:, 0, :, :], tops3[:, 1, :, :], ALU.max))
                        st.then(nc.vector.tensor_tensor(top[:], top[:], tops3[:, 2, :, :], ALU.max))
                        st.then(nc.vector.tensor_tensor(tops3[:].rearrange("p a k h -> p a (k h)"),
                                                        tops3[:].rearrange("p a k h -> p a (k h)"),
                                                        spread(top[:].rearrange("p k h -> p (k h)")[:, None, :],
                                                               [P, 3, NK * HEADS]), ALU.subtract))
                        dve.sem_inc(c.loaded_by_dve.sem, 1)
                        dve.wait_ge(c.act_step.sem, c.act_step.at(i + 1))
                        by = [spread(scale[:, n, :, :][:, :, :, None], wide) for n in range(3)]
                        st.mark(nc.vector.tensor_tensor(mean[:], got[:, :, :, 0:D + 1], by[0], ALU.mult))
                        st.then(nc.vector.tensor_tensor(part[:], more[:, :, :, 0:D + 1], by[1], ALU.mult))
                        st.then(nc.vector.tensor_tensor(mean[:], mean[:], part[:], ALU.add))
                        st.mark(nc.vector.tensor_copy(part[:, :, :, D], scale[:, 2, :, :]))
                        st.then(nc.vector.tensor_tensor(part[:, :, :, 0:D],
                                                        spread(c.x[:, here, :][:, :, None, :], [P, NK, HEADS, D]),
                                                        spread(scale[:, 2, :, :][:, :, :, None], [P, NK, HEADS, D]), ALU.mult))
                        st.then(nc.vector.tensor_tensor(mean[:], mean[:], part[:], ALU.add))
                        st.then(nc.vector.tensor_scalar(weight[:], mean[:, :, :, D], 1e-16, None, ALU.add))
                        st.then(nc.vector.reciprocal(weight[:], weight[:]))
                        dve.wait_ge(c.taken[1].sem, c.taken[1].at(i))
                        st.then(nc.vector.tensor_tensor(normed[:].rearrange("p k (h f) -> p k h f", h=HEADS),
                                                        mean[:, :, :, 0:D],
                                                        spread(weight[:][:, :, :, None], [P, NK, HEADS, D]), ALU.mult))
                        dve.sem_inc(c.dve_gave2.sem, 1)
                        dve.sem_inc(c.computed[s].sem, 1)
                        dve.wait_ge(c.taken[1].sem, c.taken[1].at(i + 1))
                        st.then(nc.vector.scalar_tensor_tensor(out=out[:, here, :], in0=product[:], scalar=1.0 / HEADS,
                                                               in1=spread(c.bias1[:][:, None, :], [P, NK, D]),
                                                               op0=ALU.mult, op1=ALU.add))
                        dve.sem_inc(c.taken[0].sem, 1)
                        st.then(nc.vector.tensor_tensor(out[:, here, :], out[:, here, :], c.x[:, here, :], ALU.add))
                        st.then(nc.vector.tensor_tensor(out[:, here, :], out[:, here, :], c.x[:, here, :], ALU.add))
                st.close(NIT)
        for s in range(2):
            c.gathered[s].counted(16 * NK * NIT)
            c.staged[s].counted(NIT)
            c.computed[s].counted(NIT)
            c.taken[s].counted(T)
        c.dve_gave.counted(T)
        c.dve_gave2.counted(T)
        c.loaded_by_dve.counted(T)
        c.act_step.counted(T)
        c.act_gave.counted(NK * T)
        c.act_gave2.counted(J * T)
        c.pe_gave.counted(NK * T)
        c.pe_gave2.counted(J * T)
        c.end_phase()


def attention_layer(c, order):
    with ExitStack() as ctx:
        scores = c.sb("scores", [P, NC, 2 * HEADS], ctx=ctx)
        carry = c.sb("carry1", [P, HEADS, HW_], ctx=ctx)
        merged = c.sb("merged", [P, ROW1 + 1], ctx=ctx)
        with ExitStack() as ctx2:
            rows = c.sb("rows_of_x", [P, NC, TAB1], ctx=ctx2)
            a_dst = c.sb("a_dst", [P, NC, HEADS], ctx=ctx2)
            head_scores(c, scores)
            attention_tables(c, scores, rows, a_dst)
            node_scatter(c, order, a_dst, c.a_dst_d, c.fill1)
        attention_edges(c, order, carry)
        merge_carries(c, order, carry, merged)
        with ExitStack() as ctx2:
            new = c.sb("new", [P, NC, D], ctx=ctx2)
            attention_nodes(c, order, scores, merged, new)
            tmp_small = c.sb("small", [P, NC], ctx=ctx2)

            def work(nc, st, by_act):
                st.then(nc.vector.tensor_copy(whole(c.x), whole(new)))
                layer_norm(c, nc, st, by_act, c.x, new, tmp_small)

            vector_phase(c, work)



def edge_halves(c, l, x, u, v):
    nc = c.nc
    T = 2 * NIT
    HALF = NK * P // 2
    with ExitStack() as ctx:
        side = c.sb("side", [P, NK, D], ctx=ctx)
        turned = c.sb("turned", [D, NK * P], ctx=ctx)
        hidden = c.sb("hidden", [P, NK * P], ctx=ctx)
        turn = c.ps("turn", [D, NK + 1, P], ctx=ctx)
        inner = c.ps("inner", [P, 2, 512], ctx=ctx)
        outer = c.ps("outer", [P, NK + 1, P], ctx=ctx)
        with nc.Block() as block:
            @block.scalar
            def _(act):
                with act.Fori(0, T) as i:
                    act.wait_ge(c.pe_gave.sem, c.pe_gave.at(2 * i))
                    nc.scalar.activation(side[:], x[:, bass.ds(NK * i, NK), :], ACT.Copy).then_inc(c.act_gave.sem, 1)
                    act.wait_ge(c.pe_gave.sem, c.pe_gave.at(2 * i + 1))
                    nc.scalar.activation(turned[:], turn[:, 0:NK, :], ACT.Copy).then_inc(c.act_gave2.sem, 1)
                    act.wait_ge(c.pe_gave.sem, c.pe_gave.at(2 * i + 2))
                    act.wait_ge(c.pe_gave2.sem, c.pe_gave2.at(i))
                    for g in range(2):
                        nc.scalar.activation(hidden[:, HALF * g:HALF * g + HALF], inner[:, g, 0:HALF], ACT.Relu,
                                             bias=c.bf[l][:]).then_inc(c.act_gave2.sem, 1)

            @block.tensor
            def _(pe):
                with pe.Fori(0, T) as i:
                    pe.wait_ge(c.act_gave.sem, c.act_gave.at(i + 1))
                    pe.sem_inc(c.pe_turn.sem, 1)
                    for k in range(NK):
                        last = nc.tensor.transpose(turn[:, k, :], side[:, k, :], c.ident[:])
                    last.then_inc(c.pe_gave.sem, 1)
                    pe.wait_ge(c.act_gave2.sem, c.act_gave2.at(3 * i + 1))
                    pe.sem_inc(c.pe_turn.sem, 1)
                    for g in range(2):
                        last = nc.tensor.matmul(inner[:, g, 0:HALF], c.wf[l][:], turned[:, HALF * g:HALF * g + HALF],
                                                start=True, stop=True)
                    last.then_inc(c.pe_gave.sem, 1)
                    pe.wait_ge(c.act_gave2.sem, c.act_gave2.at(3 * i + 3))
                    pe.wait_ge(c.dve_gave.sem, c.dve_gave.at(2 * i))
                    pe.sem_inc(c.pe_turn.sem, 1)
                    for k in range(NK):
                        last = nc.tensor.matmul(outer[:, k, :], hidden[:, k * P:k * P + P], c.wuv[l][:],
                                                start=True, stop=True)
                    last.then_inc(c.pe_gave2.sem, 1)

            @block.vector
            def _(dve):
                with dve.Fori(0, T) as i:
                    here = bass.ds(NK * i, NK)
                    dve.wait_ge(c.pe_gave2.sem, c.pe_gave2.at(i + 1))
                    nc.vector.tensor_copy(u[:, here, :], outer[:, 0:NK, 0:D]).then_inc(c.dve_gave.sem, 1)
                    nc.vector.tensor_tensor(v[:, here, :], outer[:, 0:NK, D:P],
                                            spread(c.buv[l][:][:, None, :], [P, NK, D]), ALU.add)\
                        .then_inc(c.dve_gave.sem, 1)
        c.act_gave.counted(T)
        c.act_gave2.counted(3 * T)
        c.pe_gave.counted(2 * T)
        c.pe_gave2.counted(T)
        c.dve_gave.counted(2 * T)
        c.end_phase()


def edge_logits(c, l, order, logit):
    nc = c.nc
    with ExitStack() as ctx:
        rows = [c.sb(f"rows{s}", [P, K, D], ctx=ctx) for s in range(2)]
        fill = [c.sb(f"fill{s}", [P, K, D], ctx=ctx) for s in range(2)]
        index = [c.sb(f"index{s}", [P, K], I32, ctx) for s in range(2)]
        keep = [c.sb(f"keep{s}", [P, K], ctx=ctx) for s in range(2)]
        carry = c.sb("carry", [P, D], ctx=ctx)
        per = 2 * (D + 4)
        with nc.Block() as block:
            @block.scalar
            def _(act):
                with act.Fori(0, EIT) as i:
                    for s in range(2):
                        here = bass.ds(2 * K * i + s * K, K)
                        act.wait_ge(c.gathered[s].sem, c.gathered[s].at(16 * K * i))
                        act.wait_ge(c.computed[s].sem, c.computed[s].at(i))
                        nc.scalar.activation(index[s][:], c.from_dst[:, here], ACT.Copy).then_inc(c.staged[s].sem, 1)
                        nc.scalar.activation(keep[s][:], order.keep[:, here], ACT.Copy).then_inc(c.staged[s].sem, 1)

            @block.gpsimd
            def _(pool):
                with pool.Fori(0, EIT) as i:
                    for s in range(2):
                        pool.wait_ge(c.staged[s].sem, c.staged[s].at(2 * i + 1))
                        pool.wait_ge(c.computed[s].sem, c.computed[s].at(i))
                        pool.sem_inc(c.pool_turn.sem, 1)
                        for k in range(K):
                            pool.indirect_dma_start(out=rows[s][:, k, :], out_offset=None, in_=c.table,
                                                    in_offset=at_rows(index[s][:, k:k + 1])).then_inc(c.gathered[s].sem, 16)

            @block.sync
            def _(sp):
                src = c.fill[0:EP, :].rearrange("(p j) f -> p j f", j=EC)
                with sp.Fori(0, EIT) as i:
                    for s in range(2):
                        sp.wait_ge(c.computed[s].sem, c.computed[s].at(i))
                        sp.sem_inc(c.sp_turn.sem, 1)
                        sp.dma_start(fill[s][:], src[:, bass.ds(2 * K * i + s * K, K), :]).then_inc(c.loaded[s].sem, 16)

            @block.vector
            def _(dve):
                st = Steps(dve, c.dve_step)
                st.then(nc.vector.memset(carry[:], 0.0))
                st.close()
                with dve.Fori(0, EIT) as i:
                    st = Steps(dve, c.dve_step, i, per)
                    for s in range(2):
                        dve.wait_ge(c.loaded[s].sem, c.loaded[s].at(16 * i + 16))
                        dve.wait_ge(c.staged[s].sem, c.staged[s].at(2 * i + 2))
                        st.wait()
                        for f in range(D):
                            st.mark(nc.vector.tensor_tensor_scan(fill[s][:, :, f], keep[s][:], fill[s][:, :, f],
                                                                 carry[:, f:f + 1], ALU.mult, ALU.add))
                        st.wait()
                        st.mark(nc.vector.tensor_copy(carry[:], fill[s][:, K - 1, :]))
                        dve.wait_ge(c.gathered[s].sem, c.gathered[s].at(16 * K * i + 16 * K))
                        st.then(nc.vector.tensor_tensor(rows[s][:], rows[s][:], fill[s][:], ALU.add))
                        st.then(nc.vector.scalar_tensor_tensor(out=rows[s][:], in0=rows[s][:], scalar=0.0,
                                                               in1=spread(c.w2[l][:][:, None, :], [P, K, D]),
                                                               op0=ALU.max, op1=ALU.mult))
                        st.then(nc.vector.tensor_reduce(logit[:, bass.ds(2 * K * i + s * K, K)], rows[s][:], AX_X, ALU.add))
                        dve.sem_inc(c.computed[s].sem, 1)
                st.close(EIT)
        for s in range(2):
            c.gathered[s].counted(16 * K * EIT)
            c.computed[s].counted(EIT)
            c.staged[s].counted(2 * EIT)
            c.loaded[s].counted(16 * EIT)
        c.end_phase()


def diffusion_layer(c, order):
    with ExitStack() as ctx:
        y = c.sb("y", [P, NC, D], ctx=ctx)
        mask = c.sb("mask", [P, EC], ctx=ctx)
        norm = c.sb("norm", [P, NC, 1], ctx=ctx)
        mask_carry = c.sb("mask_carry", [P, 1], ctx=ctx)
        bn = [P, NC, D]
        vector_phase(c, lambda nc, st, by_act: st.then(nc.vector.tensor_copy(whole(y), whole(c.x))))
        for l in range(N_LAYERS):
            with ExitStack() as ctx2:
                u = c.sb("u", [P, NC, D], ctx=ctx2)
                v = c.sb("v", [P, NC, D], ctx=ctx2)
                edge_halves(c, l, y, u, v)
                vector_phase(c, lambda nc, st, by_act: None,
                             [(node_rows(c.table), v[:]), (node_rows(c.table_u), u[:])])
                node_scatter(c, order, u, c.table_u, c.fill)
            edge_logits(c, l, order, mask)
            with ExitStack() as ctx2:
                scan = c.sb("scan", [P, EC], ctx=ctx2)

                def masks(nc, st, by_act):
                    by_act(ACT.Sigmoid, mask[:], mask[:], c.b2[l][:])
                    st.then(nc.vector.tensor_scalar(mask[:], mask[:], ZETA - GAMMA, GAMMA, ALU.mult, ALU.add))
                    st.then(nc.vector.tensor_scalar(mask[:], mask[:], 0.0, 1.0, ALU.max, ALU.min))
                    st.then(nc.vector.tensor_tensor_scan(scan[:], order.keep[:], mask[:], 0.0, ALU.mult, ALU.add))
                    st.then(nc.vector.tensor_copy(mask_carry[:], scan[:, EC - 1:EC]))

                vector_phase(c, masks, [(c.mask_d[0:EP, :].rearrange("(p j) a -> p (j a)", j=EC), scan[:])])
            node_sums(c, order, c.mask_d, mask_carry, norm)
            with ExitStack() as ctx2:
                agg = c.sb("agg", [P, NC, D], ctx=ctx2)

                def second_table(nc, st, by_act):
                    flat = norm[:].rearrange("p c a -> p (c a)")
                    st.then(nc.vector.tensor_scalar(flat, flat, 1e-6, None, ALU.add))
                    by_act(ACT.Sqrt, flat, flat)
                    st.then(nc.vector.reciprocal(flat, flat))
                    st.then(nc.vector.tensor_scalar(flat, flat, 0.0, 10.0, ALU.max, ALU.min))
                    st.then(nc.vector.tensor_tensor(agg[:], y[:], spread(norm[:], bn), ALU.mult))

                vector_phase(c, second_table, [(node_rows(c.table), agg[:])])
                edge_sum(c, order, c.from_dst, c.table, c.scanned, c.carry, mask)
                node_sums(c, order, c.scanned, c.carry, agg)

                def add_up(nc, st, by_act):
                    st.then(nc.vector.tensor_tensor(y[:], agg[:], spread(norm[:], bn), ALU.mult))
                    if l == 0:
                        st.then(nc.vector.tensor_tensor(whole(c.x), whole(c.x), whole(c.x), ALU.add))
                    st.then(nc.vector.tensor_tensor(whole(c.x), whole(c.x), whole(y), ALU.add))

                vector_phase(c, add_up)
        small = c.sb("small", [P, NC], ctx=ctx)
        vector_phase(c, lambda nc, st, by_act: layer_norm(c, nc, st, by_act, c.x, y, small))



def relation_table(c, a):
    nc = c.nc
    HALF = N_RELS * D // 2
    T = 2 * NIT
    with ExitStack() as ctx:
        w = c.sb("w3", [D, N_RELS, D], ctx=ctx)
        side = c.sb("side", [P, NK, D], ctx=ctx)
        turned = c.sb("turned", [D, NK, P], ctx=ctx)
        ready = [c.sb(f"ready{s}", [P, NK, N_RELS * D], ctx=ctx) for s in range(2)]
        turn = c.ps("turn", [D, NK + 1, P], ctx=ctx)
        half = [[c.ps(f"half{g}_{b}", [P, HALF], ctx=ctx) for b in range(3)] for g in range(2)]
        table = c.table3.rearrange("(p c r) o -> p c (r o)", c=NC, r=N_RELS)
        flat = w[:].rearrange("i r o -> i (r o)")
        with nc.Block() as block:
            @block.scalar
            def _(act):
                with act.Fori(0, NIT) as i2:
                    for s in range(2):
                        i = 2 * i2 + s
                        act.wait_ge(c.pe_gave.sem, c.pe_gave.at(i))
                        nc.scalar.activation(side[:], c.x[:, bass.ds(NK * i, NK), :], ACT.Copy).then_inc(c.act_gave.sem, 1)
                        act.wait_ge(c.pe_gave2.sem, c.pe_gave2.at(2 * NK * i))
                        act.wait_ge(c.pe_gave.sem, c.pe_gave.at(i + 1))
                        nc.scalar.activation(turned[:], turn[:, 0:NK, :], ACT.Copy).then_inc(c.act_gave.sem, 1)
                        act.wait_ge(c.stored[s].sem, c.stored[s].at(16 * i2))
                        for k in range(NK):
                            act.wait_ge(c.pe_gave2.sem, c.pe_gave2.at(2 * NK * i + 2 * k + 1))
                            nc.scalar.activation(ready[s][:, k, 0:HALF], half[0][k % 3][:], ACT.Copy)\
                                .then_inc(c.act_gave2.sem, 1)

            @block.vector
            def _(dve):
                with dve.Fori(0, NIT) as i2:
                    for s in range(2):
                        i = 2 * i2 + s
                        dve.wait_ge(c.stored[s].sem, c.stored[s].at(16 * i2))
                        for k in range(NK):
                            dve.wait_ge(c.pe_gave2.sem, c.pe_gave2.at(2 * NK * i + 2 * k + 2))
                            nc.vector.tensor_copy(ready[s][:, k, HALF:2 * HALF], half[1][k % 3][:])\
                                .then_inc(c.dve_gave.sem, 1)

            @block.tensor
            def _(pe):
                pe.wait_ge(c.moved.sem, c.moved.at(16))
                with pe.Fori(0, T) as i:
                    pe.wait_ge(c.act_gave.sem, c.act_gave.at(2 * i + 1))
                    pe.sem_inc(c.pe_turn.sem, 1)
                    for k in range(NK):
                        last = nc.tensor.transpose(turn[:, k, :], side[:, k, :], c.ident[:])
                    last.then_inc(c.pe_gave.sem, 1)
                    pe.wait_ge(c.act_gave.sem, c.act_gave.at(2 * i + 2))
                    pe.wait_ge(c.act_gave2.sem, c.act_gave2.at(NK * i))
                    pe.wait_ge(c.dve_gave.sem, c.dve_gave.at(NK * i))
                    pe.sem_inc(c.pe_turn.sem, 1)
                    for k in range(NK):
                        if k >= 3:
                            pe.wait_ge(c.act_gave2.sem, c.act_gave2.at(NK * i + k - 2))
                            pe.wait_ge(c.dve_gave.sem, c.dve_gave.at(NK * i + k - 2))
                            pe.sem_inc(c.pe_turn.sem, 1)
                        for g in range(2):
                            nc.tensor.matmul(half[g][k % 3][:], turned[:, k, :], flat[:, HALF * g:HALF * g + HALF],
                                             start=True, stop=True).then_inc(c.pe_gave2.sem, 1)

            @block.sync
            def _(sp):
                sp.dma_start(w[:], a["L3_gnn_weight"].rearrange("r i o -> i r o")).then_inc(c.moved.sem, 16)
                with sp.Fori(0, NIT) as i2:
                    for s in range(2):
                        i = 2 * i2 + s
                        sp.wait_ge(c.act_gave2.sem, c.act_gave2.at(NK * i + NK))
                        sp.sem_inc(c.sp_turn.sem, 1)
                        sp.wait_ge(c.dve_gave.sem, c.dve_gave.at(NK * i + NK))
                        sp.sem_inc(c.sp_turn.sem, 1)
                        sp.dma_start(table[:, bass.ds(NK * i, NK), :], ready[s][:]).then_inc(c.stored[s].sem, 16)
                for s in range(2):
                    c.stored[s].counted(16 * NIT)
                    sp.wait_ge(c.stored[s].sem, c.stored[s].at(16 * NIT))
        c.moved.counted(16)
        c.act_gave.counted(2 * T)
        c.act_gave2.counted(NK * T)
        c.dve_gave.counted(NK * T)
        c.pe_gave.counted(T)
        c.pe_gave2.counted(2 * NK * T)
        c.end_phase()


def relation_layer(c, a, order, out):
    relation_table(c, a)
    edge_sum(c, order, c.from_rel, c.table3, c.scanned, c.carry)
    with ExitStack() as ctx:
        agg = c.sb("agg", [P, NC, D], ctx=ctx)
        small = c.sb("small", [P, NC], ctx=ctx)
        node_sums(c, order, c.scanned, c.carry, agg)

        def finish(nc, st, here, product):
            st.mark(nc.vector.tensor_tensor(agg[:, here, :], agg[:, here, :], product[:], ALU.add))

        project(c, [c.x], [c.w3loop[:]], finish, 1)

        def work(nc, st, by_act):
            st.then(nc.vector.tensor_tensor(agg[:], agg[:], spread(c.bias3[:][:, None, :], [P, NC, D]), ALU.add))
            st.then(nc.vector.tensor_tensor(whole(c.x), whole(c.x), whole(agg), ALU.add))
            layer_norm(c, nc, st, by_act, c.x, agg, small)

        full = N_NODES // NC
        rest = N_NODES - full * NC
        vector_phase(c, work, [
            (out[0:96 * NC, :].rearrange("(p c) f -> p c f", c=NC), c.x[0:96, :, :]),
            (out[96 * NC:full * NC, :].rearrange("(p c) f -> p c f", c=NC), c.x[96:full, :, :]),
            (out[full * NC:N_NODES, :].rearrange("(p c) f -> p c f", p=1), c.x[full:full + 1, 0:rest, :])])


def clear_tables(c):
    nc = c.nc
    cols = 98
    with ExitStack() as ctx:
        zero = c.sb("zero", [P, cols, D], ctx=ctx)
        none1 = c.sb("none1", [P, HEADS, HW_], ctx=ctx)
        jobs = [(c.scanned[NO_EDGE_ROW:NO_EDGE_ROW + 1, :], zero[0:1, 0, :]),
                (c.mask_d[NO_EDGE_ROW:NO_EDGE_ROW + 1, :], zero[0:1, 0, 0:1]),
                (c.scanned1[NO_EDGE_ROW:NO_EDGE_ROW + 1, :], none1[0:1, :, :].rearrange("p h f -> p (h f)"))]
        fill = c.fill[0:EP, :].rearrange("(p j) f -> p j f", j=EC)
        for j in range(0, EC, cols):
            jobs.append((fill[:, j:j + cols, :], zero[:]))
        wide = cols * D // HEADS
        fill1 = c.fill1[0:EP, :].rearrange("(p j) f -> p (j f)", j=EC)
        flat = zero[:].rearrange("p c f -> p (c f)")
        for j in range(0, EC * HEADS, cols * D):
            n = min(cols * D, EC * HEADS - j)
            jobs.append((fill1[:, j:j + n], flat[:, 0:n]))
        with nc.Block() as block:
            @block.vector
            def _(dve):
                st = Steps(dve, c.dve_step)
                st.mark(nc.vector.memset(zero[:], 0.0))
                st.then(nc.vector.memset(none1[:], 0.0))
                st.mark(nc.vector.memset(none1[:, :, D + 1], -BIG))
                st.close()

            @block.sync
            def _(sp):
                sp.wait_ge(c.dve_step.sem, c.dve_step.at(3))
                for dst, src in jobs:
                    sp.dma_start(dst, src).then_inc(c.moved.sem, 16)
                c.moved.counted(16 * len(jobs))
                sp.wait_ge(c.moved.sem, c.moved.at(16 * len(jobs)))
        c.end_phase()



def graph_layers(nc, a, out):
    with ExitStack() as ctx:
        c = Core(nc, ctx)
        only_unsorted = Core(nc, ctx, "only_unsorted_", 1)
        start(c, only_unsorted, a)
        unsorted = c.sb("unsorted", [P, 1], I32)
        by_dst = Order(c, "dst", 3)
        by_src = Order(c, "src", 2)
        c.from_src = c.sb("from_src", [P, EC], I32)
        c.from_rel = c.sb("from_rel", [P, EC], I32)
        c.from_dst = c.sb("from_dst", [P, EC], I32)
        c.carry = c.sb("carry", [P, D])
        c.table = c.dram("table", [NP, D])
        c.table_u = c.dram("table_u", [NP, D])
        c.scanned = c.dram("scanned", [EP + 1, D])
        c.fill = c.dram("fill", [EP + 1 + NP, D])
        c.table1 = c.dram("table1", [NP, TAB1])
        c.a_dst_d = c.dram("a_dst_d", [NP, HEADS])
        c.fill1 = c.dram("fill1", [EP + 1 + NP, HEADS])
        c.scanned1 = c.dram("scanned1", [EP + 1, ROW1])
        c.tops_d = c.dram("tops_d", [P, HEADS])
        c.nodes_d = c.dram("nodes_d", [P + 1, 1])
        c.mask_d = c.dram("mask_d", [EP + 1, 1])
        c.table3 = c.dram("table3", [NP * N_RELS, D])

        write_list(c, by_dst, [a["dst"], a["src"], a["edge_type_16"]])
        write_list(c, by_src, [a["src"], a["dst"]])
        find_disorder(c, by_dst, unsorted)
        radix_sort(c, by_dst, only_unsorted, unsorted)
        radix_sort(c, by_src, c)

        def dst_side(nc, st, recs):
            st.mark(nc.vector.tensor_copy(c.from_src[:], recs[:, :, 1]))
            st.then(nc.vector.tensor_scalar(c.from_rel[:], recs[:, :, 1], float(N_RELS), None, ALU.mult))
            st.then(nc.vector.tensor_tensor(c.from_rel[:], c.from_rel[:], recs[:, :, 2], ALU.add))

        def src_side(nc, st, recs):
            st.mark(nc.vector.tensor_copy(c.from_dst[:], recs[:, :, 1]))

        read_order(c, by_dst, dst_side)
        read_order(c, by_src, src_side)
        clear_tables(c)
        chebyshev_layer(c, by_dst)
        attention_layer(c, by_dst)
        diffusion_layer(c, by_src)
        relation_layer(c, a, by_dst, out)


_INS = ["x", "src", "dst", "edge_type_16", "L0_gnn_W", "L0_gnn_b", "L1_gnn_W", "L1_gnn_att_src", "L1_gnn_att_dst",
        "L1_gnn_bias", "L2_gnn_nb_W", "L2_gnn_nb_b", "L2_gnn_self_W", "L2_gnn_self_b", "L2_gnn_att1_W",
        "L2_gnn_att1_b", "L2_gnn_att2_W", "L2_gnn_att2_b", "L3_gnn_weight", "L3_gnn_h_bias", "L3_gnn_loop_weight"]
_OUTS = [((N_NODES, D), "float32")]


def kernel(**inputs):
    import numpy as _np
    import concourse.bacc as _bacc
    from concourse import mybir as _mybir
    from concourse.bass_utils import run_bass_kernel_spmd as _run

    nc = _bacc.Bacc("TRN2", target_bir_lowering=False, num_devices=1)
    arrays, by_name = {}, {}
    for name in _INS:
        array = _np.ascontiguousarray(inputs[name])
        arrays[f"in_{name}_dram"] = array
        by_name[name] = nc.dram_tensor(f"in_{name}_dram", array.shape, _mybir.dt.from_np(array.dtype),
                                       kind="ExternalInput").ap()
    shape, dtype = _OUTS[0]
    out = nc.dram_tensor("out_0_dram", shape, _mybir.dt.from_np(_np.dtype(dtype)), kind="ExternalOutput").ap()
    graph_layers(nc, by_name, out)
    r = _run(nc, [arrays], core_ids=[0])
    return _np.asarray(r.results[0]["out_0_dram"])
```

```python
from contextlib import ExitStack

import numpy as np

import concourse.bass as bass
from concourse import mybir
from concourse.alu_op_type import AluOpType as ALU

ACT = mybir.ActivationFunctionType
F32 = mybir.dt.float32
BF16 = mybir.dt.bfloat16
I32 = mybir.dt.int32
AX_X = mybir.AxisListType.X

P = 128
N_NODES, N_EDGES, D = 12500, 200000, 64
HEADS, N_LAYERS, N_RELS = 5, 3, 16
NC = -(-N_NODES // P)
NP = NC * P
K = 28
EC = -(-N_EDGES // (P * 2 * K)) * 2 * K
EP = EC * P
EIT = EC // (2 * K)
NK = 7
NIT = NC // (2 * NK)
PAD_NODE = NP - 1
NO_EDGE_ROW = EP
BIG = 1.0e30
HW_ = D + 2
ROW1 = HEADS * HW_
TAB1 = 72
GAMMA, ZETA = -0.45, 1.05
LOGB = 7


class Signal:

    def __init__(self, ctx, nc, name, dma):
        self.sem = ctx.enter_context(nc.semaphore(name))
        self.dma = dma
        self.total = 0
        self.pending = 0

    def at(self, n):
        return n + self.total

    def counted(self, n):
        self.pending += n


class Steps:

    def __init__(self, eng, signal, i=None, per=0):
        self.eng, self.counter, self.i, self.per, self.k = eng, signal, i, per, 0
        self.base = signal.total + signal.pending

    def mark(self, ins):
        self.k += 1
        ins.then_inc(self.counter.sem, 1)

    def wait(self):
        if self.i is None:
            self.eng.wait_ge(self.counter.sem, self.base + self.k)
        else:
            self.eng.wait_ge(self.counter.sem, self.i * self.per + (self.base + self.k))

    def then(self, ins):
        self.mark(ins)
        self.wait()

    def close(self, iterations=1):
        assert self.i is None or self.per == self.k, (self.per, self.k)
        self.counter.counted(iterations * self.k)


class Core:

    def __init__(self, nc, ctx, prefix="", turns=4):
        self.nc, self.ctx = nc, ctx
        self.phase = 0
        self.all_signals = []

        def signal(name, dma=False):
            self.all_signals.append(Signal(ctx, nc, prefix + name, dma))
            return self.all_signals[-1]

        self.moved = signal("moved", True)
        self.gathered_by_turn = [[signal(f"gathered{n}_{s}", True) for s in range(2)] for n in range(turns)]
        self.gathered = self.gathered_by_turn[0]
        self.moved_by_pool = signal("moved_by_pool", True)
        self.stored = [signal(f"stored{s}", True) for s in range(2)]
        self.loaded = [signal(f"loaded{s}", True) for s in range(2)]
        self.staged = [signal(f"staged{s}") for s in range(2)]
        self.computed = [signal(f"computed{s}") for s in range(2)]
        self.mapped = [signal(f"mapped{s}") for s in range(2)]
        self.taken = [signal(f"taken{s}") for s in range(2)]
        self.copied = [signal(f"copied{s}") for s in range(2)]
        self.dve_step = signal("dve_step")
        self.act_step = signal("act_step")
        self.pool_step = signal("pool_step")
        self.sp_turn = signal("sp_turn")
        self.pool_turn = signal("pool_turn")
        self.pe_turn = signal("pe_turn")
        self.dve_gave = signal("dve_gave")
        self.act_gave = signal("act_gave")
        self.pe_gave = signal("pe_gave")
        self.act_gave2 = signal("act_gave2")
        self.pe_gave2 = signal("pe_gave2")
        self.dve_gave2 = signal("dve_gave2")
        self.loaded_by_dve = signal("loaded_by_dve")

    def signals(self):
        return self.all_signals

    def end_phase(self):
        self.phase += 1
        for s in self.signals():
            s.total += s.pending
            s.pending = 0
        if len(self.gathered_by_turn) > 1 and self.gathered[0].total + 16 * (K * EIT + 1) > 65535:
            self.gathered = self.gathered_by_turn[self.gathered_by_turn.index(self.gathered) + 1]

    def place(self, name, ctx):
        return f"{name}_{self.phase}" if ctx else name

    def sb(self, name, shape, dt=F32, ctx=None):
        return (ctx or self.ctx).enter_context(self.nc.sbuf_tensor(self.place(name, ctx), shape, dt))

    def ps(self, name, shape, dt=F32, ctx=None):
        return (ctx or self.ctx).enter_context(self.nc.psum_tensor(self.place(name, ctx), shape, dt))

    def dram(self, name, shape, dt=F32):
        return self.nc.dram_tensor(name, shape, dt, kind="Internal").ap()


def spread(ap, shape):
    return ap.to_broadcast(list(shape))


def at_rows(ap):
    return bass.IndirectOffsetOnAxis(ap=ap, axis=0)



def start(c, g, a):
    nc = c.nc
    c.x = c.sb("x_now", [P, NC, D])
    c.ident = c.sb("ident", [P, P])
    c.iota_f = c.sb("iota_f", [P, P])
    c.iota_row = c.sb("iota_row", [P, P], BF16)
    c.before = c.sb("before", [P, P], BF16)
    c.ones = c.sb("ones", [P, P], BF16)
    c.node_of = c.sb("node_of", [P, NK, P])
    c.w0a = c.sb("w0a", [P, D])
    c.w0b = c.sb("w0b", [D, D])
    c.bias0 = c.sb("bias0", [P, D])
    c.w1h = [c.sb(f"w1h{i}", [min(P, HEADS * D - P * i), D]) for i in range(3)]
    c.wa = c.sb("wa", [D, 2 * HEADS])
    c.bias1 = c.sb("bias1", [P, D])
    c.wf = [c.sb(f"wf{l}", [D, P]) for l in range(N_LAYERS)]
    c.bf = [c.sb(f"bf{l}", [P, 1]) for l in range(N_LAYERS)]
    c.wuv = [c.sb(f"wuv{l}", [P, P]) for l in range(N_LAYERS)]
    c.buv = [c.sb(f"buv{l}", [P, D]) for l in range(N_LAYERS)]
    c.w2 = [c.sb(f"w2{l}", [P, D]) for l in range(N_LAYERS)]
    c.b2 = [c.sb(f"b2{l}", [P, 1]) for l in range(N_LAYERS)]
    c.w3loop = c.sb("w3loop", [D, D])
    c.bias3 = c.sb("bias3", [P, D])
    c.eps = c.sb("eps", [P, 1])

    full = N_NODES // NC
    rest = N_NODES - full * NC
    with ExitStack() as ctx:
        w1 = c.sb("w1", [D, HEADS * D], ctx=ctx)
        att = c.sb("att", [D, 2, HEADS * D], ctx=ctx)
        seed = c.sb("seed", [P, 2 * len(c.gathered_by_turn + g.gathered_by_turn) + 2], ctx=ctx)

        def row(v):
            return spread(v.rearrange("(a n) -> a n", a=1), [P, v.shape[0]])

        loads = [
            (c.x[0:96, :, :], a["x"][0:96 * NC, :].rearrange("(p c) f -> p c f", c=NC)),
            (c.x[96:full, :, :], a["x"][96 * NC:full * NC, :].rearrange("(p c) f -> p c f", c=NC)),
            (c.x[full:full + 1, 0:rest, :], a["x"][full * NC:N_NODES, :].rearrange("(p c) f -> p c f", p=1)),
            (c.w0a[:], a["L0_gnn_W"][0:P, :]),
            (c.w0b[:], a["L0_gnn_W"][P:3 * D, :]),
            (c.bias0[:], row(a["L0_gnn_b"])),
            (w1[:], a["L1_gnn_W"]),
            (c.bias1[:], row(a["L1_gnn_bias"])),
            (c.w3loop[:], a["L3_gnn_loop_weight"]),
            (c.bias3[:], row(a["L3_gnn_h_bias"])),
        ]
        for h in range(HEADS):
            loads.append((c.w1h[h // 2][D * (h % 2):D * (h % 2) + D, :], a["L1_gnn_W"][:, h * D:(h + 1) * D]))
        for k, name in enumerate(("L1_gnn_att_src", "L1_gnn_att_dst")):
            flat = a[name].rearrange("(a h) d -> a (h d)", a=1)
            loads.append((att[:, k, :], spread(flat, [D, HEADS * D])))
        for l in range(N_LAYERS):
            loads += [
                (c.wf[l][:, 0:D], a["L2_gnn_nb_W"][l]),
                (c.wf[l][:, D:P], a["L2_gnn_self_W"][l]),
                (c.bf[l][0:D, :], a["L2_gnn_nb_b"][l].rearrange("(n a) -> n a", a=1)),
                (c.bf[l][D:P, :], a["L2_gnn_self_b"][l].rearrange("(n a) -> n a", a=1)),
                (c.wuv[l][0:D, 0:D], a["L2_gnn_att1_W"][l, 0:D, :]),
                (c.wuv[l][D:P, D:P], a["L2_gnn_att1_W"][l, D:P, :]),
                (c.buv[l][:], row(a["L2_gnn_att1_b"][l])),
                (c.w2[l][:], row(a["L2_gnn_att2_W"][l].rearrange("n a -> (n a)"))),
                (c.b2[l][:], row(a["L2_gnn_att2_b"][l])),
            ]
        by_pool = [s for pair in c.gathered_by_turn + g.gathered_by_turn for s in pair] + [c.moved_by_pool, g.moved_by_pool]
        signals = c.signals() + g.signals()
        by_sp = [s for s in signals if s.dma and s not in by_pool]

        with nc.Block() as block:
            @block.gpsimd
            def _(pool):
                st = Steps(pool, c.pool_step)
                st.mark(nc.gpsimd.memset(c.ident[:], 0.0))
                st.mark(nc.gpsimd.memset(c.before[:], 0.0))
                st.mark(nc.gpsimd.iota(c.iota_f[:], [[1, P]], base=0, channel_multiplier=0,
                                       allow_small_or_imprecise_dtypes=True))
                st.mark(nc.gpsimd.iota(c.node_of[:], [[1, NK], [NC, P]], base=0, channel_multiplier=0,
                                       allow_small_or_imprecise_dtypes=True))
                st.wait()
                st.mark(nc.gpsimd.affine_select(out=c.ident[:], in_=c.ident[:], compare_op=ALU.not_equal, fill=1.0,
                                                base=0, pattern=[[-1, P]], channel_multiplier=1))
                st.mark(nc.gpsimd.affine_select(out=c.before[:], in_=c.before[:], compare_op=ALU.is_ge, fill=1.0,
                                                base=0, pattern=[[-1, P]], channel_multiplier=1))
                st.wait()
                st.close()
                for k, s in enumerate(by_pool):
                    pool.dma_start(seed[:, k:k + 1], spread(a["x"][0:1, 0:1], [P, 1])).then_inc(s.sem, 16)
                    s.counted(16)
                    pool.wait_ge(s.sem, 16)

            @block.vector
            def _(dve):
                st = Steps(dve, c.dve_step)
                st.mark(nc.vector.memset(c.x[:], 0.0))
                for l in range(N_LAYERS):
                    st.mark(nc.vector.memset(c.wuv[l][:], 0.0))
                st.mark(nc.vector.memset(c.ones[:], 1.0))
                st.mark(nc.vector.memset(c.eps[:], 1e-5))
                for s in signals:
                    if not s.dma and s not in (c.dve_step, c.pool_step):
                        dve.sem_inc(s.sem, 1)
                        s.counted(1)
                dve.wait_ge(c.pool_step.sem, 4)
                st.mark(nc.vector.tensor_copy(c.iota_row[:], c.iota_f[:]))
                for k, s in enumerate(by_sp):
                    dve.wait_ge(s.sem, 16 * len(loads[k::len(by_sp)]))
                st.then(nc.vector.tensor_tensor(att[:], att[:], spread(w1[:][:, None, :], [D, 2, HEADS * D]), ALU.mult))
                st.then(nc.vector.tensor_reduce(c.wa[:], att[:].rearrange("p a (h d) -> p (a h) d", h=HEADS),
                                                AX_X, ALU.add))
                st.close()

            @block.sync
            def _(sp):
                sp.wait_ge(c.dve_step.sem, 1 + N_LAYERS)
                for k, (dst, src) in enumerate(loads):
                    s = by_sp[k % len(by_sp)]
                    sp.dma_start(dst, src).then_inc(s.sem, 16)
                    s.counted(16)
        c.end_phase()
        g.end_phase()



class Order:

    def __init__(self, c, name, fields):
        self.name, self.fields = name, fields
        self.list = c.dram(f"{name}_list", [EP + 2, fields], I32)
        self.spare = c.dram(f"{name}_spare", [EP + 2, fields], I32)
        self.rows_d = c.dram(f"{name}_rows", [3, NP])
        self.keep = c.sb(f"{name}_keep", [P, EC])
        self.spill = c.sb(f"{name}_spill", [P, 1])
        self.spill_at = c.sb(f"{name}_spill_at", [P, 2 * NIT])
        self.first_key = c.sb(f"{name}_first_key", [P, 1], I32)
        self.last_row = c.sb(f"{name}_last_row", [P, NC], I32)
        self.first_row = c.sb(f"{name}_first_row", [P, NC], I32)
        self.degree = c.sb(f"{name}_degree", [P, NC])
        self.counts = c.sb(f"{name}_counts", [P, P])


def records(edge_list):
    return edge_list[1:EP + 1, :].rearrange("(p j) r -> p j r", j=EC)


def write_list(c, order, columns):
    nc = c.nc
    full = N_EDGES // EC
    rest = N_EDGES - full * EC
    cuts = [0, 112, full - 1, full]
    with ExitStack() as ctx:
        cols = c.sb("list_cols", [P, len(columns), EC], I32, ctx)
        recs = c.sb("list_recs", [P, EC, order.fields], I32, ctx)
        ends = c.sb("list_ends", [2, order.fields], I32, ctx)
        with nc.Block() as block:
            @block.vector
            def _(dve):
                st = Steps(dve, c.dve_step)
                for f in range(len(columns)):
                    st.mark(nc.vector.memset(cols[:, f, :], PAD_NODE if f < 2 else 0))
                st.mark(nc.vector.memset(ends[:], -1))
                dve.wait_ge(c.moved.sem, c.moved.at(16 * 4 * len(columns)))
                for f in range(len(columns)):
                    st.mark(nc.vector.tensor_copy(recs[:, :, f], cols[:, f, :]))
                st.close()

            @block.sync
            def _(sp):
                sp.wait_ge(c.dve_step.sem, c.dve_step.at(len(columns) + 1))
                for f, e in enumerate(columns):
                    for lo, hi in zip(cuts, cuts[1:]):
                        sp.dma_start(cols[lo:hi, f, :],
                                     e[lo * EC:hi * EC].rearrange("(p j) -> p j", j=EC)).then_inc(c.moved.sem, 16)
                    sp.dma_start(cols[full:full + 1, f, 0:rest],
                                 e[full * EC:N_EDGES].rearrange("(p j) -> p j", p=1)).then_inc(c.moved.sem, 16)
                sp.wait_ge(c.dve_step.sem, c.dve_step.at(2 * len(columns) + 1))
                sp.dma_start(records(order.list), recs[:]).then_inc(c.moved.sem, 16)
                for edge_list in (order.list, order.spare):
                    sp.dma_start(edge_list[0:1, :], ends[0:1, :]).then_inc(c.moved.sem, 16)
                    sp.dma_start(edge_list[EP + 1:EP + 2, :], ends[1:2, :]).then_inc(c.moved.sem, 16)
                c.moved.counted(16 * (4 * len(columns) + 5))
                sp.wait_ge(c.moved.sem, c.moved.at(16 * (4 * len(columns) + 5)))
        c.end_phase()


def split_bytes(nc, st, parts, whole_i, tmp_i, n):
    for k in range(n):
        st.then(nc.vector.tensor_scalar(tmp_i, whole_i, 0xFF << (8 * k), None, ALU.bitwise_and))
        st.then(nc.vector.tensor_copy(parts[k], tmp_i))


def find_disorder(c, order, flag):
    nc = c.nc
    with ExitStack() as ctx:
        recs = c.sb("recs", [P, EC, order.fields], I32, ctx)
        next_key = c.sb("next_key", [P, 1], I32, ctx)
        falls = c.sb("falls", [P, EC], ctx=ctx)
        any_fall = c.sb("any_fall", [P, 1], ctx=ctx)
        any_bf = c.sb("any_bf", [P, 1], BF16, ctx)
        where = c.ps("where", [P, 1], ctx=ctx)
        with nc.Block() as block:
            @block.sync
            def _(sp):
                sp.dma_start(recs[:], records(order.list)).then_inc(c.moved.sem, 16)
                beyond = order.list[2:EP + 2, :].rearrange("(p j) r -> p j r", j=EC)
                sp.dma_start(next_key[:], beyond[:, EC - 1, 0:1], allow_slow_non_contiguous=True).then_inc(c.moved.sem, 16)
                c.moved.counted(32)

            @block.vector
            def _(dve):
                st = Steps(dve, c.dve_step)
                st.then(nc.vector.memset(falls[:], 0.0))
                dve.wait_ge(c.moved.sem, c.moved.at(32))
                st.mark(nc.vector.tensor_tensor(falls[:, 0:EC - 1], recs[:, 0:EC - 1, 0], recs[:, 1:EC, 0], ALU.is_gt))
                st.then(nc.vector.tensor_tensor(falls[0:P - 1, EC - 1:EC], recs[0:P - 1, EC - 1, 0:1],
                                                next_key[0:P - 1, :], ALU.is_gt))
                st.then(nc.vector.tensor_reduce(any_fall[:], falls[:], AX_X, ALU.max))
                st.then(nc.vector.tensor_copy(any_bf[:], any_fall[:]))
                dve.sem_inc(c.dve_gave.sem, 1)
                dve.wait_ge(c.pe_gave.sem, c.pe_gave.at(1))
                st.mark(nc.vector.tensor_scalar(flag[:], where[:], 1.0, None, ALU.min))
                st.close()

            @block.tensor
            def _(pe):
                pe.wait_ge(c.dve_gave.sem, c.dve_gave.at(1))
                nc.tensor.matmul(where[:], c.ones[:], any_bf[:], start=True, stop=True).then_inc(c.pe_gave.sem, 1)
        c.dve_gave.counted(1)
        c.pe_gave.counted(1)
        c.end_phase()


def radix_sort(c, order, g, flag=None, counted=(), clears=()):
    nc = c.nc
    R = order.fields
    passes = [(order.list, order.spare, 0), (order.spare, order.list, LOGB)]
    with ExitStack() as ctx:
        recs = c.sb("recs", [P, EC, R], I32, ctx)
        digit_i = c.sb("digit_i", [P, EC], I32, ctx)
        digit = c.sb("digit", [P, EC], BF16, ctx)
        match = c.sb("match", [P, EC], BF16, ctx)
        count = c.sb("count", [P, P], ctx=ctx)
        count_i = c.sb("count_i", [P, P], I32, ctx)
        part_i = c.sb("part_i", [P, P], I32, ctx)
        part = [c.sb(f"part{k}", [P, P], BF16, ctx) for k in range(2)]
        total = c.sb("total", [P, P], ctx=ctx)
        upto = c.sb("upto", [P, P], ctx=ctx)
        unit = c.sb("unit", [P, P], ctx=ctx)
        next_row = [c.sb(f"next_row{k}", [P, P], ctx=ctx) for k in range(2)]
        hot = [c.sb(f"hot{k}", [P, P], BF16, ctx) for k in range(2)]
        spent = c.sb("spent", [P, P], ctx=ctx)
        rank = [c.sb(f"rank{s}", [P, K], ctx=ctx) for s in range(2)]
        rank_i = [c.sb(f"rank_i{s}", [P, K], I32, ctx) for s in range(2)]
        digit_s = [c.sb(f"digit_s{s}", [P, K], ctx=ctx) for s in range(2)]
        send = [c.sb(f"send{s}", [P, K, R], I32, ctx) for s in range(2)]
        earlier = c.ps("earlier", [P, P], ctx=ctx)
        totals = c.ps("totals", [P, P], ctx=ctx)
        if counted:
            both = c.sb("both", [P, 2, EC], BF16, ctx)
            maps = [c.sb(f"maps{s}", [P, 2, K, P], BF16, ctx) for s in range(2)]
            nothing = c.sb("nothing", [P, P], BF16, ctx)
            counts = [c.ps(f"counts{n}", [P, P], ctx=ctx) for n in range(2)]

        def if_wanted(eng, program):
            if flag is None:
                program()
            else:
                wanted = eng.value_load(flag[0:1, 0:1], min_val=0, max_val=1)
                with eng.If(wanted > 0):
                    program()

        def load(sp):
            for n, (source, _, _) in enumerate(passes):
                if n:
                    for s in range(2):
                        sp.wait_ge(g.gathered[s].sem, g.gathered[s].at(16 * K * EIT))
                sp.dma_start(recs[:], records(source)).then_inc(g.moved.sem, 16)
                if n == 0:
                    for dst, src in clears:
                        sp.dma_start(dst, src).then_inc(g.stored[0].sem, 16)
            if clears:
                g.stored[0].counted(16 * len(clears))
                sp.wait_ge(g.stored[0].sem, g.stored[0].at(16 * len(clears)))

        def rank_edges(dve):
            for n, (_, _, shift) in enumerate(passes):
                st = Steps(dve, g.dve_step)
                dve.wait_ge(g.moved.sem, g.moved.at(16 * n + 16))
                st.then(nc.vector.tensor_scalar(digit_i[:], recs[:, :, 0], shift, P - 1,
                                                ALU.arith_shift_right, ALU.bitwise_and))
                st.mark(nc.vector.memset(unit[:], 1.0))
                st.then(nc.vector.tensor_copy(digit[:], digit_i[:]))
                dve.sem_inc(g.dve_gave.sem, 1)
                st.close()
                if counted:
                    st = Steps(dve, g.dve_step)
                    nodes = recs[:, :, counted[n][0]]
                    st.then(nc.vector.tensor_scalar(digit_i[:], nodes, LOGB, None, ALU.arith_shift_right))
                    st.then(nc.vector.tensor_copy(both[:, 0, :], digit_i[:]))
                    st.then(nc.vector.tensor_scalar(digit_i[:], nodes, P - 1, None, ALU.bitwise_and))
                    st.then(nc.vector.tensor_copy(both[:, 1, :], digit_i[:]))
                    st.then(nc.vector.memset(nothing[:], 0.0))
                    dve.sem_inc(g.dve_gave2.sem, 1)
                    st.close()
                with dve.Fori(0, P) as d:
                    st = Steps(dve, g.dve_step, d, 1)
                    st.then(nc.vector.tensor_scalar(match[:], digit[:], c.iota_f[:, bass.ds(d, 1)], 0.0, ALU.is_equal,
                                                    ALU.add, accum_out=count[:, bass.ds(d, 1)]))
                st.close(P)
                st = Steps(dve, g.dve_step)
                st.then(nc.vector.tensor_copy(count_i[:], count[:]))
                split_bytes(nc, st, [t[:] for t in part], count_i[:], part_i[:], 2)
                dve.sem_inc(g.dve_gave.sem, 1)
                dve.wait_ge(g.pe_gave.sem, g.pe_gave.at(2 * n + 2))
                st.then(nc.vector.tensor_copy(total[:], totals[:]))
                st.then(nc.vector.tensor_tensor_scan(upto[:], unit[:], total[:], 1.0, ALU.mult, ALU.add))
                st.then(nc.vector.tensor_tensor(upto[:], upto[:], total[:], ALU.subtract))
                st.then(nc.vector.tensor_tensor(next_row[0][:], earlier[:], upto[:], ALU.add))
                st.close()
                with dve.Fori(0, EIT) as i:
                    st = Steps(dve, g.dve_step, i, 2 * (3 * K + 1))
                    for s in range(2):
                        dve.wait_ge(g.staged[s].sem, g.staged[s].at(2 * i + (2 * EIT * n + 2)))
                        for k in range(K):
                            st.mark(nc.vector.tensor_scalar(hot[k % 2][:], c.iota_row[:], digit_s[s][:, k:k + 1], None,
                                                            ALU.is_equal))
                            st.wait()
                            st.mark(nc.vector.tensor_tensor_reduce(spent[:], hot[k % 2][:], next_row[k % 2][:], 1.0, 0.0,
                                                                   ALU.mult, ALU.add, rank[s][:, k:k + 1]))
                            st.mark(nc.vector.tensor_tensor(next_row[1 - k % 2][:], next_row[k % 2][:], hot[k % 2][:],
                                                            ALU.add))
                        st.wait()
                        dve.wait_ge(g.gathered[s].sem, g.gathered[s].at(16 * K * i + 16 * K * EIT * n))
                        st.then(nc.vector.tensor_copy(rank_i[s][:], rank[s][:]))
                        dve.sem_inc(g.computed[s].sem, 1)
                        if counted:
                            dve.wait_ge(g.taken[s].sem, g.taken[s].at(i + EIT * n))
                            for half in range(2):
                                nc.vector.tensor_tensor(
                                    maps[s][:, half, :, :],
                                    spread(both[:, half, bass.ds(2 * K * i + s * K, K)][:, :, None], [P, K, P]),
                                    spread(c.iota_row[:][:, None, :], [P, K, P]), ALU.is_equal)\
                                    .then_inc(g.mapped[s].sem, 1)
                st.close(EIT)
                if counted:
                    st = Steps(dve, g.dve_step)
                    dve.wait_ge(g.pe_gave2.sem, g.pe_gave2.at(n + 1))
                    st.then(nc.vector.tensor_copy(counted[n][1].counts[:], counts[n][:]))
                    st.close()

        def count_before(pe):
            for n in range(2):
                pe.wait_ge(g.dve_gave.sem, g.dve_gave.at(2 * n + 2))
                for k in range(2):
                    last = nc.tensor.matmul(earlier[:], c.before[:], part[k][:], start=k == 0, stop=k == 1)
                last.then_inc(g.pe_gave.sem, 1)
                for k in range(2):
                    last = nc.tensor.matmul(totals[:], c.ones[:], part[k][:], start=k == 0, stop=k == 1)
                last.then_inc(g.pe_gave.sem, 1)
                if counted:
                    pe.wait_ge(g.dve_gave2.sem, g.dve_gave2.at(n + 1))
                    nc.tensor.matmul(counts[n][:], nothing[:], nothing[:], start=True, stop=False, skip_group_check=True)
                    with pe.Fori(0, EIT) as i:
                        for s in range(2):
                            pe.wait_ge(g.mapped[s].sem, g.mapped[s].at(2 * i + (2 * EIT * n + 2)))
                            pe.sem_inc(g.pe_turn.sem, 1)
                            for k in range(K):
                                last = nc.tensor.matmul(counts[n][:], maps[s][:, 0, k, :], maps[s][:, 1, k, :],
                                                        start=False, stop=False, skip_group_check=True)
                            last.then_inc(g.taken[s].sem, 1)
                    nc.tensor.matmul(counts[n][:], nothing[:], nothing[:], start=False, stop=True,
                                     skip_group_check=True).then_inc(g.pe_gave2.sem, 1)

        def stage(act):
            for n in range(2):
                act.wait_ge(g.dve_gave.sem, g.dve_gave.at(2 * n + 1))
                with act.Fori(0, EIT) as i:
                    for s in range(2):
                        here = bass.ds(2 * K * i + s * K, K)
                        act.wait_ge(g.computed[s].sem, g.computed[s].at(i + EIT * n))
                        act.wait_ge(g.gathered[s].sem, g.gathered[s].at(16 * K * i + 16 * K * EIT * n))
                        nc.scalar.activation(digit_s[s][:], digit[:, here], ACT.Copy).then_inc(g.staged[s].sem, 1)
                        nc.scalar.activation(send[s][:], recs[:, here, :], ACT.Copy).then_inc(g.staged[s].sem, 1)

        def send_records(pool):
            for n, (_, target, _) in enumerate(passes):
                with pool.Fori(0, EIT) as i:
                    for s in range(2):
                        pool.wait_ge(g.staged[s].sem, g.staged[s].at(2 * i + (2 * EIT * n + 2)))
                        pool.wait_ge(g.computed[s].sem, g.computed[s].at(i + (EIT * n + 1)))
                        pool.sem_inc(g.pool_turn.sem, 1)
                        for k in range(K):
                            pool.indirect_dma_start(out=target, out_offset=at_rows(rank_i[s][:, k:k + 1]),
                                                    in_=send[s][:, k, :], in_offset=None).then_inc(g.gathered[s].sem, 16)
            for s in range(2):
                pool.wait_ge(g.gathered[s].sem, g.gathered[s].at(2 * 16 * K * EIT))

        with nc.Block() as block:
            @block.sync
            def _(sp):
                if_wanted(sp, lambda: load(sp))

            @block.vector
            def _(dve):
                if_wanted(dve, lambda: rank_edges(dve))

            @block.tensor
            def _(pe):
                if_wanted(pe, lambda: count_before(pe))

            @block.scalar
            def _(act):
                if_wanted(act, lambda: stage(act))

            @block.gpsimd
            def _(pool):
                if_wanted(pool, lambda: send_records(pool))
        g.moved.counted(32)
        g.dve_gave.counted(4)
        g.pe_gave.counted(4)
        for s in range(2):
            g.gathered[s].counted(2 * 16 * K * EIT)
            g.computed[s].counted(2 * EIT)
            g.staged[s].counted(4 * EIT)
            if counted:
                g.mapped[s].counted(4 * EIT)
                g.taken[s].counted(2 * EIT)
        if counted:
            g.dve_gave2.counted(2)
            g.pe_gave2.counted(2)
        g.end_phase()
        if g is not c:
            c.end_phase()


def read_order(c, order, neighbours):
    nc = c.nc
    R = order.fields
    with ExitStack() as ctx:
        recs = c.sb("recs", [P, EC, R], I32, ctx)
        next_key = c.sb("next_key", [P, 1], I32, ctx)
        same = c.sb("same", [P, 1], ctx=ctx)
        unit = c.sb("unit", [P, P], ctx=ctx)
        cnt = order.counts
        upto = c.sb("upto", [P, P], ctx=ctx)
        tot_i = c.sb("tot_i", [P, 1], I32, ctx)
        byte_i = c.sb("byte_i", [P, 1], I32, ctx)
        byte = [c.sb(f"byte{k}", [P, 1], BF16, ctx) for k in range(3)]
        first = c.sb("first", [P, P], ctx=ctx)
        has = c.sb("has", [P, P], ctx=ctx)
        spare_row = c.sb("spare_row", [P, P], ctx=ctx)
        found = c.sb("found", [P, 3, P], ctx=ctx)
        back = c.sb("back", [P, 3, NC], ctx=ctx)
        before = c.ps("rows_before", [P, 1], ctx=ctx)
        hi_rows = NP // P

        with nc.Block() as block:
            @block.gpsimd
            def _(pool):
                st = Steps(pool, c.pool_step)
                st.mark(nc.gpsimd.iota(spare_row[:], [[1, P]], base=EP + 1, channel_multiplier=P,
                                       allow_small_or_imprecise_dtypes=True))
                st.close()

            @block.sync
            def _(sp):
                sp.dma_start(recs[:], records(order.list)).then_inc(c.loaded[0].sem, 16)
                beyond = order.list[2:EP + 2, :].rearrange("(p j) r -> p j r", j=EC)
                sp.dma_start(next_key[:], beyond[:, EC - 1, 0:1], allow_slow_non_contiguous=True).then_inc(c.loaded[0].sem, 16)
                sp.wait_ge(c.dve_gave.sem, c.dve_gave.at(1))
                for f in range(3):
                    sp.dma_start(order.rows_d[f].rearrange("(p n) -> p n", n=P), found[0:hi_rows, f, :]).then_inc(c.moved.sem, 16)
                sp.wait_ge(c.moved.sem, c.moved.at(16 * 3))
                for f in range(3):
                    sp.dma_start(back[:, f, :], order.rows_d[f].rearrange("(p n) -> p n", n=NC)).then_inc(c.moved.sem, 16)
                c.moved.counted(16 * 6)
                c.loaded[0].counted(32)

            @block.vector
            def _(dve):
                st = Steps(dve, c.dve_step)
                st.mark(nc.vector.memset(order.keep[:, 0:1], 0.0))
                st.then(nc.vector.memset(unit[:], 1.0))
                st.then(nc.vector.tensor_tensor_scan(upto[:], unit[:], cnt[:], 0.0, ALU.mult, ALU.add))
                st.then(nc.vector.tensor_copy(tot_i[:], upto[:, P - 1:P]))
                split_bytes(nc, st, [b[:] for b in byte], tot_i[:], byte_i[:], 3)
                dve.sem_inc(c.dve_gave2.sem, 1)
                c.dve_gave2.counted(1)
                st.then(nc.vector.tensor_tensor(first[:], upto[:], cnt[:], ALU.subtract))
                dve.wait_ge(c.pe_gave.sem, c.pe_gave.at(1))
                st.then(nc.vector.tensor_copy(same[:], before[:]))
                st.then(nc.vector.tensor_scalar(first[:], first[:], same[:], None, ALU.add))
                st.mark(nc.vector.tensor_scalar(has[:], cnt[:], 1.0, None, ALU.min))
                st.then(nc.vector.tensor_tensor(found[:, 0, :], first[:], cnt[:], ALU.add))
                st.then(nc.vector.tensor_scalar(found[:, 0, :], found[:, 0, :], -1.0 - NO_EDGE_ROW, None, ALU.add))
                st.then(nc.vector.tensor_tensor(found[:, 0, :], found[:, 0, :], has[:], ALU.mult))
                st.then(nc.vector.tensor_scalar(found[:, 0, :], found[:, 0, :], float(NO_EDGE_ROW), None, ALU.add))
                dve.wait_ge(c.pool_step.sem, c.pool_step.at(1))
                st.then(nc.vector.tensor_tensor(found[:, 1, :], first[:], spare_row[:], ALU.subtract))
                st.then(nc.vector.tensor_tensor(found[:, 1, :], found[:, 1, :], has[:], ALU.mult))
                st.then(nc.vector.tensor_tensor(found[:, 1, :], found[:, 1, :], spare_row[:], ALU.add))
                st.then(nc.vector.tensor_copy(found[:, 2, :], cnt[:]))
                dve.sem_inc(c.dve_gave.sem, 1)
                c.dve_gave.counted(1)
                dve.wait_ge(c.loaded[0].sem, c.loaded[0].at(32))
                st.mark(nc.vector.tensor_tensor(order.keep[:, 1:EC], recs[:, 1:EC, 0], recs[:, 0:EC - 1, 0], ALU.is_equal))
                st.mark(nc.vector.tensor_copy(order.first_key[:], recs[:, 0, 0:1]))
                st.then(nc.vector.tensor_tensor(same[:], recs[:, EC - 1, 0:1], next_key[:], ALU.is_equal))
                st.then(nc.vector.tensor_scalar(order.spill[:], recs[:, EC - 1, 0:1], 1.0, None, ALU.add))
                st.then(nc.vector.tensor_tensor(order.spill[:], order.spill[:], same[:], ALU.mult))
                st.then(nc.vector.tensor_scalar(order.spill[:], order.spill[:], -1.0, None, ALU.add))
                for t in range(2 * NIT):
                    st.mark(nc.vector.tensor_scalar(order.spill_at[:, t:t + 1], order.spill[:], float(-NK * t), None, ALU.add))
                neighbours(nc, st, recs)
                dve.wait_ge(c.moved.sem, c.moved.at(16 * 6))
                st.mark(nc.vector.tensor_copy(order.last_row[:], back[:, 0, :]))
                st.mark(nc.vector.tensor_copy(order.first_row[:], back[:, 1, :]))
                st.mark(nc.vector.tensor_copy(order.degree[:], back[:, 2, :]))
                st.close()

            @block.tensor
            def _(pe):
                pe.wait_ge(c.dve_gave2.sem, c.dve_gave2.at(1))
                for k in range(3):
                    last = nc.tensor.matmul(before[:], c.before[:], byte[k][:], start=k == 0, stop=k == 2)
                last.then_inc(c.pe_gave.sem, 1)
                c.pe_gave.counted(1)
        c.end_phase()



def edge_sum(c, order, neighbour, table, scanned, carry, weight=None):
    nc = c.nc
    with ExitStack() as ctx:
        rows = [c.sb(f"rows{s}", [P, K, D], ctx=ctx) for s in range(2)]
        index = [c.sb(f"index{s}", [P, K], I32, ctx) for s in range(2)]
        keep = [c.sb(f"keep{s}", [P, K], ctx=ctx) for s in range(2)]
        weigh = [c.sb(f"weigh{s}", [P, K], ctx=ctx) for s in range(2)]
        n_staged = 2 if weight is None else 3
        with nc.Block() as block:
            @block.scalar
            def _(act):
                with act.Fori(0, EIT) as i:
                    for s in range(2):
                        here = bass.ds(2 * K * i + s * K, K)
                        act.wait_ge(c.gathered[s].sem, c.gathered[s].at(16 * K * i))
                        act.wait_ge(c.computed[s].sem, c.computed[s].at(i))
                        nc.scalar.activation(index[s][:], neighbour[:, here], ACT.Copy).then_inc(c.staged[s].sem, 1)
                        nc.scalar.activation(keep[s][:], order.keep[:, here], ACT.Copy).then_inc(c.staged[s].sem, 1)
                        if weight is not None:
                            nc.scalar.activation(weigh[s][:], weight[:, here], ACT.Copy).then_inc(c.staged[s].sem, 1)

            @block.gpsimd
            def _(pool):
                with pool.Fori(0, EIT) as i:
                    for s in range(2):
                        pool.wait_ge(c.staged[s].sem, c.staged[s].at(n_staged * i + 1))
                        pool.wait_ge(c.stored[s].sem, c.stored[s].at(16 * i))
                        pool.wait_ge(c.computed[s].sem, c.computed[s].at(i))
                        pool.sem_inc(c.pool_turn.sem, 1)
                        for k in range(K):
                            pool.indirect_dma_start(out=rows[s][:, k, :], out_offset=None, in_=table,
                                                    in_offset=at_rows(index[s][:, k:k + 1])).then_inc(c.gathered[s].sem, 16)

            per = 2 * (D + 1 + (weight is not None))

            @block.vector
            def _(dve):
                st = Steps(dve, c.dve_step)
                st.then(nc.vector.memset(carry[:], 0.0))
                st.close()
                with dve.Fori(0, EIT) as i:
                    st = Steps(dve, c.dve_step, i, per)
                    for s in range(2):
                        dve.wait_ge(c.gathered[s].sem, c.gathered[s].at(16 * K * i + 16 * K))
                        dve.wait_ge(c.staged[s].sem, c.staged[s].at(n_staged * i + n_staged))
                        if weight is not None:
                            st.mark(nc.vector.tensor_tensor(rows[s][:], rows[s][:],
                                                            spread(weigh[s][:][:, :, None], [P, K, D]), ALU.mult))
                        st.wait()
                        for f in range(D):
                            st.mark(nc.vector.tensor_tensor_scan(rows[s][:, :, f], keep[s][:], rows[s][:, :, f],
                                                                 carry[:, f:f + 1], ALU.mult, ALU.add))
                        st.wait()
                        st.then(nc.vector.tensor_copy(carry[:], rows[s][:, K - 1, :]))
                        dve.sem_inc(c.computed[s].sem, 1)
                st.close(EIT)

            @block.sync
            def _(sp):
                out = scanned[0:EP, :].rearrange("(p j) f -> p j f", j=EC)
                with sp.Fori(0, EIT) as i:
                    for s in range(2):
                        sp.wait_ge(c.dve_step.sem, c.dve_step.at(1 + i * per + (s + 1) * per // 2 - 1))
                        sp.sem_inc(c.sp_turn.sem, 1)
                        sp.dma_start(out[:, bass.ds(2 * K * i + s * K, K), :], rows[s][:]).then_inc(c.stored[s].sem, 16)
                for s in range(2):
                    c.stored[s].counted(16 * EIT)
                    sp.wait_ge(c.stored[s].sem, c.stored[s].at(16 * EIT))
        for s in range(2):
            c.gathered[s].counted(16 * K * EIT)
            c.computed[s].counted(EIT)
            c.staged[s].counted(n_staged * EIT)
        c.end_phase()


def node_sums(c, order, scanned, carry, out):
    nc = c.nc
    W = out.shape[2]
    with ExitStack() as ctx:
        rows = [c.sb(f"rows{s}", [P, NK, W], ctx=ctx) for s in range(2)]
        index = [c.sb(f"index{s}", [P, NK], I32, ctx) for s in range(2)]
        spills = [c.sb(f"spills{s}", [P, NK, P], ctx=ctx) for s in range(2)]
        extra = [c.ps(f"extra{s}", [P, NK, W], ctx=ctx) for s in range(2)]
        with nc.Block() as block:
            @block.scalar
            def _(act):
                with act.Fori(0, NIT) as i:
                    for s in range(2):
                        act.wait_ge(c.gathered[s].sem, c.gathered[s].at(16 * NK * i))
                        nc.scalar.activation(index[s][:], order.last_row[:, bass.ds(2 * NK * i + s * NK, NK)],
                                             ACT.Copy).then_inc(c.staged[s].sem, 1)

            @block.gpsimd
            def _(pool):
                with pool.Fori(0, NIT) as i:
                    for s in range(2):
                        pool.wait_ge(c.staged[s].sem, c.staged[s].at(i + 1))
                        pool.wait_ge(c.computed[s].sem, c.computed[s].at(i))
                        pool.sem_inc(c.pool_turn.sem, 1)
                        for k in range(NK):
                            pool.indirect_dma_start(out=rows[s][:, k, :], out_offset=None, in_=scanned,
                                                    in_offset=at_rows(index[s][:, k:k + 1])).then_inc(c.gathered[s].sem, 16)

            @block.vector
            def _(dve):
                with dve.Fori(0, NIT) as i:
                    for s in range(2):
                        dve.wait_ge(c.pe_gave.sem, c.pe_gave.at(2 * i + s - 1))
                        nc.vector.tensor_scalar(spills[s][:], c.node_of[:], order.spill_at[:, bass.ds(2 * i + s, 1)], None,
                                                ALU.is_equal).then_inc(c.dve_gave.sem, 1)
                        dve.wait_ge(c.gathered[s].sem, c.gathered[s].at(16 * NK * i + 16 * NK))
                        dve.wait_ge(c.pe_gave.sem, c.pe_gave.at(2 * i + s + 1))
                        nc.vector.tensor_tensor(out[:, bass.ds(2 * NK * i + s * NK, NK), :], rows[s][:], extra[s][:],
                                                ALU.add).then_inc(c.computed[s].sem, 1)

            @block.tensor
            def _(pe):
                with pe.Fori(0, NIT) as i:
                    for s in range(2):
                        pe.wait_ge(c.dve_gave.sem, c.dve_gave.at(2 * i + s + 1))
                        pe.wait_ge(c.computed[s].sem, c.computed[s].at(i))
                        pe.sem_inc(c.pe_turn.sem, 1)
                        for k in range(NK):
                            last = nc.tensor.matmul(extra[s][:, k, :], spills[s][:, k, :], carry[:], start=True, stop=True)
                        last.then_inc(c.pe_gave.sem, 1)
        for s in range(2):
            c.gathered[s].counted(16 * NK * NIT)
            c.staged[s].counted(NIT)
            c.computed[s].counted(NIT)
        c.pe_gave.counted(2 * NIT)
        c.dve_gave.counted(2 * NIT)
        c.end_phase()


def node_scatter(c, order, values, first, filled):
    nc = c.nc
    W = values.shape[2]
    with ExitStack() as ctx:
        rows = [c.sb(f"rows{s}", [P, NK, W], ctx=ctx) for s in range(2)]
        index = [c.sb(f"index{s}", [P, NK], I32, ctx) for s in range(2)]
        begin = c.sb("begin", [P, W], ctx=ctx)
        with nc.Block() as block:
            @block.scalar
            def _(act):
                with act.Fori(0, NIT) as i:
                    for s in range(2):
                        here = bass.ds(2 * NK * i + s * NK, NK)
                        act.wait_ge(c.gathered[s].sem, c.gathered[s].at(16 * NK * i))
                        nc.scalar.activation(index[s][:], order.first_row[:, here], ACT.Copy).then_inc(c.staged[s].sem, 1)
                        nc.scalar.activation(rows[s][:], values[:, here, :], ACT.Copy).then_inc(c.staged[s].sem, 1)

            @block.gpsimd
            def _(pool):
                with pool.Fori(0, NIT) as i:
                    for s in range(2):
                        pool.wait_ge(c.staged[s].sem, c.staged[s].at(2 * i + 2))
                        pool.sem_inc(c.pool_turn.sem, 1)
                        for k in range(NK):
                            pool.indirect_dma_start(out=filled, out_offset=at_rows(index[s][:, k:k + 1]),
                                                    in_=rows[s][:, k, :], in_offset=None).then_inc(c.gathered[s].sem, 16)
                for s in range(2):
                    pool.wait_ge(c.gathered[s].sem, c.gathered[s].at(16 * NK * NIT))
                pool.indirect_dma_start(out=begin[:], out_offset=None, in_=first,
                                        in_offset=at_rows(order.first_key[:])).then_inc(c.gathered[0].sem, 16)

            @block.sync
            def _(sp):
                sp.wait_ge(c.gathered[1].sem, c.gathered[1].at(16 * NK * NIT))
                sp.wait_ge(c.gathered[0].sem, c.gathered[0].at(16 * NK * NIT + 16))
                sp.dma_start(filled[0:EP, :].rearrange("(p j) f -> p j f", j=EC)[:, 0, :], begin[:]).then_inc(c.moved.sem, 16)
                sp.wait_ge(c.moved.sem, c.moved.at(16))
        c.gathered[0].counted(16 * NK * NIT + 16)
        c.gathered[1].counted(16 * NK * NIT)
        for s in range(2):
            c.staged[s].counted(2 * NIT)
        c.moved.counted(16)
        c.end_phase()



def project(c, sources, weights, finish, finish_steps):
    nc = c.nc
    width = sum(x.shape[2] for x in sources)
    n = weights[0].shape[1]
    cuts = [(lo, min(lo + P, width)) for lo in range(0, width, P)]
    J, S = len(cuts), len(sources)
    with ExitStack() as ctx:
        side = c.sb("side", [P, NK, width], ctx=ctx)
        turned = [c.sb(f"turned{j}", [hi - lo, NK, P], ctx=ctx) for j, (lo, hi) in enumerate(cuts)]
        turn = c.ps("turn", [P, NK + 1, P], ctx=ctx)
        product = c.ps("product", [P, NK, n], ctx=ctx)
        with nc.Block() as block:
            @block.scalar
            def _(act):
                with act.Fori(0, 2 * NIT) as i:
                    here = bass.ds(NK * i, NK)
                    act.wait_ge(c.pe_gave.sem, c.pe_gave.at(J * i))
                    at = 0
                    for x in sources:
                        nc.scalar.activation(side[:, :, at:at + x.shape[2]], x[:, here, :], ACT.Copy)\
                            .then_inc(c.act_gave.sem, 1)
                        at += x.shape[2]
                    act.wait_ge(c.pe_gave2.sem, c.pe_gave2.at(i))
                    for j, (lo, hi) in enumerate(cuts):
                        act.wait_ge(c.pe_gave.sem, c.pe_gave.at(J * i + j + 1))
                        nc.scalar.activation(turned[j][:], turn[0:hi - lo, 0:NK, :], ACT.Copy)\
                            .then_inc(c.act_gave2.sem, 1)

            @block.tensor
            def _(pe):
                with pe.Fori(0, 2 * NIT) as i:
                    pe.wait_ge(c.act_gave.sem, c.act_gave.at(S * i + S))
                    pe.sem_inc(c.pe_turn.sem, 1)
                    for j, (lo, hi) in enumerate(cuts):
                        pe.wait_ge(c.act_gave2.sem, c.act_gave2.at(J * i + j))
                        pe.sem_inc(c.pe_turn.sem, 1)
                        for k in range(NK):
                            last = nc.tensor.transpose(turn[0:hi - lo, k, :], side[:, k, lo:hi], c.ident[:])
                        last.then_inc(c.pe_gave.sem, 1)
                    pe.wait_ge(c.act_gave2.sem, c.act_gave2.at(J * i + J))
                    pe.wait_ge(c.dve_gave.sem, c.dve_gave.at(i))
                    pe.sem_inc(c.pe_turn.sem, 1)
                    for k in range(NK):
                        for j in range(J):
                            last = nc.tensor.matmul(product[:, k, :], turned[j][:, k, :], weights[j],
                                                    start=j == 0, stop=j == J - 1)
                    last.then_inc(c.pe_gave2.sem, 1)

            @block.vector
            def _(dve):
                with dve.Fori(0, 2 * NIT) as i:
                    st = Steps(dve, c.dve_step, i, finish_steps)
                    dve.wait_ge(c.pe_gave2.sem, c.pe_gave2.at(i + 1))
                    finish(nc, st, bass.ds(NK * i, NK), product)
                    st.wait()
                    dve.sem_inc(c.dve_gave.sem, 1)
                st.close(2 * NIT)
        T = 2 * NIT
        c.act_gave.counted(S * T)
        c.act_gave2.counted(J * T)
        c.pe_gave.counted(J * T)
        c.pe_gave2.counted(T)
        c.dve_gave.counted(T)
        c.end_phase()


def vector_phase(c, work, stores=()):
    nc = c.nc
    roots = []
    with nc.Block() as block:
        @block.vector
        def _(dve):
            st = Steps(dve, c.dve_step)

            def by_act(func, out, in_, bias=0.0, scale=1.0):
                st.wait()
                roots.append((func, out, in_, bias, scale, st.base + st.k))
                dve.wait_ge(c.act_step.sem, c.act_step.at(len(roots)))

            work(nc, st, by_act)
            st.close()

        @block.scalar
        def _(act):
            for func, out, in_, bias, scale, when in roots:
                act.wait_ge(c.dve_step.sem, when)
                nc.scalar.activation(out, in_, func, bias=bias, scale=scale).then_inc(c.act_step.sem, 1)
            c.act_step.counted(len(roots))

        @block.sync
        def _(sp):
            sp.wait_ge(c.dve_step.sem, c.dve_step.at(c.dve_step.pending))
            for dst, src in stores:
                sp.dma_start(dst, src).then_inc(c.moved.sem, 16)
            c.moved.counted(16 * len(stores))
            sp.wait_ge(c.moved.sem, c.moved.at(16 * len(stores)))
    c.end_phase()


def node_rows(table):
    return table[0:NP, :].rearrange("(p c) f -> p c f", c=NC)


def whole(ap):
    return ap[:].rearrange("p c f -> p (c f)")


def layer_norm(c, nc, st, by_act, x, tmp, small):
    st.then(nc.vector.tensor_reduce(small[:], x[:], AX_X, ALU.add))
    st.then(nc.vector.tensor_scalar(small[:], small[:], 1.0 / D, None, ALU.mult))
    st.then(nc.vector.tensor_tensor(x[:], x[:], spread(small[:][:, :, None], [P, NC, D]), ALU.subtract))
    st.then(nc.vector.tensor_tensor(whole(tmp), whole(x), whole(x), ALU.mult))
    st.then(nc.vector.tensor_reduce(small[:], tmp[:], AX_X, ALU.add))
    by_act(ACT.Sqrt, small[:], small[:], c.eps[:], 1.0 / D)
    st.then(nc.vector.reciprocal(small[:], small[:]))
    st.then(nc.vector.tensor_tensor(x[:], x[:], spread(small[:][:, :, None], [P, NC, D]), ALU.mult))



def chebyshev_layer(c, order):
    with ExitStack() as ctx:
        norm = c.sb("norm", [P, NC], ctx=ctx)
        agg = c.sb("agg", [P, NC, D], ctx=ctx)
        x1 = c.sb("x1", [P, NC, D], ctx=ctx)
        by_norm = [P, NC, D]

        def first_table(nc, st, by_act):
            st.then(nc.vector.tensor_scalar(norm[:], order.degree[:], 1.0, None, ALU.max))
            by_act(ACT.Sqrt, norm[:], norm[:])
            st.then(nc.vector.reciprocal(norm[:], norm[:]))
            st.then(nc.vector.tensor_tensor(agg[:], c.x[:], spread(norm[:][:, :, None], by_norm), ALU.mult))

        vector_phase(c, first_table, [(node_rows(c.table), agg[:])])
        edge_sum(c, order, c.from_src, c.table, c.scanned, c.carry)
        node_sums(c, order, c.scanned, c.carry, agg)

        def second_table(nc, st, by_act):
            st.then(nc.vector.tensor_tensor(agg[:], agg[:], spread(norm[:][:, :, None], by_norm), ALU.mult))
            st.then(nc.vector.tensor_scalar(whole(x1), whole(agg), -1.0, None, ALU.mult))
            st.then(nc.vector.tensor_tensor(agg[:], x1[:], spread(norm[:][:, :, None], by_norm), ALU.mult))

        vector_phase(c, second_table, [(node_rows(c.table), agg[:])])
        edge_sum(c, order, c.from_src, c.table, c.scanned, c.carry)
        node_sums(c, order, c.scanned, c.carry, agg)

        def third(nc, st, by_act):
            st.then(nc.vector.tensor_tensor(agg[:], agg[:], spread(norm[:][:, :, None], by_norm), ALU.mult))
            st.then(nc.vector.scalar_tensor_tensor(out=whole(agg), in0=whole(agg), scalar=-2.0, in1=whole(c.x),
                                                   op0=ALU.mult, op1=ALU.subtract))

        vector_phase(c, third)

        def finish(nc, st, here, product):
            st.then(nc.vector.tensor_tensor(agg[:, here, :], product[:], spread(c.bias0[:][:, None, :], [P, NK, D]), ALU.add))
            st.mark(nc.vector.scalar_tensor_tensor(out=c.x[:, here, :], in0=agg[:, here, :], scalar=0.0,
                                                   in1=c.x[:, here, :], op0=ALU.max, op1=ALU.add))

        project(c, [c.x, x1, agg], [c.w0a[:], c.w0b[:]], finish, 2)
        vector_phase(c, lambda nc, st, by_act: layer_norm(c, nc, st, by_act, c.x, x1, norm))



def head_scores(c, scores):
    def finish(nc, st, here, product):
        st.mark(nc.vector.tensor_copy(scores[:, here, :], product[:]))

    project(c, [c.x], [c.wa[:]], finish, 1)


def attention_tables(c, scores, rows, a_dst):
    def work(nc, st, by_act):
        st.mark(nc.vector.memset(rows[:, :, D:TAB1], 1.0))
        st.mark(nc.vector.tensor_copy(a_dst[:], scores[:, :, HEADS:2 * HEADS]))
        st.then(nc.vector.tensor_copy(rows[:, :, 0:D], c.x[:]))
        st.then(nc.vector.tensor_copy(rows[:, :, D + 1:D + 1 + HEADS], scores[:, :, 0:HEADS]))

    vector_phase(c, work, [(node_rows(c.table1), rows[:]), (node_rows(c.a_dst_d), a_dst[:])])


def attention_edges(c, order, carry):
    nc = c.nc
    small = [P, K, HEADS]
    F1 = D + 1
    with ExitStack() as ctx:
        rows = [c.sb(f"rows{s}", [P, K, TAB1], ctx=ctx) for s in range(2)]
        index = [c.sb(f"index{s}", [P, K], I32, ctx) for s in range(2)]
        keep = c.sb("keep", [P, K], ctx=ctx)
        target = [c.sb(f"target{s}", small, ctx=ctx) for s in range(2)]
        sums = [c.sb(f"sums{s}", [P, K, HEADS, HW_], ctx=ctx) for s in range(2)]
        line = [c.sb(f"line{b}", [P, F1, K + 1], ctx=ctx) for b in range(2)]
        factor = [c.sb(f"factor{b}", [P, F1, K + 1], ctx=ctx) for b in range(2)]
        target_carry = c.sb("target_carry", [P, HEADS], ctx=ctx)
        reset = c.sb("reset", [P, K], ctx=ctx)
        raw = c.sb("raw", small, ctx=ctx)
        score = c.sb("score", small, ctx=ctx)
        top = c.sb("top", [P, K + 1, HEADS], ctx=ctx)
        gap = c.sb("gap", small, ctx=ctx)
        fall = c.sb("fall", [P, K + 1, HEADS], ctx=ctx)
        power = c.sb("power", small, ctx=ctx)
        PER_SLOT = 3 * HEADS + 10

        with nc.Block() as block:
            @block.scalar
            def _(act):
                out = c.scanned1[0:EP, :].rearrange("(p j) f -> p j f", j=EC)
                with act.Fori(0, EIT) as i:
                    def begin(n):
                        s, h, b, m = n // HEADS, n % HEADS, n % 2, n // 2
                        act.wait_ge(c.taken[b].sem, c.taken[b].at(HEADS * i + m))
                        nc.scalar.activation(factor[b][:], spread(fall[:, :, h][:, None, :], [P, F1, K + 1]), ACT.Copy)\
                            .then_inc(c.act_gave2.sem, 1)
                        act.wait_ge(c.copied[b].sem, c.copied[b].at(HEADS * i + m))
                        nc.scalar.activation(line[b][:, :, 0], sums[1 - s][:, K - 1, h, 0:F1], ACT.Copy)\
                            .then_inc(c.act_gave2.sem, 1)

                    def end(n):
                        s, h, b, m = n // HEADS, n % HEADS, n % 2, n // 2
                        if h == 0:
                            act.wait_ge(c.stored[s].sem, c.stored[s].at(16 * i))
                        act.wait_ge(c.taken[b].sem, c.taken[b].at(HEADS * i + (m + 1)))
                        nc.scalar.activation(sums[s][:, :, h, 0:F1], line[b][:, :, 1:K + 1].rearrange("p f k -> p k f"),
                                             ACT.Copy).then_inc(c.copied[b].sem, 1)

                    for s in range(2):
                        act.wait_ge(c.dve_gave.sem, c.dve_gave.at(2 * (2 * i + s) + 1))
                        nc.scalar.activation(power[:], score[:], ACT.Exp).then_inc(c.act_gave.sem, 1)
                        act.wait_ge(c.dve_gave.sem, c.dve_gave.at(2 * (2 * i + s) + 2))
                        nc.scalar.activation(fall[:, 1:K + 1, :], gap[:], ACT.Exp).then_inc(c.act_gave.sem, 1)
                        act.wait_ge(c.act_gave.sem, c.act_gave.at(2 * (2 * i + s) + 2))
                        begin(s * HEADS)
                        for h in range(1, HEADS):
                            begin(s * HEADS + h)
                            end(s * HEADS + h - 1)
                        last = s * HEADS + HEADS - 1
                        end(last)
                        act.wait_ge(c.copied[last % 2].sem, c.copied[last % 2].at(HEADS * i + (last // 2 + 1)))
                        act.wait_ge(c.computed[s].sem, c.computed[s].at(i + 1))
                        act.dma_start(out[:, bass.ds(2 * K * i + s * K, K), :],
                                      sums[s][:].rearrange("p k h f -> p k (h f)")).then_inc(c.stored[s].sem, 16)
                for s in range(2):
                    c.stored[s].counted(16 * EIT)
                    act.wait_ge(c.stored[s].sem, c.stored[s].at(16 * EIT))

            @block.gpsimd
            def _(pool):
                with pool.Fori(0, EIT) as i:
                    for s in range(2):
                        pool.wait_ge(c.gathered[s].sem, c.gathered[s].at(16 * K * i))
                        pool.wait_ge(c.computed[s].sem, c.computed[s].at(i))
                        pool.sem_inc(c.pool_turn.sem, 1)
                        nc.gpsimd.tensor_copy(index[s][:], c.from_src[:, bass.ds(2 * K * i + s * K, K)])\
                            .then_inc(c.staged[s].sem, 1)
                        pool.wait_ge(c.staged[s].sem, c.staged[s].at(i + 1))
                        pool.sem_inc(c.pool_turn.sem, 1)
                        for k in range(K):
                            pool.indirect_dma_start(out=rows[s][:, k, :], out_offset=None, in_=c.table1,
                                                    in_offset=at_rows(index[s][:, k:k + 1])).then_inc(c.gathered[s].sem, 16)

            @block.sync
            def _(sp):
                fill = c.fill1[0:EP, :].rearrange("(p j) f -> p j f", j=EC)
                with sp.Fori(0, EIT) as i:
                    for s in range(2):
                        sp.wait_ge(c.computed[s].sem, c.computed[s].at(i))
                        sp.sem_inc(c.sp_turn.sem, 1)
                        sp.dma_start(target[s][:], fill[:, bass.ds(2 * K * i + s * K, K), :]).then_inc(c.loaded[s].sem, 16)
                for s in range(2):
                    c.loaded[s].counted(16 * EIT)

            @block.vector
            def _(dve):
                st = Steps(dve, c.dve_step)
                st.mark(nc.vector.memset(sums[1][:, K - 1, :, :], 0.0))
                st.mark(nc.vector.memset(fall[:, 0, :], 0.0))
                st.mark(nc.vector.memset(target_carry[:], 0.0))
                st.then(nc.vector.memset(top[:, 0, :], -BIG))
                st.close()
                with dve.Fori(0, EIT) as i:
                    st = Steps(dve, c.dve_step, i, 2 * PER_SLOT)
                    for s in range(2):
                        st.then(nc.vector.tensor_copy(keep[:], order.keep[:, bass.ds(2 * K * i + s * K, K)]))
                        dve.wait_ge(c.loaded[s].sem, c.loaded[s].at(16 * i + 16))
                        for h in range(HEADS):
                            st.mark(nc.vector.tensor_tensor_scan(target[s][:, :, h], keep[:], target[s][:, :, h],
                                                                 target_carry[:, h:h + 1], ALU.mult, ALU.add))
                        st.then(nc.vector.tensor_scalar(reset[:], keep[:], -1.0, BIG, ALU.add, ALU.mult))
                        dve.wait_ge(c.gathered[s].sem, c.gathered[s].at(16 * K * i + 16 * K))
                        st.then(nc.vector.tensor_tensor(raw[:], rows[s][:, :, F1:F1 + HEADS], target[s][:], ALU.add))
                        st.then(nc.vector.scalar_tensor_tensor(out=score[:], in0=raw[:], scalar=0.2, in1=raw[:],
                                                               op0=ALU.mult, op1=ALU.max))
                        st.mark(nc.vector.tensor_copy(target_carry[:], target[s][:, K - 1, :]))
                        for h in range(HEADS):
                            st.mark(nc.vector.tensor_tensor_scan(top[:, 1:K + 1, h], reset[:], score[:, :, h],
                                                                 top[:, 0, h:h + 1], ALU.add, ALU.max))
                        st.wait()
                        st.then(nc.vector.tensor_tensor(score[:], score[:], top[:, 1:K + 1, :], ALU.subtract))
                        dve.sem_inc(c.dve_gave.sem, 1)
                        st.then(nc.vector.tensor_tensor(gap[:], top[:, 0:K, :], top[:, 1:K + 1, :], ALU.subtract))
                        st.then(nc.vector.tensor_tensor(gap[:], gap[:], spread(reset[:][:, :, None], small), ALU.add))
                        dve.sem_inc(c.dve_gave.sem, 1)
                        dve.wait_ge(c.stored[s].sem, c.stored[s].at(16 * i))
                        st.mark(nc.vector.tensor_copy(sums[s][:, :, :, F1], top[:, 1:K + 1, :]))
                        st.mark(nc.vector.tensor_copy(top[:, 0, :], top[:, K, :]))
                        dve.wait_ge(c.act_gave.sem, c.act_gave.at(2 * (2 * i + s) + 1))
                        for h in range(HEADS):
                            n = s * HEADS + h
                            b, m = n % 2, n // 2
                            dve.wait_ge(c.copied[b].sem, c.copied[b].at(HEADS * i + m))
                            st.then(nc.vector.tensor_tensor(line[b][:, :, 1:K + 1],
                                                            rows[s][:, :, 0:F1].rearrange("p k f -> p f k"),
                                                            spread(power[:, :, h][:, None, :], [P, F1, K]), ALU.mult))
                            if h == HEADS - 1:
                                dve.sem_inc(c.computed[s].sem, 1)
                            dve.wait_ge(c.act_gave2.sem, c.act_gave2.at(2 * HEADS * (2 * i + s) + (2 * h + 2)))
                            nc.vector.tensor_tensor_scan(line[b][:].rearrange("p f k -> p (f k)"),
                                                         factor[b][:].rearrange("p f k -> p (f k)"),
                                                         line[b][:].rearrange("p f k -> p (f k)"),
                                                         0.0, ALU.mult, ALU.add).then_inc(c.taken[b].sem, 1)
                st.close(EIT)
                for b in range(2):
                    c.taken[b].counted(HEADS * EIT)
                    c.copied[b].counted(HEADS * EIT)
                    dve.wait_ge(c.copied[b].sem, c.copied[b].at(HEADS * EIT))
                st = Steps(dve, c.dve_step)
                st.mark(nc.vector.tensor_copy(carry[:], sums[1][:, K - 1, :, :]))
                st.close()
        for s in range(2):
            c.gathered[s].counted(16 * K * EIT)
            c.computed[s].counted(EIT)
            c.staged[s].counted(EIT)
        c.dve_gave.counted(4 * EIT)
        c.act_gave.counted(4 * EIT)
        c.act_gave2.counted(4 * HEADS * EIT)
        c.end_phase()


def merge_carries(c, order, carry, merged):
    nc = c.nc
    with ExitStack() as ctx:
        tops = c.sb("tops", [P, P, HEADS], ctx=ctx)
        nodes = c.sb("nodes", [P, P], ctx=ctx)
        follow = c.sb("follow", [P, 1], ctx=ctx)
        last = c.sb("last", [P, 1], ctx=ctx)
        apart = c.sb("apart", [P, P], ctx=ctx)
        seen = c.sb("seen", [P, HEADS, P], ctx=ctx)
        top = c.sb("top", [P, HEADS], ctx=ctx)
        own = c.sb("own", [P, HEADS], ctx=ctx)
        scale = c.sb("scale", [P, HEADS], ctx=ctx)
        end = c.sb("end", [P, 1], ctx=ctx)
        wide = [P, HEADS, D + 1]
        with nc.Block() as block:
            @block.sync
            def _(sp):
                sp.wait_ge(c.dve_gave.sem, c.dve_gave.at(1))
                sp.dma_start(c.tops_d, own[:]).then_inc(c.moved.sem, 16)
                sp.dma_start(c.nodes_d[0:P, :], order.spill[:]).then_inc(c.moved.sem, 16)
                sp.dma_start(c.nodes_d[P:P + 1, :], end[0:1, :]).then_inc(c.moved.sem, 16)
                sp.wait_ge(c.moved.sem, c.moved.at(48))
                sp.dma_start(tops[:].rearrange("p q h -> p (q h)"),
                             spread(c.tops_d.rearrange("(a q) h -> a (q h)", a=1), [P, P * HEADS])).then_inc(c.moved.sem, 16)
                sp.dma_start(nodes[:], spread(c.nodes_d[0:P, :].rearrange("q a -> a q"), [P, P]),
                             allow_slow_non_contiguous=True).then_inc(c.moved.sem, 16)
                sp.dma_start(follow[:], c.nodes_d[1:P + 1, :]).then_inc(c.moved.sem, 16)
                c.moved.counted(96)

            @block.vector
            def _(dve):
                st = Steps(dve, c.dve_step)
                st.mark(nc.vector.memset(end[:], -2.0))
                st.then(nc.vector.tensor_copy(own[:], carry[:, :, D + 1]))
                dve.sem_inc(c.dve_gave.sem, 1)
                dve.wait_ge(c.moved.sem, c.moved.at(96))
                st.then(nc.vector.tensor_scalar(apart[:], nodes[:], order.spill[:], None, ALU.is_equal))
                st.then(nc.vector.tensor_scalar(apart[:], apart[:], -1.0, BIG, ALU.add, ALU.mult))
                st.then(nc.vector.tensor_tensor(seen[:], tops[:].rearrange("p q h -> p h q"),
                                                spread(apart[:][:, None, :], [P, HEADS, P]), ALU.add))
                st.then(nc.vector.tensor_reduce(top[:], seen[:], AX_X, ALU.max))
                st.then(nc.vector.tensor_tensor(scale[:], own[:], top[:], ALU.subtract))
                dve.sem_inc(c.dve_gave.sem, 1)
                st.then(nc.vector.tensor_tensor(last[:], follow[:], order.spill[:], ALU.is_equal))
                st.then(nc.vector.tensor_scalar(last[:], last[:], -1.0, 1.0, ALU.mult, ALU.add))
                st.mark(nc.vector.tensor_copy(merged[:, ROW1:ROW1 + 1], last[:]))
                grid = merged[:, 0:ROW1].rearrange("p (h f) -> p h f", h=HEADS)
                st.mark(nc.vector.tensor_scalar(grid[:, :, D + 1], top[:], last[:], None, ALU.mult))
                dve.wait_ge(c.act_gave.sem, c.act_gave.at(1))
                st.mark(nc.vector.tensor_tensor(grid[:, :, 0:D + 1], carry[:, :, 0:D + 1],
                                                spread(scale[:][:, :, None], wide), ALU.mult))
                st.close()

            @block.scalar
            def _(act):
                act.wait_ge(c.dve_gave.sem, c.dve_gave.at(2))
                nc.scalar.activation(scale[:], scale[:], ACT.Exp).then_inc(c.act_gave.sem, 1)
        c.dve_gave.counted(2)
        c.act_gave.counted(1)
        c.end_phase()


def attention_nodes(c, order, scores, merged, out):
    nc = c.nc
    cuts = [(lo, min(lo + P, HEADS * D)) for lo in range(0, HEADS * D, P)]
    J = len(cuts)
    with ExitStack() as ctx:
        rows = [c.sb(f"rows{s}", [P, NK, ROW1], ctx=ctx) for s in range(2)]
        index = [c.sb(f"index{s}", [P, NK], I32, ctx) for s in range(2)]
        spills = c.sb("spills", [P, NK, P], ctx=ctx)
        extra = [c.sb(f"extra{s}", [P, NK, ROW1 + 1], ctx=ctx) for s in range(2)]
        own = c.sb("own", [P, NC, HEADS], ctx=ctx)
        top = c.sb("top", [P, NK, HEADS], ctx=ctx)
        tops3 = c.sb("tops3", [P, 3, NK, HEADS], ctx=ctx)
        scale = c.sb("scale", [P, 3, NK, HEADS], ctx=ctx)
        mean = c.sb("mean", [P, NK, HEADS, D + 1], ctx=ctx)
        part = c.sb("part", [P, NK, HEADS, D + 1], ctx=ctx)
        weight = c.sb("weight", [P, NK, HEADS], ctx=ctx)
        normed = [c.sb(f"normed{s}", [P, NK, HEADS * D], ctx=ctx) for s in range(2)]
        turned = [c.sb(f"turned{j}", [hi - lo, NK, P], ctx=ctx) for j, (lo, hi) in enumerate(cuts)]
        spilled = [c.ps(f"spilled{k}", [P, 512], ctx=ctx) for k in range(2)]
        turn = c.ps("turn", [P, NK + 1, P], ctx=ctx)
        product = c.ps("product", [P, NK, D], ctx=ctx)
        T = 2 * NIT

        wide = [P, NK, HEADS, D + 1]

        with nc.Block() as block:
            @block.gpsimd
            def _(pool):
                with pool.Fori(0, NIT) as i:
                    for s in range(2):
                        pool.wait_ge(c.gathered[s].sem, c.gathered[s].at(16 * NK * i))
                        pool.wait_ge(c.computed[s].sem, c.computed[s].at(i))
                        pool.sem_inc(c.pool_turn.sem, 1)
                        nc.gpsimd.tensor_copy(index[s][:], order.last_row[:, bass.ds(2 * NK * i + s * NK, NK)])\
                            .then_inc(c.staged[s].sem, 1)
                        pool.wait_ge(c.staged[s].sem, c.staged[s].at(i + 1))
                        pool.sem_inc(c.pool_turn.sem, 1)
                        for k in range(NK):
                            pool.indirect_dma_start(out=rows[s][:, k, :], out_offset=None, in_=c.scanned1,
                                                    in_offset=at_rows(index[s][:, k:k + 1])).then_inc(c.gathered[s].sem, 16)

            @block.tensor
            def _(pe):
                def spilled_sums(t):
                    pe.wait_ge(c.dve_gave.sem, c.dve_gave.at(t + 1))
                    pe.sem_inc(c.pe_turn.sem, 1)
                    for k in range(NK):
                        pe.wait_ge(c.act_gave.sem, c.act_gave.at(NK * t + k - 1))
                        pe.sem_inc(c.pe_turn.sem, 1)
                        nc.tensor.matmul(spilled[k % 2][:, 0:ROW1 + 1], spills[:, k, :], merged[:],
                                         start=True, stop=True).then_inc(c.pe_gave.sem, 1)

                def times_w(t, s):
                    pe.wait_ge(c.dve_gave2.sem, c.dve_gave2.at(t + 1))
                    pe.sem_inc(c.pe_turn.sem, 1)
                    for j, (lo, hi) in enumerate(cuts):
                        pe.wait_ge(c.act_gave2.sem, c.act_gave2.at(J * t + j))
                        pe.sem_inc(c.pe_turn.sem, 1)
                        for k in range(NK):
                            last = nc.tensor.transpose(turn[0:hi - lo, k, :], normed[s][:, k, lo:hi], c.ident[:])
                        last.then_inc(c.pe_gave2.sem, 1)
                    pe.wait_ge(c.act_gave2.sem, c.act_gave2.at(J * t + J))
                    pe.wait_ge(c.taken[0].sem, c.taken[0].at(t))
                    pe.sem_inc(c.pe_turn.sem, 1)
                    for k in range(NK):
                        for j in range(J):
                            last = nc.tensor.matmul(product[:, k, :], turned[j][:, k, :], c.w1h[j][:],
                                                    start=j == 0, stop=j == J - 1)
                    last.then_inc(c.taken[1].sem, 1)

                spilled_sums(0)
                spilled_sums(1)
                with pe.Fori(0, NIT - 1) as i2:
                    for s in range(2):
                        times_w(2 * i2 + s, s)
                        spilled_sums(2 * i2 + (s + 2))
                times_w(T - 2, 0)
                times_w(T - 1, 1)

            @block.scalar
            def _(act):
                def copy_spilled(t, s):
                    act.wait_ge(c.dve_gave2.sem, c.dve_gave2.at(t - 1))
                    for k in range(NK):
                        act.wait_ge(c.pe_gave.sem, c.pe_gave.at(NK * t + k + 1))
                        nc.scalar.activation(extra[s][:, k, :], spilled[k % 2][:, 0:ROW1 + 1], ACT.Copy)\
                            .then_inc(c.act_gave.sem, 1)

                def scales(t):
                    act.wait_ge(c.loaded_by_dve.sem, c.loaded_by_dve.at(t + 1))
                    nc.scalar.activation(scale[:], tops3[:], ACT.Exp).then_inc(c.act_step.sem, 1)

                def copy_turned(t):
                    act.wait_ge(c.taken[1].sem, c.taken[1].at(t))
                    for j, (lo, hi) in enumerate(cuts):
                        act.wait_ge(c.pe_gave2.sem, c.pe_gave2.at(J * t + j + 1))
                        nc.scalar.activation(turned[j][:], turn[0:hi - lo, 0:NK, :], ACT.Copy)\
                            .then_inc(c.act_gave2.sem, 1)

                copy_spilled(0, 0)
                scales(0)
                copy_spilled(1, 1)
                with act.Fori(0, NIT - 1) as i2:
                    for s in range(2):
                        scales(2 * i2 + (s + 1))
                        copy_turned(2 * i2 + s)
                        copy_spilled(2 * i2 + (s + 2), s)
                scales(T - 1)
                copy_turned(T - 2)
                copy_turned(T - 1)

            @block.vector
            def _(dve):
                def map_spilled(st, t):
                    dve.wait_ge(c.pe_gave.sem, c.pe_gave.at(NK * t))
                    st.then(nc.vector.tensor_scalar(spills[:], c.node_of[:], order.spill_at[:, bass.ds(t, 1)], None,
                                                    ALU.is_equal))
                    dve.sem_inc(c.dve_gave.sem, 1)

                def maxima(st, t, s, it):
                    got = rows[s][:].rearrange("p k (h f) -> p k h f", h=HEADS)
                    more = extra[s][:, :, 0:ROW1].rearrange("p k (h f) -> p k h f", h=HEADS)
                    dve.wait_ge(c.act_gave.sem, c.act_gave.at(NK * t + NK))
                    dve.wait_ge(c.gathered[s].sem, c.gathered[s].at(16 * NK * it + 16 * NK))
                    st.then(nc.vector.tensor_scalar(weight[:], spread(extra[s][:, :, ROW1:ROW1 + 1], [P, NK, HEADS]),
                                                    -1.0, BIG, ALU.add, ALU.mult))
                    st.then(nc.vector.tensor_tensor(tops3[:, 1, :, :], more[:, :, :, D + 1], weight[:], ALU.add))
                    st.mark(nc.vector.tensor_copy(tops3[:, 0, :, :], got[:, :, :, D + 1]))
                    st.then(nc.vector.tensor_copy(tops3[:, 2, :, :], own[:, bass.ds(NK * t, NK), :]))
                    st.then(nc.vector.tensor_tensor(top[:], tops3[:, 0, :, :], tops3[:, 1, :, :], ALU.max))
                    st.then(nc.vector.tensor_tensor(top[:], top[:], tops3[:, 2, :, :], ALU.max))
                    st.then(nc.vector.tensor_tensor(tops3[:].rearrange("p a k h -> p a (k h)"),
                                                    tops3[:].rearrange("p a k h -> p a (k h)"),
                                                    spread(top[:].rearrange("p k h -> p (k h)")[:, None, :],
                                                           [P, 3, NK * HEADS]), ALU.subtract))
                    dve.sem_inc(c.loaded_by_dve.sem, 1)

                def weigh(st, t, s):
                    got = rows[s][:].rearrange("p k (h f) -> p k h f", h=HEADS)
                    more = extra[s][:, :, 0:ROW1].rearrange("p k (h f) -> p k h f", h=HEADS)
                    dve.wait_ge(c.act_step.sem, c.act_step.at(t + 1))
                    by = [spread(scale[:, n, :, :][:, :, :, None], wide) for n in range(3)]
                    st.mark(nc.vector.tensor_tensor(mean[:], got[:, :, :, 0:D + 1], by[0], ALU.mult))
                    st.then(nc.vector.tensor_tensor(part[:], more[:, :, :, 0:D + 1], by[1], ALU.mult))
                    st.then(nc.vector.tensor_tensor(mean[:], mean[:], part[:], ALU.add))
                    st.mark(nc.vector.tensor_copy(part[:, :, :, D], scale[:, 2, :, :]))
                    st.then(nc.vector.tensor_tensor(part[:, :, :, 0:D],
                                                    spread(c.x[:, bass.ds(NK * t, NK), :][:, :, None, :], [P, NK, HEADS, D]),
                                                    spread(scale[:, 2, :, :][:, :, :, None], [P, NK, HEADS, D]), ALU.mult))
                    st.then(nc.vector.tensor_tensor(mean[:], mean[:], part[:], ALU.add))
                    st.then(nc.vector.tensor_scalar(weight[:], mean[:, :, :, D], 1e-16, None, ALU.add))
                    st.then(nc.vector.reciprocal(weight[:], weight[:]))
                    dve.wait_ge(c.taken[1].sem, c.taken[1].at(t - 1))
                    st.then(nc.vector.tensor_tensor(normed[s][:].rearrange("p k (h f) -> p k h f", h=HEADS),
                                                    mean[:, :, :, 0:D],
                                                    spread(weight[:][:, :, :, None], [P, NK, HEADS, D]), ALU.mult))
                    dve.sem_inc(c.dve_gave2.sem, 1)
                    dve.sem_inc(c.computed[s].sem, 1)

                def finish(st, t):
                    here = bass.ds(NK * t, NK)
                    dve.wait_ge(c.taken[1].sem, c.taken[1].at(t + 1))
                    st.then(nc.vector.scalar_tensor_tensor(out=out[:, here, :], in0=product[:], scalar=1.0 / HEADS,
                                                           in1=spread(c.bias1[:][:, None, :], [P, NK, D]),
                                                           op0=ALU.mult, op1=ALU.add))
                    dve.sem_inc(c.taken[0].sem, 1)
                    st.then(nc.vector.tensor_tensor(out[:, here, :], out[:, here, :], c.x[:, here, :], ALU.add))
                    st.then(nc.vector.tensor_tensor(out[:, here, :], out[:, here, :], c.x[:, here, :], ALU.add))

                st = Steps(dve, c.dve_step)
                st.then(nc.vector.tensor_tensor(own[:], scores[:, :, 0:HEADS], scores[:, :, HEADS:2 * HEADS], ALU.add))
                st.then(nc.vector.scalar_tensor_tensor(out=own[:], in0=own[:], scalar=0.2, in1=own[:],
                                                       op0=ALU.mult, op1=ALU.max))
                map_spilled(st, 0)
                maxima(st, 0, 0, 0)
                map_spilled(st, 1)
                weigh(st, 0, 0)
                st.close()
                with dve.Fori(0, NIT - 1) as i2:
                    st = Steps(dve, c.dve_step, i2, 2 * 20)
                    for s in range(2):
                        maxima(st, 2 * i2 + (s + 1), 1 - s, i2 + s)
                        map_spilled(st, 2 * i2 + (s + 2))
                        weigh(st, 2 * i2 + (s + 1), 1 - s)
                        finish(st, 2 * i2 + s)
                st.close(NIT - 1)
                st = Steps(dve, c.dve_step)
                maxima(st, T - 1, 1, NIT - 1)
                weigh(st, T - 1, 1)
                finish(st, T - 2)
                finish(st, T - 1)
                st.close()
        for s in range(2):
            c.gathered[s].counted(16 * NK * NIT)
            c.staged[s].counted(NIT)
            c.computed[s].counted(NIT)
            c.taken[s].counted(T)
        c.dve_gave.counted(T)
        c.dve_gave2.counted(T)
        c.loaded_by_dve.counted(T)
        c.act_step.counted(T)
        c.act_gave.counted(NK * T)
        c.act_gave2.counted(J * T)
        c.pe_gave.counted(NK * T)
        c.pe_gave2.counted(J * T)
        c.end_phase()


def attention_layer(c, order):
    with ExitStack() as ctx:
        scores = c.sb("scores", [P, NC, 2 * HEADS], ctx=ctx)
        carry = c.sb("carry1", [P, HEADS, HW_], ctx=ctx)
        merged = c.sb("merged", [P, ROW1 + 1], ctx=ctx)
        with ExitStack() as ctx2:
            rows = c.sb("rows_of_x", [P, NC, TAB1], ctx=ctx2)
            a_dst = c.sb("a_dst", [P, NC, HEADS], ctx=ctx2)
            head_scores(c, scores)
            attention_tables(c, scores, rows, a_dst)
            node_scatter(c, order, a_dst, c.a_dst_d, c.fill1)
        attention_edges(c, order, carry)
        merge_carries(c, order, carry, merged)
        with ExitStack() as ctx2:
            new = c.sb("new", [P, NC, D], ctx=ctx2)
            attention_nodes(c, order, scores, merged, new)
            tmp_small = c.sb("small", [P, NC], ctx=ctx2)

            def work(nc, st, by_act):
                st.then(nc.vector.tensor_copy(whole(c.x), whole(new)))
                layer_norm(c, nc, st, by_act, c.x, new, tmp_small)

            vector_phase(c, work)



def edge_halves(c, l, order, x):
    nc = c.nc
    T = 2 * NIT
    HALF = NK * P // 2
    with ExitStack() as ctx:
        side = c.sb("side", [P, NK, D], ctx=ctx)
        turned = c.sb("turned", [D, NK * P], ctx=ctx)
        hidden = c.sb("hidden", [P, NK * P], ctx=ctx)
        u = [c.sb(f"u{s}", [P, NK, D], ctx=ctx) for s in range(2)]
        v = [c.sb(f"v{s}", [P, NK, D], ctx=ctx) for s in range(2)]
        index = [c.sb(f"index{s}", [P, NK], I32, ctx) for s in range(2)]
        begin = c.sb("begin", [P, D], ctx=ctx)
        turn = c.ps("turn", [D, NK + 1, P], ctx=ctx)
        inner = c.ps("inner", [P, 2, 512], ctx=ctx)
        outer = c.ps("outer", [P, NK + 1, P], ctx=ctx)
        with nc.Block() as block:
            @block.scalar
            def _(act):
                with act.Fori(0, T) as i:
                    act.wait_ge(c.pe_gave.sem, c.pe_gave.at(2 * i))
                    nc.scalar.activation(side[:], x[:, bass.ds(NK * i, NK), :], ACT.Copy).then_inc(c.act_gave.sem, 1)
                    act.wait_ge(c.pe_gave.sem, c.pe_gave.at(2 * i + 1))
                    nc.scalar.activation(turned[:], turn[:, 0:NK, :], ACT.Copy).then_inc(c.act_gave2.sem, 1)
                    act.wait_ge(c.pe_gave.sem, c.pe_gave.at(2 * i + 2))
                    act.wait_ge(c.pe_gave2.sem, c.pe_gave2.at(i))
                    for g in range(2):
                        nc.scalar.activation(hidden[:, HALF * g:HALF * g + HALF], inner[:, g, 0:HALF], ACT.Relu,
                                             bias=c.bf[l][:]).then_inc(c.act_gave2.sem, 1)

            @block.tensor
            def _(pe):
                with pe.Fori(0, T) as i:
                    pe.wait_ge(c.act_gave.sem, c.act_gave.at(i + 1))
                    pe.sem_inc(c.pe_turn.sem, 1)
                    for k in range(NK):
                        last = nc.tensor.transpose(turn[:, k, :], side[:, k, :], c.ident[:])
                    last.then_inc(c.pe_gave.sem, 1)
                    pe.wait_ge(c.act_gave2.sem, c.act_gave2.at(3 * i + 1))
                    pe.sem_inc(c.pe_turn.sem, 1)
                    for g in range(2):
                        last = nc.tensor.matmul(inner[:, g, 0:HALF], c.wf[l][:], turned[:, HALF * g:HALF * g + HALF],
                                                start=True, stop=True)
                    last.then_inc(c.pe_gave.sem, 1)
                    pe.wait_ge(c.act_gave2.sem, c.act_gave2.at(3 * i + 3))
                    pe.wait_ge(c.dve_gave.sem, c.dve_gave.at(2 * i))
                    pe.sem_inc(c.pe_turn.sem, 1)
                    for k in range(NK):
                        last = nc.tensor.matmul(outer[:, k, :], hidden[:, k * P:k * P + P], c.wuv[l][:],
                                                start=True, stop=True)
                    last.then_inc(c.pe_gave2.sem, 1)

            @block.vector
            def _(dve):
                with dve.Fori(0, NIT) as i2:
                    for s in range(2):
                        i = 2 * i2 + s
                        dve.wait_ge(c.pe_gave2.sem, c.pe_gave2.at(i + 1))
                        dve.wait_ge(c.gathered[s].sem, c.gathered[s].at(16 * NK * i2))
                        dve.wait_ge(c.stored[s].sem, c.stored[s].at(32 * i2))
                        nc.vector.tensor_copy(u[s][:], outer[:, 0:NK, 0:D]).then_inc(c.dve_gave.sem, 1)
                        nc.vector.tensor_tensor(v[s][:], outer[:, 0:NK, D:P],
                                                spread(c.buv[l][:][:, None, :], [P, NK, D]), ALU.add)\
                            .then_inc(c.dve_gave.sem, 1)

            @block.gpsimd
            def _(pool):
                with pool.Fori(0, NIT) as i2:
                    for s in range(2):
                        i = 2 * i2 + s
                        pool.wait_ge(c.gathered[s].sem, c.gathered[s].at(16 * NK * i2))
                        pool.sem_inc(c.pool_turn.sem, 1)
                        nc.gpsimd.tensor_copy(index[s][:], order.first_row[:, bass.ds(NK * i, NK)])\
                            .then_inc(c.staged[s].sem, 1)
                        pool.wait_ge(c.staged[s].sem, c.staged[s].at(i2 + 1))
                        pool.wait_ge(c.dve_gave.sem, c.dve_gave.at(2 * i + 1))
                        pool.sem_inc(c.pool_turn.sem, 1)
                        for k in range(NK):
                            pool.indirect_dma_start(out=c.fill, out_offset=at_rows(index[s][:, k:k + 1]),
                                                    in_=u[s][:, k, :], in_offset=None).then_inc(c.gathered[s].sem, 16)
                for s in range(2):
                    pool.wait_ge(c.stored[s].sem, c.stored[s].at(32 * NIT))
                pool.indirect_dma_start(out=begin[:], out_offset=None, in_=c.table_u,
                                        in_offset=at_rows(order.first_key[:])).then_inc(c.moved_by_pool.sem, 16)

            @block.sync
            def _(sp):
                with sp.Fori(0, NIT) as i2:
                    for s in range(2):
                        i = 2 * i2 + s
                        here = bass.ds(NK * i, NK)
                        sp.wait_ge(c.dve_gave.sem, c.dve_gave.at(2 * i + 2))
                        sp.sem_inc(c.sp_turn.sem, 1)
                        sp.dma_start(node_rows(c.table_u)[:, here, :], u[s][:]).then_inc(c.stored[s].sem, 16)
                        sp.dma_start(node_rows(c.table)[:, here, :], v[s][:]).then_inc(c.stored[s].sem, 16)
                for s in range(2):
                    sp.wait_ge(c.stored[s].sem, c.stored[s].at(32 * NIT))
                    sp.wait_ge(c.gathered[s].sem, c.gathered[s].at(16 * NK * NIT))
                sp.wait_ge(c.moved_by_pool.sem, c.moved_by_pool.at(16))
                sp.dma_start(c.fill[0:EP, :].rearrange("(p j) f -> p j f", j=EC)[:, 0, :], begin[:]).then_inc(c.moved.sem, 16)
                sp.wait_ge(c.moved.sem, c.moved.at(16))
        for s in range(2):
            c.gathered[s].counted(16 * NK * NIT)
            c.staged[s].counted(NIT)
            c.stored[s].counted(32 * NIT)
        c.moved_by_pool.counted(16)
        c.moved.counted(16)
        c.act_gave.counted(T)
        c.act_gave2.counted(3 * T)
        c.pe_gave.counted(2 * T)
        c.pe_gave2.counted(T)
        c.dve_gave.counted(2 * T)
        c.end_phase()


def edge_logits(c, l, order, logit):
    nc = c.nc
    with ExitStack() as ctx:
        rows = [c.sb(f"rows{s}", [P, K, D], ctx=ctx) for s in range(2)]
        fill = [c.sb(f"fill{s}", [P, K, D], ctx=ctx) for s in range(2)]
        index = [c.sb(f"index{s}", [P, K], I32, ctx) for s in range(2)]
        keep = [c.sb(f"keep{s}", [P, K], ctx=ctx) for s in range(2)]
        carry = c.sb("carry", [P, D], ctx=ctx)
        per = 2 * (D + 4)
        with nc.Block() as block:
            @block.scalar
            def _(act):
                with act.Fori(0, EIT) as i:
                    for s in range(2):
                        here = bass.ds(2 * K * i + s * K, K)
                        act.wait_ge(c.gathered[s].sem, c.gathered[s].at(16 * K * i))
                        act.wait_ge(c.computed[s].sem, c.computed[s].at(i))
                        nc.scalar.activation(index[s][:], c.from_dst[:, here], ACT.Copy).then_inc(c.staged[s].sem, 1)
                        nc.scalar.activation(keep[s][:], order.keep[:, here], ACT.Copy).then_inc(c.staged[s].sem, 1)

            @block.gpsimd
            def _(pool):
                with pool.Fori(0, EIT) as i:
                    for s in range(2):
                        pool.wait_ge(c.staged[s].sem, c.staged[s].at(2 * i + 1))
                        pool.wait_ge(c.computed[s].sem, c.computed[s].at(i))
                        pool.sem_inc(c.pool_turn.sem, 1)
                        for k in range(K):
                            pool.indirect_dma_start(out=rows[s][:, k, :], out_offset=None, in_=c.table,
                                                    in_offset=at_rows(index[s][:, k:k + 1])).then_inc(c.gathered[s].sem, 16)

            @block.sync
            def _(sp):
                src = c.fill[0:EP, :].rearrange("(p j) f -> p j f", j=EC)
                with sp.Fori(0, EIT) as i:
                    for s in range(2):
                        sp.wait_ge(c.computed[s].sem, c.computed[s].at(i))
                        sp.sem_inc(c.sp_turn.sem, 1)
                        sp.dma_start(fill[s][:], src[:, bass.ds(2 * K * i + s * K, K), :]).then_inc(c.loaded[s].sem, 16)

            @block.vector
            def _(dve):
                st = Steps(dve, c.dve_step)
                st.then(nc.vector.memset(carry[:], 0.0))
                st.close()
                with dve.Fori(0, EIT) as i:
                    st = Steps(dve, c.dve_step, i, per)
                    for s in range(2):
                        dve.wait_ge(c.loaded[s].sem, c.loaded[s].at(16 * i + 16))
                        dve.wait_ge(c.staged[s].sem, c.staged[s].at(2 * i + 2))
                        st.wait()
                        for f in range(D):
                            st.mark(nc.vector.tensor_tensor_scan(fill[s][:, :, f], keep[s][:], fill[s][:, :, f],
                                                                 carry[:, f:f + 1], ALU.mult, ALU.add))
                        st.wait()
                        st.mark(nc.vector.tensor_copy(carry[:], fill[s][:, K - 1, :]))
                        dve.wait_ge(c.gathered[s].sem, c.gathered[s].at(16 * K * i + 16 * K))
                        st.then(nc.vector.tensor_tensor(rows[s][:], rows[s][:], fill[s][:], ALU.add))
                        st.then(nc.vector.scalar_tensor_tensor(out=rows[s][:], in0=rows[s][:], scalar=0.0,
                                                               in1=spread(c.w2[l][:][:, None, :], [P, K, D]),
                                                               op0=ALU.max, op1=ALU.mult))
                        st.then(nc.vector.tensor_reduce(logit[:, bass.ds(2 * K * i + s * K, K)], rows[s][:], AX_X, ALU.add))
                        dve.sem_inc(c.computed[s].sem, 1)
                st.close(EIT)
        for s in range(2):
            c.gathered[s].counted(16 * K * EIT)
            c.computed[s].counted(EIT)
            c.staged[s].counted(2 * EIT)
            c.loaded[s].counted(16 * EIT)
        c.end_phase()


def diffusion_layer(c, order):
    with ExitStack() as ctx:
        y = c.sb("y", [P, NC, D], ctx=ctx)
        mask = c.sb("mask", [P, EC], ctx=ctx)
        norm = c.sb("norm", [P, NC, 1], ctx=ctx)
        mask_carry = c.sb("mask_carry", [P, 1], ctx=ctx)
        bn = [P, NC, D]
        vector_phase(c, lambda nc, st, by_act: st.then(nc.vector.tensor_copy(whole(y), whole(c.x))))
        for l in range(N_LAYERS):
            edge_halves(c, l, order, y)
            edge_logits(c, l, order, mask)
            with ExitStack() as ctx2:
                scan = c.sb("scan", [P, EC], ctx=ctx2)

                def masks(nc, st, by_act):
                    by_act(ACT.Sigmoid, mask[:], mask[:], c.b2[l][:])
                    st.then(nc.vector.tensor_scalar(mask[:], mask[:], ZETA - GAMMA, GAMMA, ALU.mult, ALU.add))
                    st.then(nc.vector.tensor_scalar(mask[:], mask[:], 0.0, 1.0, ALU.max, ALU.min))
                    st.then(nc.vector.tensor_tensor_scan(scan[:], order.keep[:], mask[:], 0.0, ALU.mult, ALU.add))
                    st.then(nc.vector.tensor_copy(mask_carry[:], scan[:, EC - 1:EC]))

                vector_phase(c, masks, [(c.mask_d[0:EP, :].rearrange("(p j) a -> p (j a)", j=EC), scan[:])])
            node_sums(c, order, c.mask_d, mask_carry, norm)
            with ExitStack() as ctx2:
                agg = c.sb("agg", [P, NC, D], ctx=ctx2)

                def second_table(nc, st, by_act):
                    flat = norm[:].rearrange("p c a -> p (c a)")
                    st.then(nc.vector.tensor_scalar(flat, flat, 1e-6, None, ALU.add))
                    by_act(ACT.Sqrt, flat, flat)
                    st.then(nc.vector.reciprocal(flat, flat))
                    st.then(nc.vector.tensor_scalar(flat, flat, 0.0, 10.0, ALU.max, ALU.min))
                    st.then(nc.vector.tensor_tensor(agg[:], y[:], spread(norm[:], bn), ALU.mult))

                vector_phase(c, second_table, [(node_rows(c.table), agg[:])])
                edge_sum(c, order, c.from_dst, c.table, c.scanned, c.carry, mask)
                node_sums(c, order, c.scanned, c.carry, agg)

                def add_up(nc, st, by_act):
                    st.then(nc.vector.tensor_tensor(y[:], agg[:], spread(norm[:], bn), ALU.mult))
                    if l == 0:
                        st.then(nc.vector.tensor_tensor(whole(c.x), whole(c.x), whole(c.x), ALU.add))
                    st.then(nc.vector.tensor_tensor(whole(c.x), whole(c.x), whole(y), ALU.add))

                vector_phase(c, add_up)
        small = c.sb("small", [P, NC], ctx=ctx)
        vector_phase(c, lambda nc, st, by_act: layer_norm(c, nc, st, by_act, c.x, y, small))



def relation_table(c, a):
    nc = c.nc
    HALF = N_RELS * D // 2
    T = 2 * NIT
    with ExitStack() as ctx:
        w = c.sb("w3", [D, N_RELS, D], ctx=ctx)
        side = c.sb("side", [P, NK, D], ctx=ctx)
        turned = c.sb("turned", [D, NK, P], ctx=ctx)
        ready = [c.sb(f"ready{s}", [P, NK, N_RELS * D], ctx=ctx) for s in range(2)]
        turn = c.ps("turn", [D, NK + 1, P], ctx=ctx)
        half = [[c.ps(f"half{g}_{b}", [P, HALF], ctx=ctx) for b in range(3)] for g in range(2)]
        table = c.table3.rearrange("(p c r) o -> p c (r o)", c=NC, r=N_RELS)
        flat = w[:].rearrange("i r o -> i (r o)")
        with nc.Block() as block:
            @block.scalar
            def _(act):
                with act.Fori(0, NIT) as i2:
                    for s in range(2):
                        i = 2 * i2 + s
                        act.wait_ge(c.pe_gave.sem, c.pe_gave.at(i))
                        nc.scalar.activation(side[:], c.x[:, bass.ds(NK * i, NK), :], ACT.Copy).then_inc(c.act_gave.sem, 1)
                        act.wait_ge(c.pe_gave2.sem, c.pe_gave2.at(2 * NK * i))
                        act.wait_ge(c.pe_gave.sem, c.pe_gave.at(i + 1))
                        nc.scalar.activation(turned[:], turn[:, 0:NK, :], ACT.Copy).then_inc(c.act_gave.sem, 1)
                        act.wait_ge(c.stored[s].sem, c.stored[s].at(16 * i2))
                        for k in range(NK):
                            act.wait_ge(c.pe_gave2.sem, c.pe_gave2.at(2 * NK * i + 2 * k + 1))
                            nc.scalar.activation(ready[s][:, k, 0:HALF], half[0][k % 3][:], ACT.Copy)\
                                .then_inc(c.act_gave2.sem, 1)

            @block.vector
            def _(dve):
                with dve.Fori(0, NIT) as i2:
                    for s in range(2):
                        i = 2 * i2 + s
                        dve.wait_ge(c.stored[s].sem, c.stored[s].at(16 * i2))
                        for k in range(NK):
                            dve.wait_ge(c.pe_gave2.sem, c.pe_gave2.at(2 * NK * i + 2 * k + 2))
                            nc.vector.tensor_copy(ready[s][:, k, HALF:2 * HALF], half[1][k % 3][:])\
                                .then_inc(c.dve_gave.sem, 1)

            @block.tensor
            def _(pe):
                pe.wait_ge(c.moved.sem, c.moved.at(16))
                with pe.Fori(0, T) as i:
                    pe.wait_ge(c.act_gave.sem, c.act_gave.at(2 * i + 1))
                    pe.sem_inc(c.pe_turn.sem, 1)
                    for k in range(NK):
                        last = nc.tensor.transpose(turn[:, k, :], side[:, k, :], c.ident[:])
                    last.then_inc(c.pe_gave.sem, 1)
                    pe.wait_ge(c.act_gave.sem, c.act_gave.at(2 * i + 2))
                    pe.wait_ge(c.act_gave2.sem, c.act_gave2.at(NK * i))
                    pe.wait_ge(c.dve_gave.sem, c.dve_gave.at(NK * i))
                    pe.sem_inc(c.pe_turn.sem, 1)
                    for k in range(NK):
                        if k >= 3:
                            pe.wait_ge(c.act_gave2.sem, c.act_gave2.at(NK * i + k - 2))
                            pe.wait_ge(c.dve_gave.sem, c.dve_gave.at(NK * i + k - 2))
                            pe.sem_inc(c.pe_turn.sem, 1)
                        for g in range(2):
                            nc.tensor.matmul(half[g][k % 3][:], turned[:, k, :], flat[:, HALF * g:HALF * g + HALF],
                                             start=True, stop=True).then_inc(c.pe_gave2.sem, 1)

            @block.sync
            def _(sp):
                sp.dma_start(w[:], a["L3_gnn_weight"].rearrange("r i o -> i r o")).then_inc(c.moved.sem, 16)
                with sp.Fori(0, NIT) as i2:
                    for s in range(2):
                        i = 2 * i2 + s
                        sp.wait_ge(c.act_gave2.sem, c.act_gave2.at(NK * i + NK))
                        sp.sem_inc(c.sp_turn.sem, 1)
                        sp.wait_ge(c.dve_gave.sem, c.dve_gave.at(NK * i + NK))
                        sp.sem_inc(c.sp_turn.sem, 1)
                        sp.dma_start(table[:, bass.ds(NK * i, NK), :], ready[s][:]).then_inc(c.stored[s].sem, 16)
                for s in range(2):
                    c.stored[s].counted(16 * NIT)
                    sp.wait_ge(c.stored[s].sem, c.stored[s].at(16 * NIT))
        c.moved.counted(16)
        c.act_gave.counted(2 * T)
        c.act_gave2.counted(NK * T)
        c.dve_gave.counted(NK * T)
        c.pe_gave.counted(T)
        c.pe_gave2.counted(2 * NK * T)
        c.end_phase()


def relation_layer(c, a, order, out):
    relation_table(c, a)
    edge_sum(c, order, c.from_rel, c.table3, c.scanned, c.carry)
    with ExitStack() as ctx:
        agg = c.sb("agg", [P, NC, D], ctx=ctx)
        small = c.sb("small", [P, NC], ctx=ctx)
        node_sums(c, order, c.scanned, c.carry, agg)

        def finish(nc, st, here, product):
            st.mark(nc.vector.tensor_tensor(agg[:, here, :], agg[:, here, :], product[:], ALU.add))

        project(c, [c.x], [c.w3loop[:]], finish, 1)

        def work(nc, st, by_act):
            st.then(nc.vector.tensor_tensor(agg[:], agg[:], spread(c.bias3[:][:, None, :], [P, NC, D]), ALU.add))
            st.then(nc.vector.tensor_tensor(whole(c.x), whole(c.x), whole(agg), ALU.add))
            layer_norm(c, nc, st, by_act, c.x, agg, small)

        full = N_NODES // NC
        rest = N_NODES - full * NC
        vector_phase(c, work, [
            (out[0:96 * NC, :].rearrange("(p c) f -> p c f", c=NC), c.x[0:96, :, :]),
            (out[96 * NC:full * NC, :].rearrange("(p c) f -> p c f", c=NC), c.x[96:full, :, :]),
            (out[full * NC:N_NODES, :].rearrange("(p c) f -> p c f", p=1), c.x[full:full + 1, 0:rest, :])])


def cleared_rows(c, ctx):
    nc = c.nc
    cols = 98
    zero = c.sb("zero", [P, cols, D], ctx=ctx)
    none1 = c.sb("none1", [P, HEADS, HW_], ctx=ctx)
    jobs = [(c.scanned[NO_EDGE_ROW:NO_EDGE_ROW + 1, :], zero[0:1, 0, :]),
            (c.mask_d[NO_EDGE_ROW:NO_EDGE_ROW + 1, :], zero[0:1, 0, 0:1]),
            (c.scanned1[NO_EDGE_ROW:NO_EDGE_ROW + 1, :], none1[0:1, :, :].rearrange("p h f -> p (h f)"))]
    fill = c.fill[0:EP, :].rearrange("(p j) f -> p j f", j=EC)
    for j in range(0, EC, cols):
        jobs.append((fill[:, j:j + cols, :], zero[:]))
    wide = cols * D // HEADS
    fill1 = c.fill1[0:EP, :].rearrange("(p j) f -> p (j f)", j=EC)
    flat = zero[:].rearrange("p c f -> p (c f)")
    for j in range(0, EC * HEADS, cols * D):
        n = min(cols * D, EC * HEADS - j)
        jobs.append((fill1[:, j:j + n], flat[:, 0:n]))

    def zeros(nc, st, by_act):
        st.mark(nc.vector.memset(zero[:], 0.0))
        st.then(nc.vector.memset(none1[:], 0.0))
        st.mark(nc.vector.memset(none1[:, :, D + 1], -BIG))

    vector_phase(c, zeros)
    return jobs





def graph_layers(nc, a, out):
    with ExitStack() as ctx:
        c = Core(nc, ctx)
        only_unsorted = Core(nc, ctx, "only_unsorted_", 1)
        start(c, only_unsorted, a)
        unsorted = c.sb("unsorted", [P, 1], I32)
        by_dst = Order(c, "dst", 3)
        by_src = Order(c, "src", 2)
        c.from_src = c.sb("from_src", [P, EC], I32)
        c.from_rel = c.sb("from_rel", [P, EC], I32)
        c.from_dst = c.sb("from_dst", [P, EC], I32)
        c.carry = c.sb("carry", [P, D])
        c.table = c.dram("table", [NP, D])
        c.table_u = c.dram("table_u", [NP, D])
        c.scanned = c.dram("scanned", [EP + 1, D])
        c.fill = c.dram("fill", [EP + 1 + NP, D])
        c.table1 = c.dram("table1", [NP, TAB1])
        c.a_dst_d = c.dram("a_dst_d", [NP, HEADS])
        c.fill1 = c.dram("fill1", [EP + 1 + NP, HEADS])
        c.scanned1 = c.dram("scanned1", [EP + 1, ROW1])
        c.tops_d = c.dram("tops_d", [P, HEADS])
        c.nodes_d = c.dram("nodes_d", [P + 1, 1])
        c.mask_d = c.dram("mask_d", [EP + 1, 1])
        c.table3 = c.dram("table3", [NP * N_RELS, D])

        write_list(c, by_dst, [a["dst"], a["src"], a["edge_type_16"]])
        write_list(c, by_src, [a["src"], a["dst"]])
        find_disorder(c, by_dst, unsorted)
        radix_sort(c, by_dst, only_unsorted, unsorted)
        with ExitStack() as while_sorting:
            clears = cleared_rows(c, while_sorting)
            radix_sort(c, by_src, c, counted=[(1, by_dst), (0, by_src)], clears=clears)

        def dst_side(nc, st, recs):
            st.mark(nc.vector.tensor_copy(c.from_src[:], recs[:, :, 1]))
            st.then(nc.vector.tensor_scalar(c.from_rel[:], recs[:, :, 1], float(N_RELS), None, ALU.mult))
            st.then(nc.vector.tensor_tensor(c.from_rel[:], c.from_rel[:], recs[:, :, 2], ALU.add))

        def src_side(nc, st, recs):
            st.mark(nc.vector.tensor_copy(c.from_dst[:], recs[:, :, 1]))

        read_order(c, by_dst, dst_side)
        read_order(c, by_src, src_side)
        chebyshev_layer(c, by_dst)
        attention_layer(c, by_dst)
        diffusion_layer(c, by_src)
        relation_layer(c, a, by_dst, out)


_INS = ["x", "src", "dst", "edge_type_16", "L0_gnn_W", "L0_gnn_b", "L1_gnn_W", "L1_gnn_att_src", "L1_gnn_att_dst",
        "L1_gnn_bias", "L2_gnn_nb_W", "L2_gnn_nb_b", "L2_gnn_self_W", "L2_gnn_self_b", "L2_gnn_att1_W",
        "L2_gnn_att1_b", "L2_gnn_att2_W", "L2_gnn_att2_b", "L3_gnn_weight", "L3_gnn_h_bias", "L3_gnn_loop_weight"]
_OUTS = [((N_NODES, D), "float32")]


def kernel(**inputs):
    import numpy as _np
    import concourse.bacc as _bacc
    from concourse import mybir as _mybir
    from concourse.bass_utils import run_bass_kernel_spmd as _run

    nc = _bacc.Bacc("TRN2", target_bir_lowering=False, num_devices=1)
    arrays, by_name = {}, {}
    for name in _INS:
        array = _np.ascontiguousarray(inputs[name])
        arrays[f"in_{name}_dram"] = array
        by_name[name] = nc.dram_tensor(f"in_{name}_dram", array.shape, _mybir.dt.from_np(array.dtype),
                                       kind="ExternalInput").ap()
    shape, dtype = _OUTS[0]
    out = nc.dram_tensor("out_0_dram", shape, _mybir.dt.from_np(_np.dtype(dtype)), kind="ExternalOutput").ap()
    graph_layers(nc, by_name, out)
    r = _run(nc, [arrays], core_ids=[0])
    return _np.asarray(r.results[0]["out_0_dram"])
```
